# Optimizing a Trainium2 kernel written in Bass

```python
import numpy as np
import jax
import jax.numpy as jnp

def _softmax(x, axis=-1):
    return jax.nn.softmax(x, axis=axis)

def _gelu(x):
    return jax.nn.gelu(x, approximate=True)

def _silu(x):
    return jax.nn.silu(x)

def _sigmoid(x):
    return jax.nn.sigmoid(x)

def _layernorm(x, axis=-1, eps=1e-05):
    m = jnp.mean(x, axis=axis, keepdims=True)
    v = jnp.var(x, axis=axis, keepdims=True)
    return (x - m) / jnp.sqrt(v + eps)

def _scatter_add(tgt, idx, src, axis=0):
    return tgt.at[idx].add(src)

def _segment_sum(src, seg, n):
    return jax.ops.segment_sum(src, seg, n)
kernel_name = 'mk_xattn_ffn_d2_seqx_r4_64b215'

def setup_inputs(seed: int=0):
    np.random.seed(seed)
    _w = jnp.asarray

    def _rec_inputs():
        import jax
        import jax.numpy as jnp
        _rk = jax.random.key(seed)
        x = 0.0001212 + 1 * jax.random.normal(jax.random.fold_in(_rk, 1), (4, 512, 512), jnp.float32)
        _lenS = 512 - jax.random.randint(jax.random.fold_in(_rk, 7), (4,), 0, max(1, 512 // 4) + 1, jnp.int32)
        _lenS2 = 512 - jax.random.randint(jax.random.fold_in(_rk, 8), (4,), 0, max(1, 512 // 4) + 1, jnp.int32)
        _ctx_2048P = jax.random.normal(jax.random.fold_in(_rk, 11), (4, 16, 512), jnp.float32)
        _ctx_2048c = jax.random.dirichlet(jax.random.fold_in(_rk, 511), 0.3 * jnp.ones((16,), jnp.float32), (4, 512))
        _ctx_2048t = jnp.einsum('bsk,bkd->bsd', _ctx_2048c, _ctx_2048P)
        _ctx_2048t = _ctx_2048t * jax.lax.rsqrt(jnp.mean(jnp.square(_ctx_2048t)) + 1e-12) * 0.953939
        ctx_2048 = 0.000173663 + 1.0001 * (_ctx_2048t + 0.3 * jax.random.normal(jax.random.fold_in(_rk, 611), (4, 512, 512), jnp.float32))
        _validS = jnp.arange(512)[None, :] < _lenS[:, None]
        _validS2 = jnp.arange(512)[None, :] < _lenS2[:, None]
        _causal = jnp.tril(jnp.ones((512, 512), dtype=bool))
        mask_1xSxS2_ff0 = jnp.where(jnp.ones((1, 512, 512), dtype=bool), 0.0, -1000000000.0).astype(jnp.float32)
        return (x, ctx_2048, mask_1xSxS2_ff0)
    x, ctx_2048, mask_1xSxS2_ff0 = _rec_inputs()

    def _L0_xattn_setup():
        import jax, jax.numpy as jnp
        import numpy as np
        B_DIM, T_DIM, C_DIM = (16, 256, 512)

        def _wkv(w, u, k, v):
            Bn, Tn, Cn = k.shape
            NEG_INF = jnp.float32(-1e+38)

            def step(carry, kv_t):
                p, q, o = carry
                kt, vt = kv_t
                no = jnp.maximum(o, u + kt)
                A = jnp.exp(o - no)
                E = jnp.exp(u + kt - no)
                y = (A * p + E * vt) / (A * q + E)
                no2 = jnp.maximum(w + o, kt)
                A2 = jnp.exp(w + o - no2)
                E2 = jnp.exp(kt - no2)
                return ((A2 * p + E2 * vt, A2 * q + E2, no2), y)
            init = (jnp.zeros((Bn, Cn), k.dtype), jnp.zeros((Bn, Cn), k.dtype), jnp.full((Bn, Cn), NEG_INF, k.dtype))
            kT = jnp.moveaxis(k, 1, 0)
            vT = jnp.moveaxis(v, 1, 0)
            _, yT = jax.lax.scan(step, init, (kT, vT))
            return jnp.moveaxis(yT, 0, 1)
        key = jax.random.key(seed)
        k1, k2, k3, k4 = jax.random.split(key, 4)
        w = -jnp.exp(jax.random.normal(k1, (C_DIM,), jnp.float32))
        u = jax.random.normal(k2, (C_DIM,), jnp.float32)
        k = jax.random.normal(k3, (B_DIM, T_DIM, C_DIM), jnp.float32)
        v = jax.random.normal(k4, (B_DIM, T_DIM, C_DIM), jnp.float32)
        return {'B': B_DIM, 'T': T_DIM, 'C': C_DIM, 'w': w, 'u': u, 'k': k, 'v': v}
    _L0_xattn_all = _L0_xattn_setup()
    _L0_xattn_in = {k: v for k, v in _L0_xattn_all.items() if k in ('w', 'u')}
    del _L0_xattn_all

    def _L0_ffn_setup():
        import jax, jax.numpy as jnp
        import numpy as np
        B, S, H = (4, 256, 512)
        E = 16
        K = 2
        I = 256
        N_SHARED = 2
        I_SHARED = I * N_SHARED
        RATIO = 0.1
        EPS = 1e-09

        def _swiglu(x, wg, wu, wd):
            return jax.nn.silu(x @ wg) * (x @ wu) @ wd
        key = jax.random.key(seed)
        ks = jax.random.split(key, 9)
        scale = 0.02
        x = jax.random.normal(ks[0], (B, S, H), dtype=jnp.float32)
        centroids = jax.random.normal(ks[1], (E, H), dtype=jnp.float32)
        gate_bias = jnp.zeros((E,), dtype=jnp.float32)
        wg_s = jax.random.normal(ks[2], (H, I_SHARED), dtype=jnp.float32) * scale
        wu_s = jax.random.normal(ks[3], (H, I_SHARED), dtype=jnp.float32) * scale
        wd_s = jax.random.normal(ks[4], (I_SHARED, H), dtype=jnp.float32) * scale
        wg = jax.random.normal(ks[5], (E, H, I), dtype=jnp.float32) * scale
        wu = jax.random.normal(ks[6], (E, H, I), dtype=jnp.float32) * scale
        wd = jax.random.normal(ks[7], (E, I, H), dtype=jnp.float32) * scale
        return {'x': x, 'centroids': centroids, 'gate_bias': gate_bias, 'wg_s': wg_s, 'wu_s': wu_s, 'wd_s': wd_s, 'wg': wg, 'wu': wu, 'wd': wd}
    _L0_ffn_all = _L0_ffn_setup()
    _L0_ffn_in = {k: v for k, v in _L0_ffn_all.items() if k in ('centroids', 'gate_bias', 'wg_s', 'wu_s', 'wd_s', 'wg', 'wu', 'wd')}
    del _L0_ffn_all

    def _L1_xattn_setup():
        import jax, jax.numpy as jnp
        import numpy as np
        H = 512
        NH = 16
        NKV = 4
        HD = 128
        GROUPS = NH // NKV
        EPS = 1e-06
        B, S, SE = (1, 512, 1024)

        def _rmsnorm(x, w, eps=EPS):
            xf = x.astype(jnp.float32)
            var = jnp.mean(xf * xf, axis=-1, keepdims=True)
            return (xf * jax.lax.rsqrt(var + eps)).astype(x.dtype) * w
        key = jax.random.key(seed)
        ks = jax.random.split(key, 12)
        sc = 0.02
        return {'hidden_states': jax.random.normal(ks[0], (B, S, H), jnp.float32), 'encoder_hidden_states': jax.random.normal(ks[1], (B, SE, H), jnp.float32), 'attention_mask': jnp.zeros((B, S, SE), jnp.float32), 'Wq': jax.random.normal(ks[2], (H, NH * HD), jnp.float32) * sc, 'bq': jax.random.normal(ks[3], (NH * HD,), jnp.float32) * sc, 'Wk': jax.random.normal(ks[4], (H, NKV * HD), jnp.float32) * sc, 'bk': jax.random.normal(ks[5], (NKV * HD,), jnp.float32) * sc, 'Wv': jax.random.normal(ks[6], (H, NKV * HD), jnp.float32) * sc, 'bv': jax.random.normal(ks[7], (NKV * HD,), jnp.float32) * sc, 'Wo': jax.random.normal(ks[8], (NH * HD, H), jnp.float32) * sc, 'qn_w': jnp.ones((HD,), jnp.float32), 'kn_w': jnp.ones((HD,), jnp.float32)}
    _L1_xattn_all = _L1_xattn_setup()
    _L1_xattn_in = {k: v for k, v in _L1_xattn_all.items() if k in ('Wq', 'bq', 'Wk', 'bk', 'Wv', 'bv', 'Wo', 'qn_w', 'kn_w')}
    del _L1_xattn_all

    def _L1_ffn_setup():
        import jax, jax.numpy as jnp
        import numpy as np
        FP8_MAX = 448.0

        def _fp8_matmul(x2d, w):
            scale_x = jnp.maximum(jnp.max(jnp.abs(x2d)) / FP8_MAX, 1e-06)
            scale_w = jnp.maximum(jnp.max(jnp.abs(w)) / FP8_MAX, 1e-06)
            x8 = (x2d / scale_x).astype(jnp.float8_e4m3fn)
            w8 = (w / scale_w).astype(jnp.float8_e4m3fn)
            out = jnp.matmul(x8.astype(x2d.dtype), w8.astype(x2d.dtype).T)
            return out * (scale_x * scale_w)
        key = jax.random.key(seed)
        k1, k2, k3 = jax.random.split(key, 3)
        dim = 512
        B, S = (4, 512)
        x = jax.random.normal(k1, (B, S, dim), dtype=jnp.float32)
        std = 0.5 * dim ** (-0.5)
        w_fc = jax.random.normal(k2, (4 * dim, dim), dtype=jnp.float32) * std
        w_proj = jax.random.normal(k3, (dim, 4 * dim), dtype=jnp.float32) * std
        return {'x': x, 'w_fc': w_fc, 'w_proj': w_proj}
    _L1_ffn_all = _L1_ffn_setup()
    _L1_ffn_in = {k: v for k, v in _L1_ffn_all.items() if k in ('w_fc', 'w_proj')}
    del _L1_ffn_all
    return {'x': x, 'ctx_2048': ctx_2048, 'mask_1xSxS2_ff0': mask_1xSxS2_ff0, 'L0_xattn_w': _L0_xattn_in['w'], 'L0_xattn_u': _L0_xattn_in['u'], 'L0_ffn_centroids': _L0_ffn_in['centroids'], 'L0_ffn_gate_bias': _L0_ffn_in['gate_bias'], 'L0_ffn_wg_s': _L0_ffn_in['wg_s'], 'L0_ffn_wu_s': _L0_ffn_in['wu_s'], 'L0_ffn_wd_s': _L0_ffn_in['wd_s'], 'L0_ffn_wg': _L0_ffn_in['wg'], 'L0_ffn_wu': _L0_ffn_in['wu'], 'L0_ffn_wd': _L0_ffn_in['wd'], 'L1_xattn_Wq': _L1_xattn_in['Wq'], 'L1_xattn_bq': _L1_xattn_in['bq'], 'L1_xattn_Wk': _L1_xattn_in['Wk'], 'L1_xattn_bk': _L1_xattn_in['bk'], 'L1_xattn_Wv': _L1_xattn_in['Wv'], 'L1_xattn_bv': _L1_xattn_in['bv'], 'L1_xattn_Wo': _L1_xattn_in['Wo'], 'L1_xattn_qn_w': _L1_xattn_in['qn_w'], 'L1_xattn_kn_w': _L1_xattn_in['kn_w'], 'L1_ffn_w_fc': _L1_ffn_in['w_fc'], 'L1_ffn_w_proj': _L1_ffn_in['w_proj']}

def reference(x, ctx_2048, mask_1xSxS2_ff0, L0_xattn_w, L0_xattn_u, L0_ffn_centroids, L0_ffn_gate_bias, L0_ffn_wg_s, L0_ffn_wu_s, L0_ffn_wd_s, L0_ffn_wg, L0_ffn_wu, L0_ffn_wd, L1_xattn_Wq, L1_xattn_bq, L1_xattn_Wk, L1_xattn_bk, L1_xattn_Wv, L1_xattn_bv, L1_xattn_Wo, L1_xattn_qn_w, L1_xattn_kn_w, L1_ffn_w_fc, L1_ffn_w_proj):
    import jax
    import jax.numpy as jnp

    def _L0_xattn_ref(B, T, C, w, u, k, v):
        import jax, jax.numpy as jnp
        import numpy as np
        B_DIM, T_DIM, C_DIM = (16, 256, 512)

        def _wkv(w, u, k, v):
            Bn, Tn, Cn = k.shape
            NEG_INF = jnp.float32(-1e+38)

            def step(carry, kv_t):
                p, q, o = carry
                kt, vt = kv_t
                no = jnp.maximum(o, u + kt)
                A = jnp.exp(o - no)
                E = jnp.exp(u + kt - no)
                y = (A * p + E * vt) / (A * q + E)
                no2 = jnp.maximum(w + o, kt)
                A2 = jnp.exp(w + o - no2)
                E2 = jnp.exp(kt - no2)
                return ((A2 * p + E2 * vt, A2 * q + E2, no2), y)
            init = (jnp.zeros((Bn, Cn), k.dtype), jnp.zeros((Bn, Cn), k.dtype), jnp.full((Bn, Cn), NEG_INF, k.dtype))
            kT = jnp.moveaxis(k, 1, 0)
            vT = jnp.moveaxis(v, 1, 0)
            _, yT = jax.lax.scan(step, init, (kT, vT))
            return jnp.moveaxis(yT, 0, 1)
        return _wkv(w, u, k, v)

    def _L0_ffn_ref(x, centroids, gate_bias, wg_s, wu_s, wd_s, wg, wu, wd):
        import jax, jax.numpy as jnp
        import numpy as np
        B, S, H = (4, 256, 512)
        E = 16
        K = 2
        I = 256
        N_SHARED = 2
        I_SHARED = I * N_SHARED
        RATIO = 0.1
        EPS = 1e-09

        def _swiglu(x, wg, wu, wd):
            return jax.nn.silu(x @ wg) * (x @ wu) @ wd
        shared = _swiglu(x, wg_s, wu_s, wd_s) * RATIO
        affinity = jax.nn.sigmoid(jnp.einsum('bsh,eh->bse', x, centroids))
        biased = affinity + gate_bias
        _, top_idx = jax.lax.top_k(biased, K)
        top_aff = jnp.take_along_axis(affinity, top_idx, axis=-1)
        weights = top_aff / (top_aff.sum(-1, keepdims=True) + EPS)
        mask = (jax.nn.one_hot(top_idx, E, dtype=x.dtype) * weights[..., None]).sum(-2)
        routed = jnp.zeros_like(x)
        for e in range(E):
            routed = routed + mask[..., e:e + 1] * _swiglu(x, wg[e], wu[e], wd[e])
        return shared + routed

    def _L1_xattn_ref(hidden_states, encoder_hidden_states, attention_mask, Wq, bq, Wk, bk, Wv, bv, Wo, qn_w, kn_w):
        import jax, jax.numpy as jnp
        import numpy as np
        H = 512
        NH = 16
        NKV = 4
        HD = 128
        GROUPS = NH // NKV
        EPS = 1e-06
        B, S, SE = (1, 512, 1024)

        def _rmsnorm(x, w, eps=EPS):
            xf = x.astype(jnp.float32)
            var = jnp.mean(xf * xf, axis=-1, keepdims=True)
            return (xf * jax.lax.rsqrt(var + eps)).astype(x.dtype) * w
        b, s, _ = hidden_states.shape
        se = encoder_hidden_states.shape[1]
        q = (hidden_states @ Wq + bq).reshape(b, s, NH, HD).transpose(0, 2, 1, 3)
        k = (encoder_hidden_states @ Wk + bk).reshape(b, se, NKV, HD).transpose(0, 2, 1, 3)
        v = (encoder_hidden_states @ Wv + bv).reshape(b, se, NKV, HD).transpose(0, 2, 1, 3)
        k = jnp.repeat(k, GROUPS, axis=1)
        v = jnp.repeat(v, GROUPS, axis=1)
        q = _rmsnorm(q, qn_w)
        k = _rmsnorm(k, kn_w)
        scale = 1.0 / np.sqrt(HD).astype(np.float32)
        scores = jnp.einsum('bhsd,bhed->bhse', q, k) * scale
        scores = scores + attention_mask[:, None, :, :]
        probs = jax.nn.softmax(scores.astype(jnp.float32), axis=-1).astype(q.dtype)
        out = jnp.einsum('bhse,bhed->bhsd', probs, v)
        out = out.transpose(0, 2, 1, 3).reshape(b, s, NH * HD)
        return out @ Wo

    def _L1_ffn_ref(x, w_fc, w_proj):
        import jax, jax.numpy as jnp
        import numpy as np
        FP8_MAX = 448.0

        def _fp8_matmul(x2d, w):
            scale_x = jnp.maximum(jnp.max(jnp.abs(x2d)) / FP8_MAX, 1e-06)
            scale_w = jnp.maximum(jnp.max(jnp.abs(w)) / FP8_MAX, 1e-06)
            x8 = (x2d / scale_x).astype(jnp.float8_e4m3fn)
            w8 = (w / scale_w).astype(jnp.float8_e4m3fn)
            out = jnp.matmul(x8.astype(x2d.dtype), w8.astype(x2d.dtype).T)
            return out * (scale_x * scale_w)
        shape = x.shape
        x2d = x.reshape(-1, shape[-1])
        h = _fp8_matmul(x2d, w_fc)
        h = jnp.square(jax.nn.relu(h))
        out = _fp8_matmul(h, w_proj)
        return out.reshape(*shape[:-1], -1)
    x = x + _L0_xattn_ref(4, 512, 512, L0_xattn_w, L0_xattn_u, _layernorm(x, axis=-1), ctx_2048)
    x = x + _L0_ffn_ref(_layernorm(x, axis=-1), L0_ffn_centroids, L0_ffn_gate_bias, L0_ffn_wg_s, L0_ffn_wu_s, L0_ffn_wd_s, L0_ffn_wg, L0_ffn_wu, L0_ffn_wd)
    x = x + _L1_xattn_ref(_layernorm(x, axis=-1), ctx_2048, mask_1xSxS2_ff0, L1_xattn_Wq, L1_xattn_bq, L1_xattn_Wk, L1_xattn_bk, L1_xattn_Wv, L1_xattn_bv, L1_xattn_Wo, L1_xattn_qn_w, L1_xattn_kn_w)
    x = x + _L1_ffn_ref(_layernorm(x, axis=-1), L1_ffn_w_fc, L1_ffn_w_proj)
    return x

_drawn_inputs = setup_inputs


def setup_inputs(seed=0):
    import zlib

    import numpy as np

    out = dict(_drawn_inputs(seed))
    spreads = {'L0_ffn_gate_bias': (0.0, 0.352), 'L1_xattn_qn_w': (1.0, 0.6), 'L1_xattn_kn_w': (1.0, 0.6)}
    factors = {'L0_ffn_centroids': 3.165,
     'L0_ffn_wg_s': 5.313,
     'L0_ffn_wu_s': 6.103,
     'L0_ffn_wd_s': 4.906,
     'L0_ffn_wg': 3.261,
     'L0_ffn_wu': 3.102,
     'L0_ffn_wd': 3.204,
     'L1_xattn_bq': 6.281,
     'L1_xattn_bk': 8.0,
     'L1_xattn_bv': 3.874}
    for name, (base, spread) in spreads.items():
        noise = np.random.default_rng([zlib.crc32(name.encode()), seed]).standard_normal(out[name].shape)
        drawn = base * np.exp(spread * noise) if base else spread * noise
        out[name] = jnp.asarray(drawn.astype(out[name].dtype))
    for name, factor in factors.items():
        out[name] = (out[name] * factor).astype(out[name].dtype)
    return out
```

```python
from contextlib import ExitStack

import concourse.bass as bass
from concourse import mybir

F32 = mybir.dt.float32
BF16 = mybir.dt.bfloat16
I32 = mybir.dt.int32
ALU = mybir.AluOpType
ACT = mybir.ActivationFunctionType
AX = mybir.AxisListType

P = 128
B, S, C = 4, 512, 512
TOK = B * S
NT = TOK // P
TPB = S // P
KC = C // P
LN_EPS = 1e-5
E_ROUTED = 16
F_EXP = 256
FC = F_EXP // P
NH, NKV, HD = 16, 4, 128
GROUP = NH // NKV
RMS_EPS = 1e-6
FF = 2048
FFC = FF // P
FP8_MAX = 448.0


class Steps:

    def __init__(self, eng, sem, base=0):
        self.eng, self.sem, self.base, self.n = eng, sem, base, 0

    def mark(self, ins):
        ins.then_inc(self.sem, 1)
        self.n += 1

    def wait(self):
        self.eng.wait_ge(self.sem, self.base + self.n)


class Names:

    def __init__(self, nc, stack, stage):
        self.nc, self.stack, self.stage = nc, stack, stage

    def sb(self, name, shape, dt):
        return self.stack.enter_context(self.nc.sbuf_tensor(f"{self.stage}_{name}", shape, dt))

    def ps(self, name, shape, dt):
        return self.stack.enter_context(self.nc.psum_tensor(f"{self.stage}_{name}", shape, dt))

    def sem(self, name):
        return self.nc.alloc_semaphore(f"{self.stage}_{name}")


def stage_setup(nc, ident, ident_bf, time_row):
    made = nc.alloc_semaphore("setup_made")
    with nc.Block() as block:
        @block.gpsimd
        def _(pool):
            pool.memset(ident[:, :], 0.0).then_inc(made, 1)
            pool.memset(ident_bf[:, :], 0.0).then_inc(made, 1)
            pool.wait_ge(made, 2)
            for m in (ident, ident_bf):
                pool.affine_select(out=m[:, :], in_=m[:, :], compare_op=ALU.not_equal, fill=1.0, base=0,
                                   pattern=[[-1, P]], channel_multiplier=1).then_inc(made, 1)
            pool.iota(time_row[:, :], [[1, S]], base=0, channel_multiplier=0,
                      allow_small_or_imprecise_dtypes=True).then_inc(made, 1)
            pool.wait_ge(made, 5)


def ln_stats(dve, sem, root_ready, X, stats, mv, rstd, start=0):
    with dve.Fori(0, NT) as t:
        dve.bn_stats(stats[:, t, :], X[:, t, :]).then_inc(sem, 1)
    dve.wait_ge(sem, start + NT)
    for t in range(NT):
        dve.bn_aggr(mv[:, t, :], stats[:, t, :]).then_inc(sem, 1)
    dve.wait_ge(sem, start + 2 * NT)
    dve.tensor_scalar(rstd[:, :], mv[:, :, 1], LN_EPS, None, ALU.add).then_inc(sem, 1)
    dve.wait_ge(root_ready, 1)
    dve.reciprocal(rstd[:, :], rstd[:, :]).then_inc(sem, 1)
    dve.wait_ge(sem, start + 2 * NT + 2)


def ln_root(act, sem, root_ready, rstd, start=0):
    act.wait_ge(sem, start + 2 * NT + 1)
    act.activation(rstd[:, :], rstd[:, :], ACT.Sqrt).then_inc(root_ready, 1)


def stage_wkv(nc, X, ctxT, ident, time_row, x, ctx_t, wu_cols, w_row):
    ctxT_hi, ctxT_lo = ctxT
    with ExitStack() as stack:
        m = Names(nc, stack, "wkv")
        cols = m.sb("cols", [P, 2, KC], F32)
        cw, cu = cols[:, 0, :], cols[:, 1, :]
        wrow = m.sb("wrow", [1, C], F32)
        nwrow = m.sb("nwrow", [1, C], F32)
        wpos = m.sb("wpos", [P, KC], F32)
        upos = m.sb("upos", [P, KC], F32)
        wneg = m.sb("wneg", [P, KC], F32)
        bias_state = m.sb("bias_state", [P, KC], F32)
        bias_now = m.sb("bias_now", [P, KC], F32)
        decay = m.sb("decay", [P, KC], F32)
        stats = m.sb("stats", [P, NT, 6], F32)
        mv = m.sb("mv", [P, NT, 2], F32)
        rstd = m.sb("rstd", [P, NT], F32)
        xn = [m.sb(f"xn{j}", [P, TPB, P], F32) for j in range(2)]
        v = [m.sb(f"v{j}", [P, S], F32) for j in range(2)]
        g_state = [m.sb(f"g_state{j}", [P, S], F32) for j in range(2)]
        g_now = [m.sb(f"g_now{j}", [P, S], F32) for j in range(2)]
        f_state = [m.sb(f"f_state{j}", [P, S], F32) for j in range(2)]
        f_now = [m.sb(f"f_now{j}", [P, S], F32) for j in range(2)]
        s_scan = [m.sb(f"s_scan{j}", [P, S + 1], F32) for j in range(2)]
        q_scan = [m.sb(f"q_scan{j}", [P, S + 1], F32) for j in range(2)]
        num = [m.sb(f"num{j}", [P, S], F32) for j in range(2)]
        den = [m.sb(f"den{j}", [P, S], F32) for j in range(2)]
        y = [m.sb(f"y{j}", [P, S], F32) for j in range(2)]
        pk = [m.ps(f"pk{j}", [P, S], F32) for j in range(2)]
        py = [m.ps(f"py{j}", [P, TPB, P], F32) for j in range(2)]

        x_loaded = [m.sem(f"x_loaded{b}") for b in range(B)]
        par_loaded = m.sem("par_loaded")
        v_loaded = [m.sem(f"v_loaded{j}") for j in range(2)]
        par = m.sem("par")
        decay_ready = m.sem("decay_ready")
        stat = m.sem("stat")
        root_ready = m.sem("root_ready")
        xn_ready = m.sem("xn_ready")
        k_ready = m.sem("k_ready")
        g_ready = m.sem("g_ready")
        hi_ready = m.sem("hi_ready")
        fst_ready = m.sem("fst_ready")
        fnow_ready = m.sem("fnow_ready")
        scan_done = m.sem("scan_done")
        nd_done = m.sem("nd_done")
        rec_done = m.sem("rec_done")
        v_free = m.sem("v_free")
        y_ready = m.sem("y_ready")
        yt_ready = m.sem("yt_ready")
        x_added = m.sem("x_added")

        with nc.Block() as block:
            @block.sync
            def _(sp):
                sp.dma_start(cols[:, :, :], wu_cols).then_inc(par_loaded, 16)
                sp.dma_start(wrow[:, :], w_row).then_inc(par_loaded, 16)
                for b in range(B):
                    sp.dma_start(X[:, b * TPB:(b + 1) * TPB, :],
                                 x[b].rearrange("(t p) c -> p t c", p=P)).then_inc(x_loaded[b], 16)
                with sp.Fori(0, B) as b:
                    for c in range(KC):
                        j = c % 2
                        sp.wait_ge(v_free, 2 * (b * KC + c) + 2)
                        sp.dma_start(v[j][:, :], ctx_t[b, c * P:(c + 1) * P, :]).then_inc(v_loaded[j], 16)

            @block.vector
            def _(dve):
                dve.wait_ge(par_loaded, 32)
                dve.tensor_scalar(wpos[:, :], cw, 0.0, None, ALU.max).then_inc(par, 1)
                dve.tensor_scalar(upos[:, :], cu, 0.0, None, ALU.max).then_inc(par, 1)
                dve.tensor_scalar(wneg[:, :], cw, 0.0, None, ALU.min).then_inc(par, 1)
                dve.tensor_scalar(nwrow[:, :], wrow[:, :], 0.0, -1.0, ALU.max, ALU.mult).then_inc(par, 1)
                dve.wait_ge(par, 4)
                dve.tensor_tensor(bias_now[:, :], cu, upos[:, :], ALU.subtract).then_inc(par, 1)
                dve.tensor_tensor(bias_state[:, :], wpos[:, :], upos[:, :], ALU.add).then_inc(par, 1)
                dve.wait_ge(par, 6)
                dve.tensor_scalar(bias_state[:, :], bias_state[:, :], -1.0, None, ALU.mult).then_inc(par, 1)
                for j in range(2):
                    dve.memset(s_scan[j][:, 0:1], 0.0).then_inc(par, 1)
                    dve.memset(q_scan[j][:, 0:1], 0.0).then_inc(par, 1)
                for b in range(B):
                    dve.wait_ge(x_loaded[b], 16)
                ln_stats(dve, stat, root_ready, X, stats, mv, rstd)

                def normalise(b, c, n):
                    for i in range(TPB):
                        t = b * TPB + i
                        ins = dve.tensor_scalar(xn[c % 2][:, i, :], X[:, t, c * P:(c + 1) * P], mv[:, t, 0:1],
                                                rstd[:, t:t + 1] if isinstance(t, int) else rstd[:, bass.ds(t, 1)],
                                                ALU.subtract, ALU.mult)
                    ins.then_inc(xn_ready, 1)

                dve.wait_ge(decay_ready, 1)
                with dve.Fori(0, B) as b:
                    for c in range(KC):
                        j, n = c % 2, b * KC + c
                        normalise(b, c, n)
                        dve.wait_ge(g_ready, n + 1)
                        dve.wait_ge(fst_ready, n + 1)
                        dve.tensor_tensor_scan(q_scan[j][:, 1:S + 1], decay[:, c:c + 1].to_broadcast([P, S]),
                                               g_state[j][:, :], 0.0, ALU.mult, ALU.add).then_inc(scan_done, 1)
                        dve.tensor_tensor_scan(s_scan[j][:, 1:S + 1], decay[:, c:c + 1].to_broadcast([P, S]),
                                               f_state[j][:, :], 0.0, ALU.mult, ALU.add).then_inc(scan_done, 1)
                        dve.wait_ge(fnow_ready, n + 1)
                        dve.wait_ge(scan_done, 2 * n + 2)
                        dve.tensor_tensor(den[j][:, :], q_scan[j][:, 0:S], g_now[j][:, :], ALU.add).then_inc(nd_done, 1)
                        dve.tensor_tensor(num[j][:, :], s_scan[j][:, 0:S], f_now[j][:, :], ALU.add).then_inc(nd_done, 1)
                        dve.wait_ge(nd_done, 2 * n + 2)
                        dve.tensor_copy(y[j][:, 0:1], v[j][:, 0:1]).then_inc(v_free, 1)
                        dve.reciprocal(den[j][:, :], den[j][:, :]).then_inc(rec_done, 1)
                        dve.wait_ge(rec_done, n + 1)
                        dve.tensor_tensor(y[j][:, 1:S], num[j][:, 1:S], den[j][:, 1:S], ALU.mult).then_inc(y_ready, 1)
                        dve.wait_ge(yt_ready, n + 1)
                        xs = X[:, bass.ds(b * TPB, TPB), c * P:(c + 1) * P]
                        dve.tensor_tensor(xs, py[j][:, :, :], xs, ALU.add).then_inc(x_added, 1)

            @block.scalar
            def _(act):
                act.sem_inc(v_free, 4)
                ln_root(act, stat, root_ready, rstd)
                act.wait_ge(par, 11)
                act.activation(decay[:, :], wneg[:, :], ACT.Exp).then_inc(decay_ready, 1)
                with act.Fori(0, B) as b:
                    for c in range(KC):
                        j, n = c % 2, b * KC + c
                        act.wait_ge(k_ready, n + 1)
                        act.activation(g_state[j][:, :], pk[j][:, :], ACT.Exp, bias=bias_state[:, c:c + 1])
                        act.activation(g_now[j][:, :], pk[j][:, :], ACT.Exp,
                                       bias=bias_now[:, c:c + 1]).then_inc(g_ready, 1)
                        act.wait_ge(v_loaded[j], (b * 2 + c // 2) * 16 + 16)
                        act.activation(ctxT_hi[:, c, bass.ds(b * S, S)], v[j][:, :], ACT.Copy).then_inc(hi_ready, 1)

            @block.gpsimd
            def _(pool):
                with pool.Fori(0, B) as b:
                    for c in range(KC):
                        j, n = c % 2, b * KC + c
                        pool.wait_ge(v_loaded[j], (b * 2 + c // 2) * 16 + 16)
                        pool.wait_ge(g_ready, n + 1)
                        pool.tensor_tensor(f_state[j][:, :], g_state[j][:, :], v[j][:, :],
                                           ALU.mult).then_inc(fst_ready, 1)
                        pool.tensor_tensor(f_now[j][:, :], g_now[j][:, :], v[j][:, :],
                                           ALU.mult).then_inc(fnow_ready, 1)
                        pool.wait_ge(hi_ready, n + 1)
                        pool.tensor_tensor(ctxT_lo[:, c, bass.ds(b * S, S)], v[j][:, :],
                                           ctxT_hi[:, c, bass.ds(b * S, S)], ALU.subtract).then_inc(v_free, 1)

            @block.tensor
            def _(pe):
                pe.wait_ge(par, 11)
                with pe.Fori(0, B) as b:
                    for c in range(KC):
                        j, n = c % 2, b * KC + c
                        pe.wait_ge(xn_ready, n + 1)
                        pe.matmul(pk[j][:, :], nwrow[0:1, c * P:(c + 1) * P], time_row[0:1, :],
                                  start=True, stop=False)
                        for i in range(TPB):
                            ins = pe.matmul(pk[j][:, i * P:(i + 1) * P], xn[j][:, i, :], ident[:, :],
                                            start=False, stop=(i == TPB - 1))
                        ins.then_inc(k_ready, 1)
                        pe.wait_ge(y_ready, n + 1)
                        for i in range(TPB):
                            ins = pe.transpose(py[j][:, i, :], y[j][:, i * P:(i + 1) * P], ident[:, :])
                        ins.then_inc(yt_ready, 1)


LEAD = 2


def ln_transpose(m, X, xnT, ident, router=None):
    xnT_hi, xnT_lo = xnT
    stats = m.sb("stats", [P, NT, 6], F32)
    mv = m.sb("mv", [P, NT, 2], F32)
    rstd = m.sb("rstd", [P, NT], F32)
    xn = [m.sb(f"xn{j}", [P, C], F32) for j in range(2)]
    xf = [m.sb(f"xf{j}", [P, KC, P], F32) for j in range(2)]
    pt = [m.ps(f"pt{j}", [P, KC, P], F32) for j in range(2)]
    pl = [m.ps(f"pl{j}", [P, E_ROUTED], F32) for j in range(2)] if router else None
    stat = m.sem("stat")
    root_ready = m.sem("root_ready")
    xn_ready = m.sem("xn_ready")
    pt_ready = m.sem("pt_ready")
    xf_ready = m.sem("xf_ready")
    lo_ready = m.sem("lo_ready")
    logit_ready = m.sem("logit_ready")
    aff_ready = m.sem("aff_ready")

    def vector(dve):
        ln_stats(dve, stat, root_ready, X, stats, mv, rstd)
        with dve.Fori(0, NT // 2) as i:
            for j in range(2):
                t = 2 * i + j
                dve.wait_ge(pt_ready, t + 1)
                dve.tensor_scalar(xn[j][:, :], X[:, t, :], mv[:, t, 0:1], rstd[:, bass.ds(t, 1)],
                                  ALU.subtract, ALU.mult).then_inc(xn_ready, 1)

    def tensor(pe):
        pe.sem_inc(pt_ready, LEAD)
        if router:
            pe.sem_inc(logit_ready, LEAD)
        with pe.Fori(0, NT // 2) as i:
            for j in range(2):
                t = 2 * i + j
                pe.wait_ge(xn_ready, t + 1)
                pe.wait_ge(xf_ready, t + 1)
                for k in range(KC):
                    ins = pe.transpose(pt[j][:, k, :], xn[j][:, k * P:(k + 1) * P], ident[:, :])
                ins.then_inc(pt_ready, 1)
                if router:
                    pe.wait_ge(xf_ready, t + 1 + LEAD)
                    pe.wait_ge(aff_ready, t + 1)
                    for k in range(KC):
                        ins = pe.matmul(pl[j][:, :], xf[j][:, k, :], router[0][:, k, :],
                                        start=(k == 0), stop=(k == KC - 1))
                    ins.then_inc(logit_ready, 1)

    def scalar(act):
        act.sem_inc(xf_ready, LEAD)
        if router:
            act.sem_inc(aff_ready, LEAD)
        ln_root(act, stat, root_ready, rstd)
        with act.Fori(0, NT // 2) as i:
            for j in range(2):
                t = 2 * i + j
                act.wait_ge(pt_ready, t + 1 + LEAD)
                act.wait_ge(lo_ready, t + 1)
                if router:
                    act.wait_ge(logit_ready, t + 1)
                act.activation(xnT_hi[:, :, bass.ds(t * P, P)], pt[j][:, :, :], ACT.Copy)
                act.activation(xf[j][:, :, :], pt[j][:, :, :], ACT.Copy).then_inc(xf_ready, 1)
                if router:
                    act.wait_ge(logit_ready, t + 1 + LEAD)
                    act.activation(router[1][:, t, :], pl[j][:, :], ACT.Sigmoid).then_inc(aff_ready, 1)

    def gpsimd(pool):
        pool.sem_inc(lo_ready, LEAD)
        with pool.Fori(0, NT // 2) as i:
            for j in range(2):
                t = 2 * i + j
                pool.wait_ge(xf_ready, t + 1 + LEAD)
                pool.tensor_tensor(xnT_lo[:, :, bass.ds(t * P, P)], xf[j][:, :, :],
                                   xnT_hi[:, :, bass.ds(t * P, P)], ALU.subtract).then_inc(lo_ready, 1)

    return vector, tensor, scalar, gpsimd, aff_ready


def stage_route(nc, X, xnT, gate, ident, centroids, gate_bias):
    with ExitStack() as stack:
        m = Names(nc, stack, "route")
        cent = m.sb("cent", [P, KC, E_ROUTED], F32)
        bias = m.sb("bias", [P, E_ROUTED], F32)
        aff = m.sb("aff", [P, NT, E_ROUTED], F32)
        biased = m.sb("biased", [P, NT, E_ROUTED], F32)
        top_v = m.sb("top_v", [P, NT, 8], F32)
        top_i = m.sb("top_i", [P, NT, 8], mybir.dt.uint32)
        top_f = m.sb("top_f", [P, NT, 2], F32)
        expert_no = m.sb("expert_no", [P, NT, E_ROUTED], F32)
        hot = [m.sb(f"hot{k}", [P, NT, E_ROUTED], F32) for k in range(2)]
        picked = m.sb("picked", [P, NT, E_ROUTED], F32)
        a = [m.sb(f"a{k}", [P, NT], F32) for k in range(2)]
        total = m.sb("total", [P, NT], F32)
        loaded = m.sem("loaded")
        counted = m.sem("counted")
        step = m.sem("step")
        vector, tensor, scalar, gpsimd, aff_ready = ln_transpose(m, X, xnT, ident, (cent, aff))

        with nc.Block() as block:
            @block.sync
            def _(sp):
                sp.dma_start(cent[:, :, :], centroids).then_inc(loaded, 16)
                sp.dma_start(bias[:, :], gate_bias).then_inc(loaded, 16)
                sp.wait_ge(loaded, 32)

            @block.tensor
            def _(pe):
                pe.wait_ge(loaded, 32)
                tensor(pe)

            @block.scalar
            def _(act):
                scalar(act)

            @block.gpsimd
            def _(pool):
                pool.iota(expert_no[:, :, :], [[0, NT], [1, E_ROUTED]], base=0, channel_multiplier=0,
                          allow_small_or_imprecise_dtypes=True).then_inc(counted, 1)
                gpsimd(pool)

            @block.vector
            def _(dve):
                vector(dve)
                done = Steps(dve, step)
                wide = [P, NT, E_ROUTED]
                dve.wait_ge(loaded, 32)
                dve.wait_ge(counted, 1)
                dve.wait_ge(aff_ready, NT + LEAD)
                done.mark(dve.tensor_tensor(biased[:, :, :], aff[:, :, :],
                                            bias[:, :].unsqueeze(1).to_broadcast(wide), ALU.add))
                done.wait()
                for t in range(NT):
                    done.mark(dve.max(top_v[:, t, :], biased[:, t, :]))
                done.wait()
                for t in range(NT):
                    done.mark(dve.max_index(top_i[:, t, :], top_v[:, t, :], biased[:, t, :]))
                done.wait()
                done.mark(dve.tensor_copy(top_f[:, :, :], top_i[:, :, 0:2]))
                done.wait()
                for k in range(2):
                    done.mark(dve.tensor_tensor(hot[k][:, :, :], expert_no[:, :, :],
                                                top_f[:, :, k:k + 1].to_broadcast(wide), ALU.is_equal))
                done.wait()
                for k in range(2):
                    done.mark(dve.tensor_tensor(picked[:, :, :], aff[:, :, :], hot[k][:, :, :], ALU.mult))
                    done.wait()
                    done.mark(dve.tensor_reduce(a[k][:, :], picked[:, :, :], AX.X, ALU.add))
                    done.wait()
                done.mark(dve.tensor_tensor(total[:, :], a[0][:, :], a[1][:, :], ALU.add))
                done.wait()
                done.mark(dve.tensor_scalar(total[:, :], total[:, :], 1e-9, None, ALU.add))
                done.wait()
                done.mark(dve.reciprocal(total[:, :], total[:, :]))
                done.wait()
                for k in range(2):
                    done.mark(dve.tensor_tensor(a[k][:, :], a[k][:, :], total[:, :], ALU.mult))
                done.wait()
                for k in range(2):
                    done.mark(dve.tensor_tensor(hot[k][:, :, :], hot[k][:, :, :],
                                                a[k][:, :].unsqueeze(2).to_broadcast(wide), ALU.mult))
                done.mark(dve.memset(gate[:, :, E_ROUTED:], 0.1))
                done.wait()
                done.mark(dve.tensor_tensor(gate[:, :, 0:E_ROUTED], hot[0][:, :, :], hot[1][:, :, :], ALU.add))
                done.wait()


def stage_norm(nc, X, xnT, ident):
    with ExitStack() as stack:
        vector, tensor, scalar, gpsimd, _ = ln_transpose(Names(nc, stack, "norm"), X, xnT, ident)
        with nc.Block() as block:
            block.tensor(tensor)
            block.scalar(scalar)
            block.vector(vector)
            block.gpsimd(gpsimd)


def stage_experts(nc, X, xnT, gate, w_gate_up, w_down):
    n_exp = w_gate_up.shape[0]
    NG = TOK // 512
    Y_LEAD = 2 * 4 * NG
    with ExitStack() as stack:
        m = Names(nc, stack, "exp")
        gu_f = m.sb("gu_f", [P, KC, 2 * F_EXP], F32)
        dn_f = m.sb("dn_f", [P, FC, C], F32)
        gu = [[m.sb(f"gu_{h}{j}", [P, KC, 2 * F_EXP], BF16) for h in ("hi", "lo")] for j in range(2)]
        dn = [[m.sb(f"dn_{h}{j}", [P, FC, C], BF16) for h in ("hi", "lo")] for j in range(2)]
        act_g = [m.sb(f"act_g{f}", [P, 512], F32) for f in range(FC)]
        hid = [m.sb(f"hid{f}", [P, 512], F32) for f in range(FC)]
        hid_hi = [m.sb(f"hid_hi{f}", [P, 512], BF16) for f in range(FC)]
        hid_lo = [m.sb(f"hid_lo{f}", [P, 512], BF16) for f in range(FC)]
        pg = [m.ps(f"pg{f}", [P, 512], F32) for f in range(FC)]
        pu = [m.ps(f"pu{f}", [P, 512], F32) for f in range(FC)]
        py = [m.ps(f"py{i}", [P, C], F32) for i in range(4)]

        w_loaded = m.sem("w_loaded")
        split = m.sem("split")
        turn = m.sem("turn")
        w_ready = m.sem("w_ready")
        pg_ready = m.sem("pg_ready")
        pu_ready = m.sem("pu_ready")
        g_ready = m.sem("g_ready")
        hid_ready = m.sem("hid_ready")
        hi_ready = m.sem("hi_ready")
        lo_ready = m.sem("lo_ready")
        y_ready = m.sem("y_ready")
        y_added = m.sem("y_added")

        with nc.Block() as block:
            @block.sync
            def _(sp):
                with sp.Fori(0, n_exp) as e:
                    sp.wait_ge(w_ready, 2 * e + 1)
                    sp.dma_start(gu_f[:, :, :], w_gate_up[e]).then_inc(w_loaded, 16)
                    sp.dma_start(dn_f[:, :, :], w_down[e]).then_inc(w_loaded, 16)

            @block.gpsimd
            def _(pool):
                pool.sem_inc(w_ready, 1)
                with pool.Fori(0, n_exp // 2) as e2:
                    for j in range(2):
                        e = 2 * e2 + j
                        pool.wait_ge(w_loaded, 32 * e + 32)
                        pool.wait_ge(y_ready, 4 * NG * (e + 1))
                        pool.sem_inc(turn, 1)
                        pool.tensor_copy(gu[j][0][:, :, :], gu_f[:, :, :]).then_inc(split, 1)
                        pool.tensor_copy(dn[j][0][:, :, :], dn_f[:, :, :]).then_inc(split, 1)
                        pool.wait_ge(split, 2 * e + 2)
                        pool.tensor_tensor(gu[j][1][:, :, :], gu_f[:, :, :], gu[j][0][:, :, :],
                                           ALU.subtract).then_inc(w_ready, 1)
                        pool.tensor_tensor(dn[j][1][:, :, :], dn_f[:, :, :], dn[j][0][:, :, :],
                                           ALU.subtract).then_inc(w_ready, 1)

            @block.tensor
            def _(pe):
                pe.sem_inc(y_ready, Y_LEAD)
                with pe.Fori(0, n_exp // 2) as e2:
                    for j in range(2):
                        with pe.Fori(0, NG) as g:
                            n = (2 * e2 + j) * NG + g
                            pe.wait_ge(w_ready, 2 * (2 * e2 + j) + 3)
                            for f in range(FC):
                                for which, bank, ready in ((0, pg, pg_ready), (1, pu, pu_ready)):
                                    pe.wait_ge((g_ready, hid_ready)[which], FC * n + f + 1)
                                    for k in range(KC):
                                        for a, b in ((0, 0), (0, 1), (1, 0)):
                                            col = which * F_EXP + f * P
                                            ins = pe.matmul(bank[f][:, :], gu[j][a][:, k, col:col + P],
                                                            xnT[b][:, k, bass.ds(g * 512, 512)],
                                                            start=(k == 0 and a + b == 0),
                                                            stop=(k == KC - 1 and a == 1))
                                    ins.then_inc(ready, 1)
                            for f in range(FC):
                                pe.wait_ge(lo_ready, FC * n + f + 1)
                                for i in range(4):
                                    if f == 0:
                                        pe.wait_ge(y_added, 4 * n + i + 1)
                                    for h, w in ((hid_hi, 0), (hid_hi, 1), (hid_lo, 0)):
                                        ins = pe.matmul(py[i][:, :], h[f][:, i * P:(i + 1) * P], dn[j][w][:, f, :],
                                                        start=(f == 0 and h is hid_hi and w == 0),
                                                        stop=(f == FC - 1 and h is hid_lo))
                                    if f == FC - 1:
                                        ins.then_inc(y_ready, 1)

            @block.scalar
            def _(act):
                act.sem_inc(g_ready, LEAD)
                with act.Fori(0, n_exp * NG) as n:
                    for f in range(FC):
                        act.wait_ge(pg_ready, FC * n + f + 1)
                        act.wait_ge(hid_ready, FC * n + f + 1)
                        act.activation(act_g[f][:, :], pg[f][:, :], ACT.Silu).then_inc(g_ready, 1)
                        act.wait_ge(hid_ready, FC * n + f + 1 + LEAD)
                        act.wait_ge(y_ready, 4 * n + Y_LEAD)
                        act.activation(hid_hi[f][:, :], hid[f][:, :], ACT.Copy).then_inc(hi_ready, 1)

            @block.vector
            def _(dve):
                dve.sem_inc(hid_ready, LEAD)
                dve.sem_inc(y_added, 4)
                with dve.Fori(0, n_exp) as e:
                    with dve.Fori(0, NG) as g:
                        n = e * NG + g
                        for f in range(FC):
                            dve.wait_ge(g_ready, FC * n + f + 1 + LEAD)
                            dve.wait_ge(pu_ready, FC * n + f + 1)
                            dve.tensor_tensor(hid[f][:, :], act_g[f][:, :], pu[f][:, :], ALU.mult).then_inc(hid_ready, 1)
                            dve.wait_ge(hi_ready, FC * n + f + 1)
                            dve.tensor_tensor(hid_lo[f][:, :], hid[f][:, :], hid_hi[f][:, :],
                                              ALU.subtract).then_inc(lo_ready, 1)
                        for i in range(4):
                            dve.wait_ge(y_ready, 4 * n + i + 1 + Y_LEAD)
                            xt = X[:, 4 * g + i, :]
                            dve.scalar_tensor_tensor(xt, py[i][:, :], gate[:, 4 * g + i, bass.ds(e, 1)], xt,
                                                     ALU.mult, ALU.add).then_inc(y_added, 1)


def stage_kv(nc, ctxT, KT, v_parts, ident, w_kv, bias_kv, kn_w):
    KW = NKV * HD
    with ExitStack() as stack:
        m = Names(nc, stack, "kv")
        w_f = m.sb("w_f", [P, 2, KC, KW], F32)
        w = [m.sb(f"w_{h}", [P, 2, KC, KW], BF16) for h in ("hi", "lo")]
        bias = m.sb("bias", [P, 2, KW], F32)
        kw = m.sb("kw", [P, HD], F32)
        V = [m.sb(f"V_{h}", [P, NKV, NT, HD], BF16) for h in ("hi", "lo")]
        kf = [m.sb(f"kf{j}", [P, KW], F32) for j in range(2)]
        ksq = m.sb("ksq", [P, KW], F32)
        ssq = m.sb("ssq", [P, NKV], F32)
        msq = m.sb("msq", [P, NKV], F32)
        root = m.sb("root", [P, NKV], F32)
        rk = m.sb("rk", [P, NKV], F32)
        kn = [m.sb(f"kn{j}", [P, KW], F32) for j in range(2)]
        vf = [m.sb(f"vf{j}", [P, KW], F32) for j in range(2)]
        pk = [m.ps(f"pk{j}", [P, KW], F32) for j in range(2)]
        pv = [m.ps(f"pv{j}", [P, KW], F32) for j in range(2)]
        pt = [m.ps(f"pt{j}", [P, NKV, P], F32) for j in range(2)]
        w_loaded = m.sem("w_loaded")
        c_loaded = m.sem("c_loaded")
        w_hi = m.sem("w_hi")
        w_lo = m.sem("w_lo")
        pk_ready = m.sem("pk_ready")
        pv_ready = m.sem("pv_ready")
        kf_ready = m.sem("kf_ready")
        sq_ready = m.sem("sq_ready")
        step = m.sem("step")
        msq_ready = m.sem("msq_ready")
        root_ready = m.sem("root_ready")
        kn_ready = m.sem("kn_ready")
        pt_ready = m.sem("pt_ready")
        khi_ready = m.sem("khi_ready")
        klo_ready = m.sem("klo_ready")
        vf_ready = m.sem("vf_ready")
        vhi_ready = m.sem("vhi_ready")
        vlo_ready = m.sem("vlo_ready")
        v_stored = m.sem("v_stored")

        with nc.Block() as block:
            @block.sync
            def _(sp):
                for i in range(2):
                    sp.dma_start(w_f[:, i, :, :], w_kv[i]).then_inc(w_loaded, 16)
                sp.dma_start(bias[:, :, :], bias_kv).then_inc(c_loaded, 16)
                sp.dma_start(kw[:, :], kn_w).then_inc(c_loaded, 16)
                sp.wait_ge(vlo_ready, NT + LEAD)
                sp.wait_ge(vhi_ready, NT)
                for h in range(2):
                    for g in range(NKV):
                        sp.dma_start(v_parts[g, h], V[h][:, g, :, :]).then_inc(v_stored, 16)
                sp.wait_ge(v_stored, 2 * NKV * 16)

            @block.tensor
            def _(pe):
                pe.sem_inc(pt_ready, LEAD)
                pe.wait_ge(w_hi, 1)
                pe.wait_ge(w_lo, 1)

                def project(t, j):
                    for which, bank, ready, free in ((0, pk, pk_ready, kf_ready), (1, pv, pv_ready, vf_ready)):
                        pe.wait_ge(free, t + 1)
                        for k in range(KC):
                            for a, b in ((0, 0), (0, 1), (1, 0)):
                                ins = pe.matmul(bank[j][:, :], ctxT[a][:, k, bass.ds(t * P, P)],
                                                w[b][:, which, k, :],
                                                start=(k == 0 and a + b == 0), stop=(k == KC - 1 and a == 1))
                        ins.then_inc(ready, 1)

                def transpose_k(t, j):
                    pe.wait_ge(kn_ready, t + 1)
                    pe.wait_ge(klo_ready, t + 1)
                    for h in range(NKV):
                        ins = pe.transpose(pt[j][:, h, :], kn[j][:, h * HD:(h + 1) * HD], ident[:, :])
                    ins.then_inc(pt_ready, 1)

                with pe.Fori(0, NT // 2) as i:
                    project(2 * i, 0)
                    project(2 * i + 1, 1)
                    transpose_k(2 * i, 0)
                    transpose_k(2 * i + 1, 1)

            @block.scalar
            def _(act):
                act.wait_ge(w_loaded, 32)
                act.activation(w[0][:, :, :, :], w_f[:, :, :, :], ACT.Copy).then_inc(w_hi, 1)

                def squares(t, j):
                    act.wait_ge(kf_ready, t + 1 + LEAD)
                    act.activation(ksq[:, :], kf[j][:, :], ACT.Square).then_inc(sq_ready, 1)
                    act.wait_ge(vf_ready, t + 1 + LEAD)
                    act.activation(V[0][:, :, t, :], vf[j][:, :].rearrange("p (g d) -> p g d", d=HD),
                                   ACT.Copy).then_inc(vhi_ready, 1)
                    act.wait_ge(msq_ready, t + 1)
                    act.activation(root[:, :], msq[:, :], ACT.Sqrt).then_inc(root_ready, 1)

                def high(t, j):
                    act.wait_ge(pt_ready, t + 1 + LEAD)
                    act.activation(KT[0][:, :, bass.ds(t * P, P)], pt[j][:, :, :], ACT.Copy).then_inc(khi_ready, 1)

                with act.Fori(0, NT // 2) as i:
                    squares(2 * i, 0)
                    squares(2 * i + 1, 1)
                    high(2 * i, 0)
                    high(2 * i + 1, 1)

            @block.vector
            def _(dve):
                dve.sem_inc(kf_ready, LEAD)
                dve.sem_inc(vf_ready, LEAD)
                dve.sem_inc(klo_ready, LEAD)
                dve.wait_ge(w_hi, 1)
                dve.tensor_tensor(w[1][:, :, :, :], w_f[:, :, :, :], w[0][:, :, :, :], ALU.subtract).then_inc(w_lo, 1)
                dve.wait_ge(c_loaded, 32)
                STEPS = 2

                def normalise(t, j):
                    done = Steps(dve, step, STEPS * t)
                    dve.wait_ge(pk_ready, t + 1)
                    dve.tensor_tensor(kf[j][:, :], pk[j][:, :], bias[:, 0, :], ALU.add).then_inc(kf_ready, 1)
                    dve.wait_ge(pv_ready, t + 1)
                    dve.wait_ge(vlo_ready, t + 1)
                    dve.tensor_tensor(vf[j][:, :], pv[j][:, :], bias[:, 1, :], ALU.add).then_inc(vf_ready, 1)
                    dve.wait_ge(sq_ready, t + 1)
                    done.mark(dve.tensor_reduce(ssq[:, :], ksq[:, :].rearrange("p (g d) -> p g d", d=HD),
                                                AX.X, ALU.add))
                    done.wait()
                    dve.tensor_scalar(msq[:, :], ssq[:, :], 1.0 / HD, RMS_EPS, ALU.mult, ALU.add).then_inc(msq_ready, 1)
                    dve.wait_ge(root_ready, t + 1)
                    done.mark(dve.reciprocal(rk[:, :], root[:, :]))
                    done.wait()
                    dve.wait_ge(pt_ready, t + 1)
                    for h in range(NKV):
                        s = slice(h * HD, (h + 1) * HD)
                        ins = dve.scalar_tensor_tensor(kn[j][:, s], kf[j][:, s], rk[:, h:h + 1], kw[:, :],
                                                       ALU.mult, ALU.mult)
                        if h == NKV - 1:
                            ins.then_inc(kn_ready, 1)
                    assert done.n == STEPS

                def low(t, j):
                    dve.wait_ge(khi_ready, t + 1)
                    dve.tensor_tensor(KT[1][:, :, bass.ds(t * P, P)], pt[j][:, :, :], KT[0][:, :, bass.ds(t * P, P)],
                                      ALU.subtract).then_inc(klo_ready, 1)

                with dve.Fori(0, NT // 2) as i:
                    normalise(2 * i, 0)
                    normalise(2 * i + 1, 1)
                    low(2 * i, 0)
                    low(2 * i + 1, 1)

            @block.gpsimd
            def _(pool):
                pool.sem_inc(vlo_ready, LEAD)
                with pool.Fori(0, NT // 2) as i:
                    for j in range(2):
                        t = 2 * i + j
                        pool.wait_ge(vhi_ready, t + 1)
                        pool.tensor_tensor(V[1][:, :, t, :], vf[j][:, :].rearrange("p (g d) -> p g d", d=HD),
                                           V[0][:, :, t, :], ALU.subtract).then_inc(vlo_ready, 1)


def stage_attention(nc, X, xnT, KT, v_parts, ident_bf, mask, w_q, w_o, bq_cols, qn_w):
    NIT = NKV * B
    with ExitStack() as stack:
        m = Names(nc, stack, "att")
        nmask = m.sb("nmask", [P, TPB, S], F32)
        wq_f = m.sb("wq_f", [P, KC, 512], F32)
        wo_f = m.sb("wo_f", [P, GROUP, C], F32)
        wq = [m.sb(f"wq_{h}", [P, KC, 512], BF16) for h in ("hi", "lo")]
        wo = [m.sb(f"wo_{h}", [P, GROUP, C], BF16) for h in ("hi", "lo")]
        V = [m.sb(f"V_{h}", [P, NT, HD], BF16) for h in ("hi", "lo")]
        bq = m.sb("bq", [P, NH], F32)
        qw = m.sb("qw", [P, 1], F32)
        nqw = m.sb("nqw", [P, 1], F32)
        eps = m.sb("eps", [P, 1], F32)
        ones = m.sb("ones", [P, P], BF16)
        qf = [m.sb(f"qf{j}", [P, S], F32) for j in range(2)]
        sq_f = m.sb("sq_f", [P, S], F32)
        sq = [m.sb(f"sq_{h}", [P, S], BF16) for h in ("hi", "lo")]
        rq = m.sb("rq", [P, S], F32)
        q = [m.sb(f"q_{h}", [P, GROUP, S], BF16) for h in ("hi", "lo")]
        s = [m.sb(f"s{j}", [P, S], F32) for j in range(2)]
        prob = [m.sb(f"prob{j}", [P, S], F32) for j in range(2)]
        p = [[m.sb(f"p_{h}{j}", [P, TPB, S], BF16) for h in ("hi", "lo")] for j in range(2)]
        low = m.sb("low", [P, 2, TPB], F32)
        total = m.sb("total", [P, 2, TPB], F32)
        inv = m.sb("inv", [P, 2, TPB], F32)
        pT = [m.sb(f"pT{j}", [P, 2, S], BF16) for j in range(2)]
        oT = [m.sb(f"oT_{h}", [P, GROUP, S], BF16) for h in ("hi", "lo")]
        bank_q = [m.ps(f"bank_q{j}", [P, 512], F32) for j in range(2)]
        bank_ss = m.ps("bank_ss", [P, 512], F32)
        bank_s = [m.ps(f"bank_s{j}", [P, 512], F32) for j in range(2)]
        bank_t = [m.ps(f"bank_t{j}", [P, 2, 512], BF16) for j in range(2)]
        bank_o = m.ps("bank_o", [P, 512], F32)

        c_loaded = m.sem("c_loaded")
        const_ready = m.sem("const_ready")
        wq_loaded = m.sem("wq_loaded")
        wo_loaded = m.sem("wo_loaded")
        v_loaded = m.sem("v_loaded")
        wq_split = m.sem("wq_split")
        wo_split = m.sem("wo_split")
        wo_turn = m.sem("wo_turn")
        turn = m.sem("turn")
        wo_high = m.sem("wo_high")
        q_proj = m.sem("q_proj")
        qf_ready = m.sem("qf_ready")
        sq_hi = m.sem("sq_hi")
        sqf_ready = m.sem("sqf_ready")
        sq_lo = m.sem("sq_lo")
        ss_ready = m.sem("ss_ready")
        ln_ready = m.sem("ln_ready")
        rq_ready = m.sem("rq_ready")
        qn_ready = m.sem("qn_ready")
        q_hi = m.sem("q_hi")
        q_lo = m.sem("q_lo")
        s_ready = m.sem("s_ready")
        s_done = m.sem("s_done")
        exp_done = m.sem("exp_done")
        inv_ready = m.sem("inv_ready")
        p_hi = m.sem("p_hi")
        p_lo = m.sem("p_lo")
        t_ready = m.sem("t_ready")
        t_even = m.sem("t_even")
        t_odd = m.sem("t_odd")
        pv_step = m.sem("pv_step")
        o_hi = m.sem("o_hi")
        o_lo = m.sem("o_lo")
        y_ready = m.sem("y_ready")
        x_added = m.sem("x_added")

        with nc.Block() as block:
            @block.sync
            def _(sp):
                sp.dma_start(nmask[:, :, :], mask).then_inc(c_loaded, 16)
                sp.dma_start(bq[:, :], bq_cols).then_inc(c_loaded, 16)
                sp.dma_start(qw[:, :], qn_w).then_inc(c_loaded, 16)
                with sp.Fori(0, NKV) as g:
                    sp.wait_ge(wq_split, 2 * g + 2)
                    sp.dma_start(wq_f[:, :, :], w_q[g]).then_inc(wq_loaded, 16)
                    sp.wait_ge(wo_split, g + 1)
                    sp.dma_start(wo_f[:, :, :], w_o[g]).then_inc(wo_loaded, 16)
                    sp.wait_ge(pv_step, g * B * GROUP * TPB + LEAD)
                    for h in range(2):
                        sp.dma_start(V[h][:, :, :], v_parts[g, h]).then_inc(v_loaded, 16)

            @block.tensor
            def _(pe):
                pe.sem_inc(ss_ready, 1)
                pe.sem_inc(pv_step, LEAD)
                pe.sem_inc(y_ready, 1)
                pe.wait_ge(const_ready, 4)

                def project(it, b, h):
                    n = GROUP * it + h
                    pe.wait_ge(qf_ready, n + 1)
                    if h < 2:
                        pe.wait_ge(x_added, 4 * it + 1)
                    for k in range(KC):
                        for a, c in ((0, 0), (1, 0), (0, 1)):
                            ins = pe.matmul(bank_q[h % 2][:, :], wq[a][:, k, h * HD:(h + 1) * HD],
                                            xnT[c][:, k, bass.ds(b * S, S)],
                                            start=(k == 0 and a + c == 0), stop=(k == KC - 1 and c == 1))
                    ins.then_inc(q_proj, 1)

                def sum_squares(it, h):
                    n = GROUP * it + h
                    pe.wait_ge(sq_hi, n + 1)
                    pe.wait_ge(sq_lo, n + 1)
                    pe.wait_ge(ln_ready, n + 1)
                    for a in range(2):
                        ins = pe.matmul(bank_ss[:, :], ones[:, :], sq[a][:, :], start=(a == 0), stop=(a == 1))
                    ins.then_inc(ss_ready, 1)

                def scores(it, g, b, h, i):
                    n = (GROUP * it + h) * TPB + i
                    if i == 0:
                        pe.wait_ge(q_hi, GROUP * it + h + 1)
                        pe.wait_ge(q_lo, GROUP * it + h + 1 + LEAD)
                    pe.wait_ge(s_done, n + 1)
                    for a, c in ((0, 0), (0, 1), (1, 0)):
                        ins = pe.matmul(bank_s[i % 2][:, :], q[a][:, h, i * P:(i + 1) * P],
                                        KT[c][:, g, bass.ds(b * S, S)],
                                        start=(a + c == 0), stop=(a == 1))
                    ins.then_inc(s_ready, 1)

                def transposes(it, h, i):
                    n = (GROUP * it + h) * TPB + i
                    if i == 0:
                        pe.wait_ge(p_lo, (GROUP * it + h + 1) * TPB + LEAD)
                    half = (GROUP * it + h) * (TPB // 2) + i // 2
                    pe.wait_ge((t_even, t_odd)[i % 2], half + 1)
                    for a in range(2):
                        for t in range(TPB):
                            ins = pe.transpose(bank_t[i % 2][:, a, t * P:(t + 1) * P],
                                               p[h % 2][a][:, t, i * P:(i + 1) * P], ident_bf[:, :])
                    ins.then_inc(t_ready, 1)

                def times_v(it, b, h, i):
                    half = (GROUP * it + h) * (TPB // 2) + i // 2
                    pe.wait_ge((t_even, t_odd)[i % 2], half + 2)
                    if i == 0:
                        pe.wait_ge(o_lo, GROUP * it + h + 1)
                    for a, c in ((0, 0), (0, 1), (1, 0)):
                        ins = pe.matmul(bank_o[:, :], V[a][:, b * TPB + i, :], pT[i % 2][:, c, :],
                                        start=(i == 0 and a + c == 0), stop=(i == TPB - 1 and a == 1))
                    ins.then_inc(pv_step, 1)

                def step(it, g, b, h):
                    for i in range(TPB):
                        if h < GROUP:
                            scores(it, g, b, h, i)
                        if h > 0:
                            transposes(it, h - 1, i)
                            if i > 0:
                                times_v(it, b, h - 1, i - 1)
                    if h > 0:
                        times_v(it, b, h - 1, TPB - 1)

                with pe.Fori(0, NKV) as g:
                    with pe.Fori(0, B) as b:
                        it = g * B + b
                        pe.wait_ge(wq_split, 2 * g + 4)
                        project(it, b, 0)
                        project(it, b, 1)
                        sum_squares(it, 0)
                        project(it, b, 2)
                        sum_squares(it, 1)
                        project(it, b, 3)
                        sum_squares(it, 2)
                        step(it, g, b, 0)
                        sum_squares(it, 3)
                        pe.wait_ge(v_loaded, 32 * g + 32)
                        for h in range(1, GROUP + 1):
                            step(it, g, b, h)
                        pe.wait_ge(wo_split, g + 2)
                        pe.wait_ge(o_lo, GROUP * it + GROUP + 1)
                        for i in range(4):
                            if i >= 2:
                                pe.wait_ge(x_added, 4 * it + i)
                            for h in range(GROUP):
                                for a, c in ((0, 0), (0, 1), (1, 0)):
                                    ins = pe.matmul(bank_q[i % 2][:, :], oT[a][:, h, i * P:(i + 1) * P], wo[c][:, h, :],
                                                    start=(h == 0 and a + c == 0), stop=(h == GROUP - 1 and a == 1))
                            ins.then_inc(y_ready, 1)

            @block.scalar
            def _(act):
                act.sem_inc(qf_ready, LEAD)
                act.sem_inc(ln_ready, 1)
                act.sem_inc(exp_done, LEAD)
                act.sem_inc(t_odd, 1)
                act.wait_ge(c_loaded, 48)
                act.wait_ge(const_ready, 4)

                def evacuate(it, g, h):
                    n = GROUP * it + h
                    act.wait_ge(q_proj, n + 1)
                    act.wait_ge(q_lo, n + 1)
                    bias = bq[:, bass.ds(g * GROUP + h, 1)]
                    act.wait_ge(ss_ready, n + 1)
                    act.activation(sq[0][:, :], bank_q[h % 2][:, :], ACT.Square, bias=bias).then_inc(sq_hi, 1)
                    act.activation(qf[h % 2][:, :], bank_q[h % 2][:, :], ACT.Identity, bias=bias).then_inc(qf_ready, 1)

                def root(it, h):
                    n = GROUP * it + h
                    act.wait_ge(ss_ready, n + 2)
                    act.wait_ge(qn_ready, n + 1)
                    act.activation(rq[:, :], bank_ss[:, :], ACT.Ln, bias=eps[:, :]).then_inc(ln_ready, 1)
                    act.wait_ge(ln_ready, n + 2)
                    act.activation(rq[:, :], rq[:, :], ACT.Exp, scale=-0.5).then_inc(rq_ready, 1)

                def high(it, h):
                    n = GROUP * it + h
                    act.wait_ge(qn_ready, n + 2)
                    act.activation(q[0][:, h, :], qf[h % 2][:, :], ACT.Copy).then_inc(q_hi, 1)

                def exponent(it, h, i):
                    n = (GROUP * it + h) * TPB + i
                    act.wait_ge(s_done, n + 1 + LEAD)
                    act.wait_ge(p_lo, n + 1)
                    act.activation(prob[i % 2][:, :], s[i % 2][:, :], ACT.Exp, scale=-1.0,
                                   bias=low[:, h % 2, i:i + 1],
                                   accum_out=total[:, h % 2, i:i + 1]).then_inc(exp_done, 1)

                def prob_high(it, h, i):
                    n = (GROUP * it + h) * TPB + i
                    act.wait_ge(inv_ready, n + 1)
                    act.activation(p[h % 2][0][:, i, :], prob[i % 2][:, :], ACT.Copy,
                                   scale=inv[:, h % 2, i:i + 1]).then_inc(p_hi, 1)

                def step(it, h):
                    for i in range(TPB):
                        if h < GROUP:
                            exponent(it, h, i)
                        if h > 0 and i % 2:
                            act.wait_ge(t_ready, (GROUP * it + h - 1) * TPB + i + 1)
                            act.wait_ge(pv_step, (GROUP * it + h - 1) * TPB + i + 1)
                            act.activation(pT[1][:, :, :], bank_t[1][:, :, :], ACT.Copy).then_inc(t_odd, 1)
                        if h < GROUP and i > 0:
                            prob_high(it, h, i - 1)
                    if h < GROUP:
                        prob_high(it, h, TPB - 1)
                    if h > 0:
                        act.wait_ge(pv_step, (GROUP * it + h) * TPB + LEAD)
                        act.wait_ge(y_ready, 4 * it + 1)
                        act.activation(oT[0][:, h - 1, :], bank_o[:, :], ACT.Copy).then_inc(o_hi, 1)

                with act.Fori(0, NKV) as g:
                    with act.Fori(0, B) as b:
                        it = g * B + b
                        evacuate(it, g, 0)
                        evacuate(it, g, 1)
                        root(it, 0)
                        high(it, 0)
                        root(it, 1)
                        evacuate(it, g, 2)
                        high(it, 1)
                        root(it, 2)
                        evacuate(it, g, 3)
                        high(it, 2)
                        step(it, 0)
                        root(it, 3)
                        high(it, 3)
                        for h in range(1, GROUP + 1):
                            step(it, h)

            @block.vector
            def _(dve):
                dve.sem_inc(qn_ready, 1)
                dve.sem_inc(wq_split, 2)
                dve.sem_inc(s_done, LEAD)
                dve.sem_inc(p_lo, LEAD)
                dve.sem_inc(t_even, 1)
                dve.sem_inc(o_lo, 1)
                dve.sem_inc(x_added, 1)
                dve.wait_ge(c_loaded, 48)
                dve.memset(ones[:, :], 1.0).then_inc(const_ready, 1)
                dve.memset(eps[:, :], HD * RMS_EPS).then_inc(const_ready, 1)
                dve.tensor_scalar(nqw[:, :], qw[:, :], -1.0, None, ALU.mult).then_inc(const_ready, 1)
                dve.tensor_scalar(nmask[:, :, :], nmask[:, :, :], -1.0, None, ALU.mult).then_inc(const_ready, 1)
                dve.wait_ge(const_ready, 4)

                def normalise(it, h):
                    n = GROUP * it + h
                    dve.wait_ge(rq_ready, n + 1)
                    dve.scalar_tensor_tensor(qf[h % 2][:, :], qf[h % 2][:, :], nqw[:, 0:1], rq[:, :],
                                             ALU.mult, ALU.mult).then_inc(qn_ready, 1)

                def mask_max(it, h, i):
                    n = (GROUP * it + h) * TPB + i
                    dve.wait_ge(s_ready, n + 1)
                    dve.wait_ge(exp_done, n + 1)
                    dve.sem_inc(turn, 1)
                    dve.tensor_tensor_reduce(s[i % 2][:, :], bank_s[i % 2][:, :], nmask[:, i, :], 1.0, 3.0e38,
                                             ALU.add, ALU.min, low[:, h % 2, i:i + 1]).then_inc(s_done, 1)

                def inverse(it, h, i):
                    n = (GROUP * it + h) * TPB + i
                    dve.wait_ge(exp_done, n + 1 + LEAD)
                    dve.reciprocal(inv[:, h % 2, i:i + 1], total[:, h % 2, i:i + 1]).then_inc(inv_ready, 1)

                def prob_low(it, h, i):
                    n = (GROUP * it + h) * TPB + i
                    dve.wait_ge(p_hi, n + 1)
                    dve.scalar_tensor_tensor(p[h % 2][1][:, i, :], prob[i % 2][:, :], inv[:, h % 2, i:i + 1],
                                             p[h % 2][0][:, i, :], ALU.mult, ALU.subtract).then_inc(p_lo, 1)

                def step(it, h):
                    for i in range(TPB):
                        if h < GROUP:
                            mask_max(it, h, i)
                            if i > 0:
                                inverse(it, h, i - 1)
                        if h > 0 and i % 2 == 0:
                            dve.wait_ge(t_ready, (GROUP * it + h - 1) * TPB + i + 1)
                            dve.wait_ge(pv_step, (GROUP * it + h - 1) * TPB + i + 1)
                            dve.tensor_copy(pT[0][:, :, :], bank_t[0][:, :, :]).then_inc(t_even, 1)
                        if h < GROUP and i > 0:
                            prob_low(it, h, i - 1)
                    if h < GROUP:
                        inverse(it, h, TPB - 1)
                        prob_low(it, h, TPB - 1)
                    if h > 0:
                        dve.wait_ge(o_hi, GROUP * it + h)
                        dve.tensor_tensor(oT[1][:, h - 1, :], bank_o[:, :], oT[0][:, h - 1, :],
                                          ALU.subtract).then_inc(o_lo, 1)

                with dve.Fori(0, NKV) as g:
                    dve.wait_ge(wq_loaded, 16 * g + 16)
                    dve.tensor_copy(wq[0][:, :, :], wq_f[:, :, :]).then_inc(wq_split, 1)
                    dve.wait_ge(wq_split, 2 * g + 3)
                    dve.tensor_tensor(wq[1][:, :, :], wq_f[:, :, :], wq[0][:, :, :], ALU.subtract).then_inc(wq_split, 1)
                    with dve.Fori(0, B) as b:
                        it = g * B + b
                        normalise(it, 0)
                        normalise(it, 1)
                        normalise(it, 2)
                        step(it, 0)
                        normalise(it, 3)
                        for h in range(1, GROUP + 1):
                            step(it, h)
                        for i in range(4):
                            dve.wait_ge(y_ready, 4 * it + i + 2)
                            xt = X[:, b * TPB + i, :]
                            dve.tensor_tensor(xt, bank_q[i % 2][:, :], xt, ALU.add).then_inc(x_added, 1)

            @block.gpsimd
            def _(pool):
                pool.sem_inc(q_lo, LEAD)
                pool.sem_inc(wo_split, 1)

                def square_low(it, h):
                    n = GROUP * it + h
                    pool.wait_ge(qf_ready, n + 1 + LEAD)
                    pool.tensor_tensor(sq_f[:, :], qf[h % 2][:, :], qf[h % 2][:, :], ALU.mult).then_inc(sqf_ready, 1)
                    pool.wait_ge(sqf_ready, n + 1)
                    pool.tensor_tensor(sq[1][:, :], sq_f[:, :], sq[0][:, :], ALU.subtract).then_inc(sq_lo, 1)

                def query_low(it, h):
                    n = GROUP * it + h
                    pool.wait_ge(q_hi, n + 1)
                    pool.tensor_tensor(q[1][:, h, :], qf[h % 2][:, :], q[0][:, h, :], ALU.subtract).then_inc(q_lo, 1)

                with pool.Fori(0, NKV) as g:
                    pool.wait_ge(wo_loaded, 16 * g + 16)
                    pool.wait_ge(y_ready, 4 * B * g + 1)
                    pool.sem_inc(wo_turn, 1)
                    pool.tensor_copy(wo[0][:, :, :], wo_f[:, :, :]).then_inc(wo_high, 1)
                    pool.wait_ge(wo_high, g + 1)
                    pool.tensor_tensor(wo[1][:, :, :], wo_f[:, :, :], wo[0][:, :, :], ALU.subtract).then_inc(wo_split, 1)
                    with pool.Fori(0, B) as b:
                        it = g * B + b
                        square_low(it, 0)
                        square_low(it, 1)
                        query_low(it, 0)
                        square_low(it, 2)
                        query_low(it, 1)
                        square_low(it, 3)
                        query_low(it, 2)
                        query_low(it, 3)


class Rounding:

    def __init__(self, m, width):
        self.v = [m.sb(f"v{j}", [P, width], F32) for j in range(2)]
        self.m = [m.sb(f"m{j}", [P, width], F32) for j in range(2)]
        self.v_ready = m.sem("v_ready")
        self.e_ready = m.sem("e_ready")
        self.m_ready = m.sem("m_ready")
        self.t_ready = m.sem("t_ready")
        self.o_ready = m.sem("o_ready")

    def scale(self, act, n, j, src, func, factor):
        act.wait_ge(self.o_ready, n + 1)
        act.activation(self.v[j][:, :], src, func, scale=factor).then_inc(self.v_ready, 1)

    def magic(self, dve, n, j):
        bits = self.m[j][:, :].bitcast(I32)
        dve.wait_ge(self.o_ready, n + 1)
        dve.wait_ge(self.v_ready, n + 1)
        dve.tensor_scalar(bits, self.v[j][:, :].bitcast(I32), 0x7F800000, None, ALU.bitwise_and).then_inc(self.e_ready, 1)
        dve.wait_ge(self.e_ready, n + 1)
        dve.tensor_scalar(self.m[j][:, :], self.m[j][:, :], 2.0 ** -6, 1.5 * 2.0 ** 20,
                          ALU.max, ALU.mult).then_inc(self.m_ready, 1)

    def add(self, pool, n, j):
        pool.wait_ge(self.m_ready, n + 1)
        pool.tensor_tensor(self.v[j][:, :], self.v[j][:, :], self.m[j][:, :], ALU.add).then_inc(self.t_ready, 1)

    def subtract(self, dve, n, j, out):
        dve.wait_ge(self.t_ready, n + 1)
        dve.tensor_tensor(out, self.v[j][:, :], self.m[j][:, :], ALU.subtract).then_inc(self.o_ready, 1)


def stage_quantise(nc, X, xqT, w8_fc, w8_proj_dram, scales, ident_bf, w_fc, w_proj):
    WIDTH = 1024
    NP = KC * FF // WIDTH
    with ExitStack() as stack:
        m = Names(nc, stack, "quant")
        w_f = [m.sb(f"w_f{i}", [P, KC * FF], F32) for i in range(2)]
        w8_proj = m.sb("w8_proj", [P, FFC * C], BF16)
        xn = m.sb("xn", [P, NT * C], F32)
        xq = [m.sb(f"xq{j}", [P, WIDTH], BF16) for j in range(2)]
        stats = m.sb("stats", [P, NT, 6], F32)
        mv = m.sb("mv", [P, NT, 2], F32)
        rstd = m.sb("rstd", [P, NT], F32)
        top = m.sb("top", [P, 3], F32)
        top_all = m.sb("top_all", [P, 3], F32)
        inv = m.sb("inv", [P, 3], F32)
        pt = [m.ps(f"pt{j}", [P, 8, P], BF16) for j in range(2)]
        rnd = Rounding(m, WIDTH)
        w_loaded = [m.sem(f"w_loaded{i}") for i in range(2)]
        stat = m.sem("stat")
        root_ready = m.sem("root_ready")
        xn_ready = m.sem("xn_ready")
        top_ready = m.sem("top_ready")
        all_ready = m.sem("all_ready")
        step = m.sem("step")
        pt_ready = m.sem("pt_ready")
        xt_ready = m.sem("xt_ready")
        stored = m.sem("stored")

        with nc.Block() as block:
            @block.sync
            def _(sp):
                sp.dma_start(w_f[0][:, :], w_fc).then_inc(w_loaded[0], 16)
                sp.dma_start(w_f[1][:, :], w_proj).then_inc(w_loaded[1], 16)
                sp.wait_ge(rnd.o_ready, 2 * NP + LEAD)
                sp.dma_start(w8_proj_dram, w8_proj[:, :]).then_inc(stored, 16)
                sp.wait_ge(stored, 16)

            @block.vector
            def _(dve):
                dve.sem_inc(rnd.o_ready, LEAD)
                ln_stats(dve, stat, root_ready, X, stats, mv, rstd)
                with dve.Fori(0, NT) as t:
                    dve.tensor_scalar(xn[:, bass.ds(t * C, C)], X[:, t, :], mv[:, t, 0:1], rstd[:, bass.ds(t, 1)],
                                      ALU.subtract, ALU.mult).then_inc(xn_ready, 1)
                for i, src in enumerate((w_f[0], w_f[1], xn)):
                    if i < 2:
                        dve.wait_ge(w_loaded[i], 16)
                    else:
                        dve.wait_ge(xn_ready, NT)
                    dve.tensor_reduce(top[:, i:i + 1], src[:, :], AX.X, ALU.max,
                                      apply_absolute_value=True).then_inc(top_ready, 1)
                done = Steps(dve, step)
                dve.wait_ge(all_ready, 1)
                done.mark(dve.tensor_scalar(scales[:, 0:3], top_all[:, :], 1.0 / FP8_MAX, 1e-6, ALU.mult, ALU.max))
                done.wait()
                done.mark(dve.reciprocal(inv[:, :], scales[:, 0:3]))
                for i, out in enumerate((w8_fc, w8_proj)):
                    flat = out[:, :, :].rearrange("p k f -> p (k f)") if i == 0 else out[:, :]
                    with dve.Fori(0, NP // 2) as c2:
                        for j in range(2):
                            rnd.magic(dve, i * NP + 2 * c2 + j, j)
                        for j in range(2):
                            rnd.subtract(dve, i * NP + 2 * c2 + j, j, flat[:, bass.ds((2 * c2 + j) * WIDTH, WIDTH)])
                with dve.Fori(0, NP // 2) as c2:
                    for j in range(2):
                        rnd.magic(dve, 2 * NP + 2 * c2 + j, j)
                    for j in range(2):
                        dve.wait_ge(pt_ready, 2 * c2 + j + 1)
                        rnd.subtract(dve, 2 * NP + 2 * c2 + j, j, xq[j][:, :])
                    for j in range(2):
                        c = 2 * c2 + j
                        dve.wait_ge(pt_ready, c + 1 + LEAD)
                        for i in range(2):
                            ins = dve.tensor_copy(xqT[:, :, bass.ds((2 * c + i) * P, P)],
                                                  pt[j][:, i * KC:(i + 1) * KC, :])
                        ins.then_inc(xt_ready, 1)

            @block.gpsimd
            def _(pool):
                pool.wait_ge(top_ready, 3)
                pool.partition_all_reduce(top_all[:, :], top[:, :], P, bass.bass_isa.ReduceOp.max).then_inc(all_ready, 1)
                with pool.Fori(0, 3 * NP // 2) as c2:
                    for j in range(2):
                        rnd.add(pool, 2 * c2 + j, j)

            @block.scalar
            def _(act):
                ln_root(act, stat, root_ready, rstd)
                act.wait_ge(step, 2)
                for i, src in enumerate((w_f[0], w_f[1], xn)):
                    with act.Fori(0, NP // 2) as c2:
                        for j in range(2):
                            c = 2 * c2 + j
                            rnd.scale(act, i * NP + c, j, src[:, bass.ds(c * WIDTH, WIDTH)], ACT.Copy, inv[:, i:i + 1])

            @block.tensor
            def _(pe):
                pe.sem_inc(pt_ready, LEAD)
                pe.sem_inc(xt_ready, LEAD)
                with pe.Fori(0, NP // 2) as c2:
                    for j in range(2):
                        c = 2 * c2 + j
                        pe.wait_ge(rnd.o_ready, 2 * NP + c + 1 + LEAD)
                        pe.wait_ge(xt_ready, c + 1)
                        for k in range(8):
                            ins = pe.transpose(pt[j][:, k, :], xq[j][:, k * P:(k + 1) * P], ident_bf[:, :])
                        ins.then_inc(pt_ready, 1)


def stage_up(nc, xqT, w8_fc, R, r_top, scales):
    NG = TOK // 512
    with ExitStack() as stack:
        m = Names(nc, stack, "up")
        s1 = m.sb("s1", [P, 1], F32)
        part = m.sb("part", [P, FFC * NG], F32)
        top = m.sb("top", [P, 1], F32)
        bank = [[m.ps(f"bank{j}_{g}", [P, 512], F32) for g in range(NG)] for j in range(2)]
        s1_ready = m.sem("s1_ready")
        z_ready = m.sem("z_ready")
        r_ready = m.sem("r_ready")
        part_ready = m.sem("part_ready")
        top_ready = m.sem("top_ready")
        all_ready = m.sem("all_ready")

        with nc.Block() as block:
            @block.tensor
            def _(pe):
                with pe.Fori(0, FFC // 2) as f2:
                    for j in range(2):
                        f = 2 * f2 + j
                        for k in range(KC):
                            for g in range(NG):
                                if k == 0:
                                    pe.wait_ge(r_ready, NG * f + g + 1)
                                ins = pe.matmul(bank[j][g][:, :], w8_fc[:, k, bass.ds(f * P, P)],
                                                xqT[:, k, g * 512:(g + 1) * 512], start=(k == 0), stop=(k == KC - 1))
                                if k == KC - 1:
                                    ins.then_inc(z_ready, 1)

            @block.scalar
            def _(act):
                act.sem_inc(r_ready, 2 * NG)
                act.wait_ge(s1_ready, 1)
                with act.Fori(0, FFC // 2) as f2:
                    for j in range(2):
                        f = 2 * f2 + j
                        for g in range(NG):
                            act.wait_ge(z_ready, NG * f + g + 1)
                            act.activation(R[:, f, g * 512:(g + 1) * 512], bank[j][g][:, :], ACT.Relu,
                                           scale=s1[:, 0:1]).then_inc(r_ready, 1)

            @block.vector
            def _(dve):
                dve.tensor_tensor(s1[:, :], scales[:, 2:3], scales[:, 0:1], ALU.mult).then_inc(s1_ready, 1)
                with dve.Fori(0, FFC) as f:
                    for g in range(NG):
                        dve.wait_ge(r_ready, NG * f + g + 1 + 2 * NG)
                        dve.tensor_reduce(part[:, bass.ds(NG * f + g, 1)], R[:, f, g * 512:(g + 1) * 512],
                                          AX.X, ALU.max).then_inc(part_ready, 1)
                dve.wait_ge(part_ready, NG * FFC)
                dve.tensor_reduce(top[:, :], part[:, :], AX.X, ALU.max).then_inc(top_ready, 1)

            @block.gpsimd
            def _(pool):
                pool.wait_ge(top_ready, 1)
                pool.partition_all_reduce(r_top[:, :], top[:, :], P, bass.bass_isa.ReduceOp.max).then_inc(all_ready, 1)
                pool.wait_ge(all_ready, 1)


def stage_down(nc, X, R, r_top, w8_proj_dram, scales, out):
    WIDTH = 1024
    NB = WIDTH // P
    HALVES = TOK // WIDTH
    with ExitStack() as stack:
        m = Names(nc, stack, "down")
        w8 = m.sb("w8", [P, FFC, C], BF16)
        h8 = [m.sb(f"h8{j}", [P, WIDTH], BF16) for j in range(2)]
        h_top = m.sb("h_top", [P, 1], F32)
        h_scale = m.sb("h_scale", [P, 1], F32)
        inv = m.sb("inv", [P, 1], F32)
        root = m.sb("root", [P, 1], F32)
        s2 = m.sb("s2", [P, 1], F32)
        rnd = Rounding(m, WIDTH)
        bank = [m.ps(f"bank{i}", [P, C], F32) for i in range(NB)]
        w_loaded = m.sem("w_loaded")
        step = m.sem("step")
        root_ready = m.sem("root_ready")
        h_used = m.sem("h_used")
        x_ready = m.sem("x_ready")
        stored = m.sem("stored")

        with nc.Block() as block:
            @block.sync
            def _(sp):
                sp.dma_start(w8[:, :, :], w8_proj_dram.rearrange("p (f c) -> p f c", c=C)).then_inc(w_loaded, 16)
                for t in range(NT):
                    b, i = t // TPB, t % TPB
                    sp.wait_ge(x_ready, t + 1 + NB)
                    sp.dma_start(out[b, i * P:(i + 1) * P, :], X[:, t, :]).then_inc(stored, 16)
                sp.wait_ge(stored, 16 * NT)

            @block.vector
            def _(dve):
                dve.sem_inc(rnd.o_ready, LEAD)
                dve.sem_inc(x_ready, NB)
                done = Steps(dve, step)
                done.mark(dve.tensor_tensor(h_top[:, :], r_top[:, :], r_top[:, :], ALU.mult))
                done.wait()
                done.mark(dve.tensor_scalar(h_scale[:, :], h_top[:, :], 1.0 / FP8_MAX, 1e-6, ALU.mult, ALU.max))
                done.wait()
                done.mark(dve.reciprocal(inv[:, :], h_scale[:, :]))
                done.mark(dve.tensor_tensor(s2[:, :], h_scale[:, :], scales[:, 1:2], ALU.mult))
                done.wait()
                with dve.Fori(0, HALVES) as half:
                    with dve.Fori(0, FFC // 2) as f2:
                        for j in range(2):
                            rnd.magic(dve, half * FFC + 2 * f2 + j, j)
                        for j in range(2):
                            n = half * FFC + 2 * f2 + j
                            dve.wait_ge(h_used, n + 1)
                            rnd.subtract(dve, n, j, h8[j][:, :])
                    for i in range(NB):
                        if i == 0:
                            dve.wait_ge(h_used, FFC * (half + 1) + LEAD)
                        xt = X[:, half * NB + i, :]
                        dve.scalar_tensor_tensor(xt, bank[i][:, :], s2[:, 0:1], xt, ALU.mult, ALU.add).then_inc(x_ready, 1)

            @block.scalar
            def _(act):
                act.wait_ge(step, 4)
                act.activation(root[:, :], inv[:, :], ACT.Sqrt).then_inc(root_ready, 1)
                act.wait_ge(root_ready, 1)
                with act.Fori(0, HALVES) as half:
                    with act.Fori(0, FFC // 2) as f2:
                        for j in range(2):
                            rnd.scale(act, half * FFC + 2 * f2 + j, j, R[:, 2 * f2 + j, bass.ds(half * WIDTH, WIDTH)],
                                      ACT.Square, root[:, 0:1])

            @block.gpsimd
            def _(pool):
                with pool.Fori(0, HALVES * FFC // 2) as n2:
                    for j in range(2):
                        rnd.add(pool, 2 * n2 + j, j)

            @block.tensor
            def _(pe):
                pe.sem_inc(h_used, LEAD)
                pe.wait_ge(w_loaded, 16)
                with pe.Fori(0, HALVES) as half:
                    for f in range(FFC):
                        n = half * FFC + f
                        pe.wait_ge(rnd.o_ready, n + 1 + LEAD)
                        for i in range(NB):
                            if f == 0:
                                pe.wait_ge(x_ready, half * NB + i + 1)
                            ins = pe.matmul(bank[i][:, :], h8[f % 2][:, i * P:(i + 1) * P], w8[:, f, :],
                                            start=(f == 0), stop=(f == FFC - 1))
                        ins.then_inc(h_used, 1)


def build(nc, x, ctx_t, wu_cols, w_row, centroids, gate_bias, w_gate_up, w_down,
          w_kv, bias_kv, kn_w, w_q, w_o, bq_cols, qn_w, mask, w_fc, w_proj, out):
    with ExitStack() as keep:
        def tensor(stack, name, shape, dt, **where):
            return stack.enter_context(nc.sbuf_tensor(name, shape, dt, **where))

        X = tensor(keep, "X", [P, NT, C], F32)
        ident = tensor(keep, "ident", [P, P], F32)
        ident_bf = tensor(keep, "ident_bf", [P, P], BF16)
        v_parts = nc.dram_tensor("v_parts", (NKV, 2, P, NT, HD), BF16, kind="Internal").ap()
        with ExitStack() as attention:
            KT = [tensor(attention, f"KT_{h}", [P, NKV, TOK], BF16) for h in ("hi", "lo")]
            with ExitStack() as first:
                ctxT = [tensor(first, f"ctxT_{h}", [P, KC, TOK], BF16) for h in ("hi", "lo")]
                with ExitStack() as wkv:
                    time_row = tensor(wkv, "time_row", [1, S], F32)
                    stage_setup(nc, ident, ident_bf, time_row)
                    stage_wkv(nc, X, ctxT, ident, time_row, x, ctx_t, wu_cols, w_row)
                stage_kv(nc, ctxT, KT, v_parts, ident, w_kv, bias_kv, kn_w)
            xnT = [tensor(attention, f"xnT_{h}", [P, KC, TOK], BF16) for h in ("hi", "lo")]
            with ExitStack() as moe:
                gate = tensor(moe, "gate", [P, NT, E_ROUTED + 2], F32)
                stage_route(nc, X, xnT, gate, ident, centroids, gate_bias)
                stage_experts(nc, X, xnT, gate, w_gate_up, w_down)
            stage_norm(nc, X, xnT, ident)
            stage_attention(nc, X, xnT, KT, v_parts, ident_bf, mask, w_q, w_o, bq_cols, qn_w)
        w8_proj = nc.dram_tensor("w8_proj", (P, FFC * C), BF16, kind="Internal").ap()
        scales = tensor(keep, "scales", [P, 3], F32)
        r_top = tensor(keep, "r_top", [P, 1], F32)
        with ExitStack() as hidden:
            with ExitStack() as up:
                right = bass.opposite_side(nc.default_side)
                xqT = tensor(up, "xqT", [P, KC, TOK], BF16, side=right)
                w8_fc = tensor(up, "w8_fc", [P, KC, FF], BF16, side=right)
                stage_quantise(nc, X, xqT, w8_fc, w8_proj, scales, ident_bf, w_fc, w_proj)
                R = tensor(hidden, "R", [P, FFC, TOK], F32)
                stage_up(nc, xqT, w8_fc, R, r_top, scales)
            stage_down(nc, X, R, r_top, w8_proj, scales, out)


def kernel(**inputs):
    import numpy as np
    import concourse.bacc as bacc
    from concourse.bass_utils import run_bass_kernel_spmd

    def host(name):
        return np.asarray(inputs[name])

    w, u = host("L0_xattn_w"), host("L0_xattn_u")
    wg, wu, wd = host("L0_ffn_wg"), host("L0_ffn_wu"), host("L0_ffn_wd")
    wgs, wus = (host(n).reshape(C, 2, F_EXP).transpose(1, 0, 2) for n in ("L0_ffn_wg_s", "L0_ffn_wu_s"))
    wds = host("L0_ffn_wd_s").reshape(2, F_EXP, C)
    gate_up = np.concatenate([np.concatenate([wg, wgs]), np.concatenate([wu, wus])], axis=2)
    down = np.concatenate([wd, wds])
    arrays = {
        "w_fc": host("L1_ffn_w_fc").T.reshape(KC, P, FF).transpose(1, 0, 2).reshape(P, KC * FF),
        "w_proj": host("L1_ffn_w_proj").T.reshape(FFC, P, C).transpose(1, 0, 2).reshape(P, FFC * C),
        "w_kv": np.stack([host(n).reshape(KC, P, NKV * HD).transpose(1, 0, 2) for n in ("L1_xattn_Wk", "L1_xattn_Wv")]),
        "bias_kv": np.tile(np.stack([host("L1_xattn_bk"), host("L1_xattn_bv")]), (P, 1, 1)),
        "kn_w": np.tile(host("L1_xattn_kn_w"), (P, 1)),
        "qn_w": host("L1_xattn_qn_w").reshape(P, 1),
        "bq_cols": host("L1_xattn_bq").reshape(NH, HD).T,
        "w_q": host("L1_xattn_Wq").reshape(KC, P, NKV, GROUP * HD).transpose(2, 1, 0, 3),
        "w_o": host("L1_xattn_Wo").reshape(NKV, GROUP, HD, C).transpose(0, 2, 1, 3),
        "mask": host("mask_1xSxS2_ff0")[0].reshape(TPB, P, S).transpose(1, 0, 2),
        "centroids": host("L0_ffn_centroids").T.reshape(KC, P, E_ROUTED).transpose(1, 0, 2),
        "gate_bias": np.tile(host("L0_ffn_gate_bias"), (P, 1)),
        "w_gate_up": gate_up.reshape(-1, KC, P, 2 * F_EXP).transpose(0, 2, 1, 3),
        "w_down": down.reshape(-1, FC, P, C).transpose(0, 2, 1, 3),
        "x": host("x"),
        "ctx_t": host("ctx_2048").transpose(0, 2, 1),
        "wu_cols": np.stack([w.reshape(KC, P).T, u.reshape(KC, P).T], axis=1),
        "w_row": w.reshape(1, C),
    }
    arrays = {name: np.ascontiguousarray(a) for name, a in arrays.items()}
    nc = bacc.Bacc("TRN2", target_bir_lowering=False, num_devices=1)
    aps = {name: nc.dram_tensor(name, a.shape, mybir.dt.from_np(a.dtype), kind="ExternalInput").ap()
           for name, a in arrays.items()}
    out = nc.dram_tensor("out", (B, S, C), F32, kind="ExternalOutput").ap()
    build(nc, out=out, **aps)
    r = run_bass_kernel_spmd(nc, [arrays], core_ids=[0])
    return r.results[0]["out"]
```

```python
from contextlib import ExitStack

import concourse.bass as bass
from concourse import mybir

F32 = mybir.dt.float32
BF16 = mybir.dt.bfloat16
I32 = mybir.dt.int32
U32 = mybir.dt.uint32
ALU = mybir.AluOpType
ACT = mybir.ActivationFunctionType
AX = mybir.AxisListType

P = 128
B, S, C = 4, 512, 512
TOK = B * S
NT = TOK // P
TPB = S // P
KC = C // P
LN_EPS = 1e-5
E_ROUTED = 16
F_EXP = 256
FC = F_EXP // P
SHARED_RATIO = 0.1
NH, NKV, HD = 16, 4, 128
GROUP = NH // NKV
RMS_EPS = 1e-6
FF = 2048
FFC = FF // P
FP8_MAX = 448.0


class Steps:

    def __init__(self, eng, sem, base=0):
        self.eng, self.sem, self.base, self.n = eng, sem, base, 0

    def mark(self, ins):
        ins.then_inc(self.sem, 1)
        self.n += 1

    def wait(self):
        self.eng.wait_ge(self.sem, self.base + self.n)


class Names:

    def __init__(self, nc, stack, stage):
        self.nc, self.stack, self.stage, self.sems = nc, stack, stage, []
        stack.callback(self.clear)

    def clear(self):
        self.nc.clear_and_free_semaphores(self.sems)
        self.nc.all_engine_barrier()

    def sb(self, name, shape, dt):
        return self.stack.enter_context(self.nc.sbuf_tensor(f"{self.stage}_{name}", shape, dt))

    def ps(self, name, shape, dt):
        return self.stack.enter_context(self.nc.psum_tensor(f"{self.stage}_{name}", shape, dt))

    def sem(self, name):
        self.sems.append(self.nc.alloc_semaphore(f"{self.stage}_{name}"))
        return self.sems[-1]


def stage_setup(nc, ident, ident_bf, time_row):
    made = nc.alloc_semaphore("setup_made")
    with nc.Block() as block:
        @block.gpsimd
        def _(pool):
            pool.memset(ident[:, :], 0.0).then_inc(made, 1)
            pool.memset(ident_bf[:, :], 0.0).then_inc(made, 1)
            pool.wait_ge(made, 2)
            for m in (ident, ident_bf):
                pool.affine_select(out=m[:, :], in_=m[:, :], compare_op=ALU.not_equal, fill=1.0, base=0,
                                   pattern=[[-1, P]], channel_multiplier=1).then_inc(made, 1)
            pool.iota(time_row[:, :], [[1, S]], base=0, channel_multiplier=0,
                      allow_small_or_imprecise_dtypes=True).then_inc(made, 1)
            pool.wait_ge(made, 5)


def ln_stats(dve, sem, root_ready, X, stats, mv, rstd, start=0):
    with dve.Fori(0, NT) as t:
        dve.bn_stats(stats[:, t, :], X[:, t, :]).then_inc(sem, 1)
    dve.wait_ge(sem, start + NT)
    for t in range(NT):
        dve.bn_aggr(mv[:, t, :], stats[:, t, :]).then_inc(sem, 1)
    dve.wait_ge(sem, start + 2 * NT)
    dve.tensor_scalar(rstd[:, :], mv[:, :, 1], LN_EPS, None, ALU.add).then_inc(sem, 1)
    dve.wait_ge(root_ready, 1)
    dve.reciprocal(rstd[:, :], rstd[:, :]).then_inc(sem, 1)
    dve.wait_ge(sem, start + 2 * NT + 2)


def ln_root(act, sem, root_ready, rstd, start=0):
    act.wait_ge(sem, start + 2 * NT + 1)
    act.activation(rstd[:, :], rstd[:, :], ACT.Sqrt).then_inc(root_ready, 1)


def stage_wkv(nc, X, ctxT, ident, time_row, x, ctx_t, wu_cols, w_row):
    ctxT_hi, ctxT_lo = ctxT
    with ExitStack() as stack:
        m = Names(nc, stack, "wkv")
        cols = m.sb("cols", [P, 2, KC], F32)
        cw, cu = cols[:, 0, :], cols[:, 1, :]
        wrow = m.sb("wrow", [1, C], F32)
        nwrow = m.sb("nwrow", [1, C], F32)
        wpos = m.sb("wpos", [P, KC], F32)
        upos = m.sb("upos", [P, KC], F32)
        wneg = m.sb("wneg", [P, KC], F32)
        bias_state = m.sb("bias_state", [P, KC], F32)
        bias_now = m.sb("bias_now", [P, KC], F32)
        decay = m.sb("decay", [P, KC], F32)
        stats = m.sb("stats", [P, NT, 6], F32)
        mv = m.sb("mv", [P, NT, 2], F32)
        rstd = m.sb("rstd", [P, NT], F32)
        xn = [m.sb(f"xn{j}", [P, TPB, P], F32) for j in range(2)]
        v = [m.sb(f"v{j}", [P, S], F32) for j in range(2)]
        g_state = [m.sb(f"g_state{j}", [P, S], F32) for j in range(2)]
        g_now = [m.sb(f"g_now{j}", [P, S], F32) for j in range(2)]
        f_state = [m.sb(f"f_state{j}", [P, S], F32) for j in range(2)]
        f_now = [m.sb(f"f_now{j}", [P, S], F32) for j in range(2)]
        s_scan = [m.sb(f"s_scan{j}", [P, S + 1], F32) for j in range(2)]
        q_scan = [m.sb(f"q_scan{j}", [P, S + 1], F32) for j in range(2)]
        num = [m.sb(f"num{j}", [P, S], F32) for j in range(2)]
        den = [m.sb(f"den{j}", [P, S], F32) for j in range(2)]
        y = [m.sb(f"y{j}", [P, S], F32) for j in range(2)]
        pk = [m.ps(f"pk{j}", [P, S], F32) for j in range(2)]
        py = [m.ps(f"py{j}", [P, TPB, P], F32) for j in range(2)]

        x_loaded = [m.sem(f"x_loaded{b}") for b in range(B)]
        par_loaded = m.sem("par_loaded")
        v_loaded = [m.sem(f"v_loaded{j}") for j in range(2)]
        par = m.sem("par")
        decay_ready = m.sem("decay_ready")
        stat = m.sem("stat")
        root_ready = m.sem("root_ready")
        xn_ready = m.sem("xn_ready")
        k_ready = m.sem("k_ready")
        g_ready = m.sem("g_ready")
        hi_ready = m.sem("hi_ready")
        fst_ready = m.sem("fst_ready")
        fnow_ready = m.sem("fnow_ready")
        scan_done = m.sem("scan_done")
        nd_done = m.sem("nd_done")
        rec_done = m.sem("rec_done")
        v_free = m.sem("v_free")
        y_ready = m.sem("y_ready")
        yt_ready = m.sem("yt_ready")
        x_added = m.sem("x_added")

        with nc.Block() as block:
            @block.sync
            def _(sp):
                sp.dma_start(cols[:, :, :], wu_cols).then_inc(par_loaded, 16)
                sp.dma_start(wrow[:, :], w_row).then_inc(par_loaded, 16)
                for b in range(B):
                    sp.dma_start(X[:, b * TPB:(b + 1) * TPB, :],
                                 x[b].rearrange("(t p) c -> p t c", p=P)).then_inc(x_loaded[b], 16)
                with sp.Fori(0, B) as b:
                    for c in range(KC):
                        j = c % 2
                        sp.wait_ge(v_free, 2 * (b * KC + c) + 2)
                        sp.dma_start(v[j][:, :], ctx_t[b, c * P:(c + 1) * P, :]).then_inc(v_loaded[j], 16)

            @block.vector
            def _(dve):
                dve.wait_ge(par_loaded, 32)
                dve.tensor_scalar(wpos[:, :], cw, 0.0, None, ALU.max).then_inc(par, 1)
                dve.tensor_scalar(upos[:, :], cu, 0.0, None, ALU.max).then_inc(par, 1)
                dve.tensor_scalar(wneg[:, :], cw, 0.0, None, ALU.min).then_inc(par, 1)
                dve.tensor_scalar(nwrow[:, :], wrow[:, :], 0.0, -1.0, ALU.max, ALU.mult).then_inc(par, 1)
                dve.wait_ge(par, 4)
                dve.tensor_tensor(bias_now[:, :], cu, upos[:, :], ALU.subtract).then_inc(par, 1)
                dve.tensor_tensor(bias_state[:, :], wpos[:, :], upos[:, :], ALU.add).then_inc(par, 1)
                dve.wait_ge(par, 6)
                dve.tensor_scalar(bias_state[:, :], bias_state[:, :], -1.0, None, ALU.mult).then_inc(par, 1)
                for j in range(2):
                    dve.memset(s_scan[j][:, 0:1], 0.0).then_inc(par, 1)
                    dve.memset(q_scan[j][:, 0:1], 0.0).then_inc(par, 1)
                for b in range(B):
                    dve.wait_ge(x_loaded[b], 16)
                ln_stats(dve, stat, root_ready, X, stats, mv, rstd)

                def normalise(b, c, n):
                    for i in range(TPB):
                        t = b * TPB + i
                        ins = dve.tensor_scalar(xn[c % 2][:, i, :], X[:, t, c * P:(c + 1) * P], mv[:, t, 0:1],
                                                rstd[:, t:t + 1] if isinstance(t, int) else rstd[:, bass.ds(t, 1)],
                                                ALU.subtract, ALU.mult)
                    ins.then_inc(xn_ready, 1)

                dve.wait_ge(decay_ready, 1)
                with dve.Fori(0, B) as b:
                    for c in range(KC):
                        j, n = c % 2, b * KC + c
                        normalise(b, c, n)
                        dve.wait_ge(g_ready, n + 1)
                        dve.wait_ge(fst_ready, n + 1)
                        dve.tensor_tensor_scan(q_scan[j][:, 1:S + 1], decay[:, c:c + 1].to_broadcast([P, S]),
                                               g_state[j][:, :], 0.0, ALU.mult, ALU.add).then_inc(scan_done, 1)
                        dve.tensor_tensor_scan(s_scan[j][:, 1:S + 1], decay[:, c:c + 1].to_broadcast([P, S]),
                                               f_state[j][:, :], 0.0, ALU.mult, ALU.add).then_inc(scan_done, 1)
                        dve.wait_ge(fnow_ready, n + 1)
                        dve.wait_ge(scan_done, 2 * n + 2)
                        dve.tensor_tensor(den[j][:, :], q_scan[j][:, 0:S], g_now[j][:, :], ALU.add).then_inc(nd_done, 1)
                        dve.tensor_tensor(num[j][:, :], s_scan[j][:, 0:S], f_now[j][:, :], ALU.add).then_inc(nd_done, 1)
                        dve.wait_ge(nd_done, 2 * n + 2)
                        dve.tensor_copy(y[j][:, 0:1], v[j][:, 0:1]).then_inc(v_free, 1)
                        dve.reciprocal(den[j][:, :], den[j][:, :]).then_inc(rec_done, 1)
                        dve.wait_ge(rec_done, n + 1)
                        dve.tensor_tensor(y[j][:, 1:S], num[j][:, 1:S], den[j][:, 1:S], ALU.mult).then_inc(y_ready, 1)
                        dve.wait_ge(yt_ready, n + 1)
                        xs = X[:, bass.ds(b * TPB, TPB), c * P:(c + 1) * P]
                        dve.tensor_tensor(xs, py[j][:, :, :], xs, ALU.add).then_inc(x_added, 1)

            @block.scalar
            def _(act):
                act.sem_inc(v_free, 4)
                ln_root(act, stat, root_ready, rstd)
                act.wait_ge(par, 11)
                act.activation(decay[:, :], wneg[:, :], ACT.Exp).then_inc(decay_ready, 1)
                with act.Fori(0, B) as b:
                    for c in range(KC):
                        j, n = c % 2, b * KC + c
                        act.wait_ge(k_ready, n + 1)
                        act.activation(g_state[j][:, :], pk[j][:, :], ACT.Exp, bias=bias_state[:, c:c + 1])
                        act.activation(g_now[j][:, :], pk[j][:, :], ACT.Exp,
                                       bias=bias_now[:, c:c + 1]).then_inc(g_ready, 1)
                        act.wait_ge(v_loaded[j], (b * 2 + c // 2) * 16 + 16)
                        act.activation(ctxT_hi[:, c, bass.ds(b * S, S)], v[j][:, :], ACT.Copy).then_inc(hi_ready, 1)

            @block.gpsimd
            def _(pool):
                with pool.Fori(0, B) as b:
                    for c in range(KC):
                        j, n = c % 2, b * KC + c
                        pool.wait_ge(v_loaded[j], (b * 2 + c // 2) * 16 + 16)
                        pool.wait_ge(g_ready, n + 1)
                        pool.tensor_tensor(f_state[j][:, :], g_state[j][:, :], v[j][:, :],
                                           ALU.mult).then_inc(fst_ready, 1)
                        pool.tensor_tensor(f_now[j][:, :], g_now[j][:, :], v[j][:, :],
                                           ALU.mult).then_inc(fnow_ready, 1)
                        pool.wait_ge(hi_ready, n + 1)
                        pool.tensor_tensor(ctxT_lo[:, c, bass.ds(b * S, S)], v[j][:, :],
                                           ctxT_hi[:, c, bass.ds(b * S, S)], ALU.subtract).then_inc(v_free, 1)

            @block.tensor
            def _(pe):
                pe.wait_ge(par, 11)
                with pe.Fori(0, B) as b:
                    for c in range(KC):
                        j, n = c % 2, b * KC + c
                        pe.wait_ge(xn_ready, n + 1)
                        pe.matmul(pk[j][:, :], nwrow[0:1, c * P:(c + 1) * P], time_row[0:1, :],
                                  start=True, stop=False)
                        for i in range(TPB):
                            ins = pe.matmul(pk[j][:, i * P:(i + 1) * P], xn[j][:, i, :], ident[:, :],
                                            start=False, stop=(i == TPB - 1))
                        ins.then_inc(k_ready, 1)
                        pe.wait_ge(y_ready, n + 1)
                        for i in range(TPB):
                            ins = pe.transpose(py[j][:, i, :], y[j][:, i * P:(i + 1) * P], ident[:, :])
                        ins.then_inc(yt_ready, 1)


LEAD = 2


def ln_transpose(m, X, xnT, ident, router=None):
    xnT_hi, xnT_lo = xnT
    stats = m.sb("stats", [P, NT, 6], F32)
    mv = m.sb("mv", [P, NT, 2], F32)
    rstd = m.sb("rstd", [P, NT], F32)
    xn = [m.sb(f"xn{j}", [P, C], F32) for j in range(2)]
    xf = [m.sb(f"xf{j}", [P, KC, P], F32) for j in range(2)]
    pt = [m.ps(f"pt{j}", [P, KC, P], F32) for j in range(2)]
    pl = [m.ps(f"pl{j}", [P, E_ROUTED], F32) for j in range(2)] if router else None
    stat = m.sem("stat")
    root_ready = m.sem("root_ready")
    xn_ready = m.sem("xn_ready")
    pt_ready = m.sem("pt_ready")
    xf_ready = m.sem("xf_ready")
    lo_ready = m.sem("lo_ready")
    logit_ready = m.sem("logit_ready")
    aff_ready = m.sem("aff_ready")
    row_hi = m.sem("row_hi")
    row_lo = m.sem("row_lo")

    def vector(dve):
        ln_stats(dve, stat, root_ready, X, stats, mv, rstd)
        with dve.Fori(0, NT // 2) as i:
            for j in range(2):
                t = 2 * i + j
                dve.wait_ge(pt_ready, t + 1)
                if router:
                    dve.wait_ge(row_lo, t + 1)
                dve.tensor_scalar(xn[j][:, :], X[:, t, :], mv[:, t, 0:1], rstd[:, bass.ds(t, 1)],
                                  ALU.subtract, ALU.mult).then_inc(xn_ready, 1)

    def tensor(pe):
        pe.sem_inc(pt_ready, LEAD)
        if router:
            pe.sem_inc(logit_ready, LEAD)
        with pe.Fori(0, NT // 2) as i:
            for j in range(2):
                t = 2 * i + j
                pe.wait_ge(xn_ready, t + 1)
                pe.wait_ge(xf_ready, t + 1)
                for k in range(KC):
                    ins = pe.transpose(pt[j][:, k, :], xn[j][:, k * P:(k + 1) * P], ident[:, :])
                ins.then_inc(pt_ready, 1)
                if router:
                    pe.wait_ge(xf_ready, t + 1 + LEAD)
                    pe.wait_ge(aff_ready, t + 1)
                    for k in range(KC):
                        ins = pe.matmul(pl[j][:, :], xf[j][:, k, :], router[0][:, k, :],
                                        start=(k == 0), stop=(k == KC - 1))
                    ins.then_inc(logit_ready, 1)

    def scalar(act):
        act.sem_inc(xf_ready, LEAD)
        if router:
            act.sem_inc(aff_ready, LEAD)
        ln_root(act, stat, root_ready, rstd)
        if router:
            act.preload_act_table(ACT.Sigmoid)
        with act.Fori(0, NT // 2) as i:
            for j in range(2):
                t = 2 * i + j
                if router:
                    act.wait_ge(xn_ready, t + 1)
                    act.activation(router[2][:, t, 0:C], xn[j][:, :], ACT.Copy).then_inc(row_hi, 1)
                act.wait_ge(pt_ready, t + 1 + LEAD)
                act.wait_ge(lo_ready, t + 1)
                if router:
                    act.wait_ge(logit_ready, t + 1)
                act.activation(xnT_hi[:, :, bass.ds(t * P, P)], pt[j][:, :, :], ACT.Copy)
                act.activation(xf[j][:, :, :], pt[j][:, :, :], ACT.Copy).then_inc(xf_ready, 1)
                if router:
                    act.wait_ge(logit_ready, t + 1 + LEAD)
                    act.activation(router[1][:, t, :], pl[j][:, :], ACT.Sigmoid).then_inc(aff_ready, 1)

    def gpsimd(pool):
        pool.sem_inc(lo_ready, LEAD)
        if router:
            pool.sem_inc(row_lo, LEAD)
        with pool.Fori(0, NT // 2) as i:
            for j in range(2):
                t = 2 * i + j
                if router:
                    pool.wait_ge(row_hi, t + 1)
                    pool.tensor_tensor(router[2][:, t, C:], xn[j][:, :], router[2][:, t, 0:C],
                                       ALU.subtract).then_inc(row_lo, 1)
                pool.wait_ge(xf_ready, t + 1 + LEAD)
                pool.tensor_tensor(xnT_lo[:, :, bass.ds(t * P, P)], xf[j][:, :, :],
                                   xnT_hi[:, :, bass.ds(t * P, P)], ALU.subtract).then_inc(lo_ready, 1)

    return vector, tensor, scalar, gpsimd, aff_ready


SLOTS = 256
SUB = SLOTS // P
TILES_R = (2 * TOK + E_ROUTED * (SLOTS - 1)) // SLOTS
W_ROW = KC * 2 * F_EXP + FC * C
GU = KC * 2 * F_EXP


def stage_route(nc, X, xnT, rows, share, slot, w_rows, ident, centroids, gate_bias):
    with ExitStack() as stack:
        m = Names(nc, stack, "route")
        wide = [P, NT, E_ROUTED]
        cent = m.sb("cent", [P, KC, E_ROUTED], F32)
        bias = m.sb("bias", [P, E_ROUTED], F32)
        aff = m.sb("aff", wide, F32)
        biased = m.sb("biased", wide, F32)
        top_v = m.sb("top_v", [P, NT, 8], F32)
        top_i = m.sb("top_i", [P, NT, 8], U32)
        top_f = m.sb("top_f", [P, NT, 2], F32)
        expert_no = m.sb("expert_no", wide, F32)
        tile_no = m.sb("tile_no", [P, TILES_R, E_ROUTED], F32)
        row_no = m.sb("row_no", [P, TILES_R], F32)
        earlier = m.sb("earlier", [P, P], BF16)
        ones = m.sb("ones", [P, P], BF16)
        hot = [m.sb(f"hot{k}", wide, F32) for k in range(2)]
        both = m.sb("both", [P, NT * E_ROUTED], BF16)
        picked = [m.sb(f"picked{k}", wide, F32) for k in range(2)]
        total = m.sb("total", [P, NT], F32)
        before = m.sb("before", [P, NT + 1, E_ROUTED], F32)
        filled = m.sb("filled", [P, E_ROUTED], F32)
        filled_i = m.sb("filled_i", [P, E_ROUTED], I32)
        tiles = m.sb("tiles", [P, E_ROUTED], F32)
        tiles_end = m.sb("tiles_end", [P, E_ROUTED], F32)
        base = m.sb("base", [P, E_ROUTED], F32)
        one_row = m.sb("one_row", [P, E_ROUTED], F32)
        place = m.sb("place", wide, F32)
        slot_f = [m.sb(f"slot_f{k}", [P, NT], F32) for k in range(2)]
        passed = m.sb("passed", [P, TILES_R, E_ROUTED], F32)
        owner = m.sb("owner", [P, TILES_R], F32)
        p_rank = m.ps("p_rank", [P, NT * E_ROUTED], F32)
        p_count = m.ps("p_count", [P, NT, E_ROUTED], F32)
        loaded = m.sem("loaded")
        made = m.sem("made")
        step = m.sem("step")
        both_ready = m.sem("both_ready")
        count_ready = m.sem("count_ready")
        vector, tensor, scalar, gpsimd, aff_ready = ln_transpose(m, X, xnT, ident, (cent, aff, rows))

        with nc.Block() as block:
            @block.sync
            def _(sp):
                sp.dma_start(cent[:, :, :], centroids).then_inc(loaded, 16)
                sp.dma_start(bias[:, :], gate_bias).then_inc(loaded, 16)
                sp.wait_ge(loaded, 32)

            @block.tensor
            def _(pe):
                pe.wait_ge(loaded, 32)
                tensor(pe)
                pe.wait_ge(both_ready, 1)
                pe.wait_ge(made, 6)
                pe.matmul(p_count[:, :, :].rearrange("p t e -> p (t e)"), ones[:, :], both[:, :],
                          start=True, stop=True).then_inc(count_ready, 1)
                pe.matmul(p_rank[:, :], earlier[:, :], both[:, :], start=True, stop=True).then_inc(count_ready, 1)

            @block.scalar
            def _(act):
                scalar(act)

            @block.gpsimd
            def _(pool):
                pool.iota(expert_no[:, :, :], [[0, NT], [1, E_ROUTED]], base=0, channel_multiplier=0,
                          allow_small_or_imprecise_dtypes=True).then_inc(made, 1)
                pool.iota(tile_no[:, :, :], [[1, TILES_R], [0, E_ROUTED]], base=0, channel_multiplier=0,
                          allow_small_or_imprecise_dtypes=True).then_inc(made, 1)
                pool.iota(row_no[:, :], [[0, TILES_R]], base=0, channel_multiplier=1,
                          allow_small_or_imprecise_dtypes=True).then_inc(made, 1)
                pool.memset(ones[:, :], 1.0).then_inc(made, 1)
                pool.memset(earlier[:, :], 1.0).then_inc(made, 1)
                pool.wait_ge(made, 5)
                pool.affine_select(out=earlier[:, :], in_=earlier[:, :], compare_op=ALU.is_gt, fill=0.0, base=0,
                                   pattern=[[1, P]], channel_multiplier=-1).then_inc(made, 1)
                gpsimd(pool)

            @block.vector
            def _(dve):
                dve.memset(before[:, 0, :], 0.0).then_inc(step, 1)
                dve.memset(one_row[:, :], 1.0).then_inc(step, 1)
                vector(dve)
                done = Steps(dve, step)
                done.n = 2
                dve.wait_ge(loaded, 32)
                dve.wait_ge(made, 3)
                dve.wait_ge(aff_ready, NT + LEAD)
                done.mark(dve.tensor_tensor(biased[:, :, :], aff[:, :, :],
                                            bias[:, :].unsqueeze(1).to_broadcast(wide), ALU.add))
                done.wait()
                for t in range(NT):
                    done.mark(dve.max(top_v[:, t, :], biased[:, t, :]))
                done.wait()
                for t in range(NT):
                    done.mark(dve.max_index(top_i[:, t, :], top_v[:, t, :], biased[:, t, :]))
                done.wait()
                done.mark(dve.tensor_copy(top_f[:, :, :], top_i[:, :, 0:2]))
                done.wait()
                for k in range(2):
                    done.mark(dve.tensor_tensor(hot[k][:, :, :], expert_no[:, :, :],
                                                top_f[:, :, k:k + 1].to_broadcast(wide), ALU.is_equal))
                done.wait()
                dve.tensor_tensor(both[:, :], hot[0][:, :, :].rearrange("p t e -> p (t e)"),
                                  hot[1][:, :, :].rearrange("p t e -> p (t e)"), ALU.add).then_inc(both_ready, 1)
                for k in range(2):
                    done.mark(dve.tensor_tensor(picked[k][:, :, :], aff[:, :, :], hot[k][:, :, :], ALU.mult))
                done.wait()
                for k in range(2):
                    done.mark(dve.tensor_reduce(share[k][:, :], picked[k][:, :, :], AX.X, ALU.add))
                done.wait()
                done.mark(dve.tensor_tensor(total[:, :], share[0][:, :], share[1][:, :], ALU.add))
                done.wait()
                done.mark(dve.tensor_scalar(total[:, :], total[:, :], 1e-9, None, ALU.add))
                done.wait()
                done.mark(dve.reciprocal(total[:, :], total[:, :]))
                done.wait()
                for k in range(2):
                    done.mark(dve.tensor_tensor(share[k][:, :], share[k][:, :], total[:, :], ALU.mult))
                dve.wait_ge(count_ready, 2)
                for t in range(NT):
                    done.wait()
                    done.mark(dve.tensor_tensor(before[:, t + 1, :], before[:, t, :], p_count[:, t, :], ALU.add))
                done.wait()
                done.mark(dve.tensor_scalar(filled[:, :], before[:, NT, :], SLOTS - 1.0, None, ALU.add))
                done.wait()
                done.mark(dve.tensor_copy(filled_i[:, :], filled[:, :]))
                done.wait()
                done.mark(dve.tensor_scalar(filled_i[:, :], filled_i[:, :], SLOTS.bit_length() - 1, None,
                                            ALU.arith_shift_right))
                done.wait()
                done.mark(dve.tensor_copy(tiles[:, :], filled_i[:, :]))
                done.wait()
                done.mark(dve.tensor_tensor_scan(tiles_end[:, :], one_row[:, :], tiles[:, :], 0.0, ALU.mult, ALU.add))
                done.wait()
                done.mark(dve.tensor_tensor(base[:, :], tiles_end[:, :], tiles[:, :], ALU.subtract))
                done.wait()
                done.mark(dve.tensor_scalar(base[:, :], base[:, :], float(SLOTS), None, ALU.mult))
                done.mark(dve.tensor_tensor(place[:, :, :], p_rank[:, :].rearrange("p (t e) -> p t e", e=E_ROUTED),
                                            before[:, 0:NT, :], ALU.add))
                done.wait()
                done.mark(dve.tensor_tensor(place[:, :, :], place[:, :, :],
                                            base[:, :].unsqueeze(1).to_broadcast(wide), ALU.add))
                done.wait()
                for k in range(2):
                    done.mark(dve.tensor_tensor(picked[k][:, :, :], place[:, :, :], hot[k][:, :, :], ALU.mult))
                done.wait()
                for k in range(2):
                    done.mark(dve.tensor_reduce(slot_f[k][:, :], picked[k][:, :, :], AX.X, ALU.add))
                done.wait()
                for k in range(2):
                    done.mark(dve.tensor_copy(slot[k][:, :], slot_f[k][:, :]))
                done.mark(dve.tensor_tensor(passed[:, :, :], tile_no[:, :, :], tiles_end[:, :].unsqueeze(1)
                                            .to_broadcast([P, TILES_R, E_ROUTED]), ALU.is_ge))
                done.wait()
                done.mark(dve.tensor_reduce(owner[:, :], passed[:, :, :], AX.X, ALU.add))
                done.wait()
                done.mark(dve.tensor_scalar(owner[:, :], owner[:, :], E_ROUTED - 1.0, float(P), ALU.min, ALU.mult))
                done.wait()
                done.mark(dve.tensor_tensor(owner[:, :], owner[:, :], row_no[:, :], ALU.add))
                done.wait()
                done.mark(dve.tensor_copy(w_rows[:, :], owner[:, :]))
                done.wait()


def stage_norm(nc, X, xnT, ident):
    with ExitStack() as stack:
        vector, tensor, scalar, gpsimd, _ = ln_transpose(Names(nc, stack, "norm"), X, xnT, ident)
        with nc.Block() as block:
            block.tensor(tensor)
            block.scalar(scalar)
            block.vector(vector)
            block.gpsimd(gpsimd)


def stage_shared(nc, X, xnT, rows, slot, slot_rows, w_gate_up, w_down):
    n_exp = w_gate_up.shape[0]
    NG = TOK // 512
    Y_LEAD = 2 * 4 * NG
    with ExitStack() as stack:
        m = Names(nc, stack, "shared")
        gu_f = m.sb("gu_f", [P, KC, 2 * F_EXP], F32)
        dn_f = m.sb("dn_f", [P, FC, C], F32)
        gu = [[m.sb(f"gu_{h}{j}", [P, KC, 2 * F_EXP], BF16) for h in ("hi", "lo")] for j in range(2)]
        dn = [[m.sb(f"dn_{h}{j}", [P, FC, C], BF16) for h in ("hi", "lo")] for j in range(2)]
        act_g = [m.sb(f"act_g{f}", [P, 512], F32) for f in range(FC)]
        hid = [m.sb(f"hid{f}", [P, 512], F32) for f in range(FC)]
        hid_hi = [m.sb(f"hid_hi{f}", [P, 512], BF16) for f in range(FC)]
        hid_lo = [m.sb(f"hid_lo{f}", [P, 512], BF16) for f in range(FC)]
        pg = [m.ps(f"pg{f}", [P, 512], F32) for f in range(FC)]
        pu = [m.ps(f"pu{f}", [P, 512], F32) for f in range(FC)]
        py = [m.ps(f"py{i}", [P, C], F32) for i in range(4)]

        w_loaded = m.sem("w_loaded")
        split = m.sem("split")
        turn = m.sem("turn")
        w_ready = m.sem("w_ready")
        pg_ready = m.sem("pg_ready")
        pu_ready = m.sem("pu_ready")
        g_ready = m.sem("g_ready")
        hid_ready = m.sem("hid_ready")
        hi_ready = m.sem("hi_ready")
        lo_ready = m.sem("lo_ready")
        y_ready = m.sem("y_ready")
        y_added = m.sem("y_added")
        scattered = m.sem("scattered")

        with nc.Block() as block:
            @block.sync
            def _(sp):
                with sp.Fori(0, n_exp) as e:
                    sp.wait_ge(w_ready, 2 * e + 1)
                    sp.dma_start(gu_f[:, :, :], w_gate_up[e]).then_inc(w_loaded, 16)
                    sp.dma_start(dn_f[:, :, :], w_down[e]).then_inc(w_loaded, 16)

            @block.gpsimd
            def _(pool):
                pool.sem_inc(w_ready, 1)
                with pool.Fori(0, n_exp // 2) as e2:
                    for j in range(2):
                        e = 2 * e2 + j
                        pool.wait_ge(w_loaded, 32 * e + 32)
                        pool.wait_ge(y_ready, 4 * NG * (e + 1))
                        pool.sem_inc(turn, 1)
                        pool.tensor_copy(gu[j][0][:, :, :], gu_f[:, :, :]).then_inc(split, 1)
                        pool.tensor_copy(dn[j][0][:, :, :], dn_f[:, :, :]).then_inc(split, 1)
                        pool.wait_ge(split, 2 * e + 2)
                        pool.tensor_tensor(gu[j][1][:, :, :], gu_f[:, :, :], gu[j][0][:, :, :],
                                           ALU.subtract).then_inc(w_ready, 1)
                        pool.tensor_tensor(dn[j][1][:, :, :], dn_f[:, :, :], dn[j][0][:, :, :],
                                           ALU.subtract).then_inc(w_ready, 1)
                for t in range(NT):
                    for k in range(2):
                        pool.indirect_dma_start(slot_rows, bass.IndirectOffsetOnAxis(ap=slot[k][:, t:t + 1], axis=0),
                                                rows[:, t, :], None).then_inc(scattered, 16)
                pool.wait_ge(scattered, 2 * NT * 16)

            @block.tensor
            def _(pe):
                pe.sem_inc(y_ready, Y_LEAD)
                with pe.Fori(0, n_exp // 2) as e2:
                    for j in range(2):
                        with pe.Fori(0, NG) as g:
                            n = (2 * e2 + j) * NG + g
                            pe.wait_ge(w_ready, 2 * (2 * e2 + j) + 3)
                            for f in range(FC):
                                for which, bank, ready in ((0, pg, pg_ready), (1, pu, pu_ready)):
                                    pe.wait_ge((g_ready, hid_ready)[which], FC * n + f + 1)
                                    for k in range(KC):
                                        for a, b in ((0, 0), (0, 1), (1, 0)):
                                            col = which * F_EXP + f * P
                                            ins = pe.matmul(bank[f][:, :], gu[j][a][:, k, col:col + P],
                                                            xnT[b][:, k, bass.ds(g * 512, 512)],
                                                            start=(k == 0 and a + b == 0),
                                                            stop=(k == KC - 1 and a == 1))
                                    ins.then_inc(ready, 1)
                            for f in range(FC):
                                pe.wait_ge(lo_ready, FC * n + f + 1)
                                for i in range(4):
                                    if f == 0:
                                        pe.wait_ge(y_added, 4 * n + i + 1)
                                    for h, w in ((hid_hi, 0), (hid_hi, 1), (hid_lo, 0)):
                                        ins = pe.matmul(py[i][:, :], h[f][:, i * P:(i + 1) * P], dn[j][w][:, f, :],
                                                        start=(f == 0 and h is hid_hi and w == 0),
                                                        stop=(f == FC - 1 and h is hid_lo))
                                    if f == FC - 1:
                                        ins.then_inc(y_ready, 1)

            @block.scalar
            def _(act):
                act.preload_act_table(ACT.Silu)
                act.sem_inc(g_ready, LEAD)
                with act.Fori(0, n_exp * NG) as n:
                    for f in range(FC):
                        act.wait_ge(pg_ready, FC * n + f + 1)
                        act.wait_ge(hid_ready, FC * n + f + 1)
                        act.activation(act_g[f][:, :], pg[f][:, :], ACT.Silu).then_inc(g_ready, 1)
                        act.wait_ge(hid_ready, FC * n + f + 1 + LEAD)
                        act.wait_ge(y_ready, 4 * n + Y_LEAD)
                        act.activation(hid_hi[f][:, :], hid[f][:, :], ACT.Copy).then_inc(hi_ready, 1)

            @block.vector
            def _(dve):
                dve.sem_inc(hid_ready, LEAD)
                dve.sem_inc(y_added, 4)
                with dve.Fori(0, n_exp) as e:
                    with dve.Fori(0, NG) as g:
                        n = e * NG + g
                        for f in range(FC):
                            dve.wait_ge(g_ready, FC * n + f + 1 + LEAD)
                            dve.wait_ge(pu_ready, FC * n + f + 1)
                            dve.tensor_tensor(hid[f][:, :], act_g[f][:, :], pu[f][:, :], ALU.mult).then_inc(hid_ready, 1)
                            dve.wait_ge(hi_ready, FC * n + f + 1)
                            dve.tensor_tensor(hid_lo[f][:, :], hid[f][:, :], hid_hi[f][:, :],
                                              ALU.subtract).then_inc(lo_ready, 1)
                        for i in range(4):
                            dve.wait_ge(y_ready, 4 * n + i + 1 + Y_LEAD)
                            xt = X[:, 4 * g + i, :]
                            dve.scalar_tensor_tensor(xt, py[i][:, :], SHARED_RATIO, xt,
                                                     ALU.mult, ALU.add).then_inc(y_added, 1)


def stage_routed(nc, slot_rows, slot_out, w_rows, w_table):
    assert TILES_R % 2 == 1
    with ExitStack() as stack:
        m = Names(nc, stack, "routed")
        w_f = [m.sb(f"w_f{j}", [P, W_ROW], F32) for j in range(2)]
        w = [[m.sb(f"w_{h}{j}", [P, W_ROW], BF16) for h in ("hi", "lo")] for j in range(2)]
        row = [m.sb(f"row{j}", [P, 1], U32) for j in range(2)]
        xr = [m.sb(f"xr{j}", [P, SUB, 2 * C], BF16) for j in range(2)]
        xT = [[m.sb(f"xT_{h}{j}", [P, KC, SLOTS], BF16) for h in ("hi", "lo")] for j in range(2)]
        act_g = [m.sb(f"act_g{f}", [P, SLOTS], F32) for f in range(FC)]
        hid = [m.sb(f"hid{f}", [P, SLOTS], F32) for f in range(FC)]
        hid_p = [[[m.sb(f"hid_{h}{f}{j}", [P, SLOTS], BF16) for h in ("hi", "lo")] for f in range(FC)]
                 for j in range(2)]
        y = [m.sb(f"y{j}", [P, SUB, C], F32) for j in range(2)]
        pt = [m.ps(f"pt_{h}", [P, KC, SLOTS], BF16) for h in ("hi", "lo")]
        pg = [m.ps(f"pg{f}", [P, 512], F32) for f in range(FC)]
        pu = [m.ps(f"pu{f}", [P, 512], F32) for f in range(FC)]
        py = [m.ps(f"py{s}", [P, C], F32) for s in range(SUB)]
        ident_bf = m.sb("ident", [P, P], BF16)

        made = m.sem("made")
        x_loaded = [m.sem(f"x_loaded{j}") for j in range(2)]
        w_loaded = [m.sem(f"w_loaded{j}") for j in range(2)]
        stored = [m.sem(f"stored{j}") for j in range(2)]
        t_ready = m.sem("t_ready")
        xt_hi = m.sem("xt_hi")
        xt_lo = m.sem("xt_lo")
        gu_hi = m.sem("gu_hi")
        gu_lo = m.sem("gu_lo")
        dn_hi = m.sem("dn_hi")
        dn_lo = m.sem("dn_lo")
        turn = m.sem("turn")
        row_ready = m.sem("row_ready")
        pg_ready = m.sem("pg_ready")
        pu_ready = m.sem("pu_ready")
        g_ready = m.sem("g_ready")
        hid_ready = m.sem("hid_ready")
        hi_ready = m.sem("hi_ready")
        lo_ready = m.sem("lo_ready")
        y_ready = m.sem("y_ready")
        y_copied = m.sem("y_copied")

        def walk(eng, first, last, turn_of):
            i = first
            if i % 2:
                turn_of(i, 1)
                i += 1
            with eng.Fori(0, (last + 1 - i) // 2) as m2:
                for j in range(2):
                    turn_of(2 * m2 + i + j, j)
            if (last + 1 - i) % 2:
                turn_of(last, last % 2)

        with nc.Block() as block:
            @block.sync
            def _(sp):
                def load(i, j):
                    sp.wait_ge(t_ready, i + 1)
                    sp.dma_start(xr[j][:, :, :], slot_rows[bass.ds(i * SLOTS, SLOTS), :]
                                 .rearrange("(s p) c -> p s c", p=P)).then_inc(x_loaded[j], 16)

                def turn_of(i, j):
                    load(i + 2, j)
                    store(i, j)

                def store(i, j):
                    sp.wait_ge(y_copied, SUB * i + 2 * SUB)
                    sp.dma_start(slot_out[bass.ds(i * SLOTS, SLOTS), :].rearrange("(s p) c -> p s c", p=P),
                                 y[j][:, :, :]).then_inc(stored[j], 16)

                load(0, 0)
                load(1, 1)
                walk(sp, 0, TILES_R - 3, turn_of)
                store(TILES_R - 2, 1)
                store(TILES_R - 1, 0)
                for j in range(2):
                    sp.wait_ge(stored[j], 16 + 16 * ((TILES_R + 1 - j) // 2))

            @block.tensor
            def _(pe):
                pe.sem_inc(t_ready, LEAD)
                pe.sem_inc(pu_ready, 2 * FC)
                pe.sem_inc(y_ready, 2 * SUB)
                pe.wait_ge(made, 2)

                def transposes(i, j):
                    pe.wait_ge(x_loaded[j], 16 * ((i - j) // 2 + 1) if isinstance(i, int) else 8 * (i - j) + 16)
                    pe.wait_ge(xt_hi, i + LEAD)
                    pe.wait_ge(xt_lo, i + LEAD)
                    for h in range(2):
                        for s in range(SUB):
                            for k in range(KC):
                                ins = pe.transpose(pt[h][:, k, s * P:(s + 1) * P],
                                                   xr[j][:, s, h * C + k * P:h * C + (k + 1) * P], ident_bf[:, :])
                    ins.then_inc(t_ready, 1)

                def gate_up(i, j, f):
                    if f == 0:
                        pe.wait_ge(gu_lo, i + 1)
                        pe.wait_ge(xt_hi, i + 1 + LEAD)
                        pe.wait_ge(xt_lo, i + 1 + LEAD)
                    for which, bank, ready, free in ((0, pg, pg_ready, g_ready), (1, pu, pu_ready, hid_ready)):
                        pe.wait_ge(free, FC * i + f + 1)
                        for k in range(KC):
                            at = k * 2 * F_EXP + which * F_EXP + f * P
                            for a, b in ((0, 0), (0, 1), (1, 0)):
                                ins = pe.matmul(bank[f][:, 0:SLOTS], w[j][a][:, at:at + P], xT[j][b][:, k, :],
                                                start=(k == 0 and a + b == 0), stop=(k == KC - 1 and a == 1))
                        ins.then_inc(ready, 1)

                def down(i, j):
                    pe.wait_ge(dn_lo, i + 1)
                    for f in range(FC):
                        pe.wait_ge(lo_ready, FC * i + f + 1 + FC)
                        for s in range(SUB):
                            if f == 0:
                                pe.wait_ge(y_copied, SUB * i + s + 1)
                            for a, b in ((0, 0), (0, 1), (1, 0)):
                                at = GU + f * C
                                ins = pe.matmul(py[s][:, :], hid_p[j][f][a][:, s * P:(s + 1) * P],
                                                w[j][b][:, at:at + C], start=(f == 0 and a + b == 0),
                                                stop=(f == FC - 1 and a == 1))
                            if f == FC - 1:
                                ins.then_inc(y_ready, 1)

                def turn_of(i, j):
                    gate_up(i, j, 0)
                    transposes(i + 1, 1 - j)
                    down(i - 1, 1 - j)
                    gate_up(i, j, 1)

                transposes(0, 0)
                gate_up(0, 0, 0)
                transposes(1, 1)
                gate_up(0, 0, 1)
                walk(pe, 1, TILES_R - 2, turn_of)
                gate_up(TILES_R - 1, 0, 0)
                down(TILES_R - 2, 1)
                gate_up(TILES_R - 1, 0, 1)
                down(TILES_R - 1, 0)

            @block.scalar
            def _(act):
                act.preload_act_table(ACT.Silu)
                act.sem_inc(xt_hi, LEAD)
                act.sem_inc(g_ready, FC)

                def weights(i, j, part):
                    if part == 0:
                        act.wait_ge(w_loaded[j], 8 * (i - j) + 16)
                        act.wait_ge(pu_ready, FC * i + FC)
                    if part == 2:
                        act.wait_ge(y_ready, SUB * i + SUB)
                    at = slice(part * GU // 2, min((part + 1) * GU // 2, W_ROW))
                    ins = act.activation(w[j][0][:, at], w_f[j][:, at], ACT.Copy)
                    if part:
                        ins.then_inc((gu_hi, dn_hi)[part - 1], 1)

                def x_high(i, j):
                    act.wait_ge(t_ready, i + 1 + LEAD)
                    act.wait_ge(pu_ready, FC * i + FC)
                    act.activation(xT[j][0][:, :, :], pt[0][:, :, :], ACT.Copy).then_inc(xt_hi, 1)

                def silu(i, f):
                    act.wait_ge(pg_ready, FC * i + f + 1)
                    act.wait_ge(hid_ready, FC * i + f + 1)
                    act.activation(act_g[f][:, :], pg[f][:, 0:SLOTS], ACT.Silu).then_inc(g_ready, 1)

                def hidden_high(i, j, f):
                    act.wait_ge(hid_ready, FC * i + f + 1 + FC)
                    act.wait_ge(y_ready, SUB * i + SUB)
                    act.activation(hid_p[j][f][0][:, :], hid[f][:, :], ACT.Copy).then_inc(hi_ready, 1)

                def turn_of(i, j):
                    silu(i - 1, 1)
                    weights(i + 1, 1 - j, 0)
                    hidden_high(i - 1, 1 - j, 1)
                    weights(i + 1, 1 - j, 1)
                    silu(i, 0)
                    x_high(i + 1, 1 - j)
                    hidden_high(i, j, 0)
                    weights(i + 1, 1 - j, 2)

                for part in range(3):
                    weights(0, 0, part)
                x_high(0, 0)
                weights(1, 1, 0)
                weights(1, 1, 1)
                silu(0, 0)
                x_high(1, 1)
                hidden_high(0, 0, 0)
                weights(1, 1, 2)
                walk(act, 1, TILES_R - 2, turn_of)
                last = TILES_R - 1
                silu(last - 1, 1)
                hidden_high(last - 1, 1, 1)
                silu(last, 0)
                hidden_high(last, 0, 0)
                silu(last, 1)
                hidden_high(last, 0, 1)

            @block.vector
            def _(dve):
                dve.sem_inc(xt_lo, LEAD)
                dve.sem_inc(hid_ready, FC)
                dve.sem_inc(lo_ready, FC)
                dve.sem_inc(y_copied, SUB)
                dve.sem_inc(stored[0], 16)
                dve.sem_inc(stored[1], 16)

                def x_low(i, j):
                    dve.wait_ge(t_ready, i + 1 + LEAD)
                    dve.wait_ge(pu_ready, FC * i + FC)
                    dve.tensor_copy(xT[j][1][:, :, :], pt[1][:, :, :]).then_inc(xt_lo, 1)

                def hidden(i, f):
                    dve.wait_ge(g_ready, FC * i + f + 1 + FC)
                    dve.wait_ge(pu_ready, FC * i + f + 1 + 2 * FC)
                    dve.wait_ge(lo_ready, FC * i + f + 1)
                    dve.tensor_tensor(hid[f][:, :], act_g[f][:, :], pu[f][:, 0:SLOTS], ALU.mult).then_inc(hid_ready, 1)

                def hidden_low(i, j, f):
                    dve.wait_ge(hi_ready, FC * i + f + 1)
                    dve.tensor_tensor(hid_p[j][f][1][:, :], hid[f][:, :], hid_p[j][f][0][:, :],
                                      ALU.subtract).then_inc(lo_ready, 1)

                def down_low(i, j):
                    dve.wait_ge(dn_hi, i + 1)
                    dve.tensor_tensor(w[j][1][:, GU:], w_f[j][:, GU:], w[j][0][:, GU:], ALU.subtract).then_inc(dn_lo, 1)

                def copy_out(i, j):
                    for s in range(SUB):
                        dve.wait_ge(y_ready, SUB * i + s + 1 + 2 * SUB)
                        if s == 0:
                            dve.wait_ge(stored[j], 8 * (i - j) + 16)
                        dve.tensor_copy(y[j][:, s, :], py[s][:, :]).then_inc(y_copied, 1)

                def turn_of(i, j):
                    hidden(i - 1, 1)
                    hidden_low(i - 1, 1 - j, 1)
                    hidden(i, 0)
                    x_low(i + 1, 1 - j)
                    hidden_low(i, j, 0)
                    copy_out(i - 1, 1 - j)
                    down_low(i + 1, 1 - j)

                down_low(0, 0)
                x_low(0, 0)
                hidden(0, 0)
                x_low(1, 1)
                hidden_low(0, 0, 0)
                down_low(1, 1)
                walk(dve, 1, TILES_R - 2, turn_of)
                last = TILES_R - 1
                hidden(last - 1, 1)
                hidden_low(last - 1, 1, 1)
                hidden(last, 0)
                hidden_low(last, 0, 0)
                copy_out(last - 1, 1)
                hidden(last, 1)
                hidden_low(last, 0, 1)
                copy_out(last, 0)

            @block.gpsimd
            def _(pool):
                pool.memset(ident_bf[:, :], 0.0).then_inc(made, 1)
                pool.wait_ge(made, 1)
                pool.affine_select(out=ident_bf[:, :], in_=ident_bf[:, :], compare_op=ALU.not_equal, fill=1.0, base=0,
                                   pattern=[[-1, P]], channel_multiplier=1).then_inc(made, 1)

                def fetch(i, j):
                    pool.tensor_copy(row[j][:, :], w_rows[:, bass.ds(i, 1)]).then_inc(row_ready, 1)
                    pool.wait_ge(row_ready, i + 1)
                    pool.sem_inc(turn, 1)
                    pool.indirect_dma_start(w_f[j][:, :], None, w_table,
                                            bass.IndirectOffsetOnAxis(ap=row[j][:, :], axis=0)
                                            ).then_inc(w_loaded[j], 16)

                def low(i, j):
                    pool.wait_ge(gu_hi, i + 1)
                    pool.tensor_tensor(w[j][1][:, 0:GU], w_f[j][:, 0:GU], w[j][0][:, 0:GU],
                                       ALU.subtract).then_inc(gu_lo, 1)

                def turn_of(i, j):
                    low(i, j)
                    pool.wait_ge(gu_lo, i + 1)
                    pool.wait_ge(dn_lo, i + 1)
                    pool.sem_inc(turn, 1)
                    fetch(i + 2, j)

                fetch(0, 0)
                fetch(1, 1)
                walk(pool, 0, TILES_R - 3, turn_of)
                low(TILES_R - 2, 1)
                low(TILES_R - 1, 0)


def stage_combine(nc, X, share, slot, slot_out):
    DEPTH = 4
    with ExitStack() as stack:
        m = Names(nc, stack, "combine")
        y = [[m.sb(f"y{k}{j}", [P, C], F32) for k in range(2)] for j in range(DEPTH)]
        fetched = [m.sem(f"fetched{j}") for j in range(DEPTH)]
        x_added = m.sem("x_added")
        with nc.Block() as block:
            @block.gpsimd
            def _(pool):
                for t in range(NT):
                    if t >= DEPTH:
                        pool.wait_ge(x_added, 2 * (t - DEPTH + 1))
                    for k in range(2):
                        pool.indirect_dma_start(y[t % DEPTH][k][:, :], None, slot_out,
                                                bass.IndirectOffsetOnAxis(ap=slot[k][:, t:t + 1], axis=0)
                                                ).then_inc(fetched[t % DEPTH], 16)

            @block.vector
            def _(dve):
                for t in range(NT):
                    dve.wait_ge(fetched[t % DEPTH], 32 * (t // DEPTH + 1))
                    for k in range(2):
                        if k:
                            dve.wait_ge(x_added, 2 * t + 1)
                        dve.scalar_tensor_tensor(X[:, t, :], y[t % DEPTH][k][:, :], share[k][:, t:t + 1], X[:, t, :],
                                                 ALU.mult, ALU.add).then_inc(x_added, 1)


def stage_kv(nc, ctxT, KT, v_parts, ident, w_kv, bias_kv, kn_w, slot_rows):
    Z_TILES = 4
    KW = NKV * HD
    with ExitStack() as stack:
        m = Names(nc, stack, "kv")
        w_f = m.sb("w_f", [P, 2, KC, KW], F32)
        w = [m.sb(f"w_{h}", [P, 2, KC, KW], BF16) for h in ("hi", "lo")]
        bias = m.sb("bias", [P, 2, KW], F32)
        kw = m.sb("kw", [P, HD], F32)
        V = [m.sb(f"V_{h}", [P, NKV, NT, HD], BF16) for h in ("hi", "lo")]
        kf = [m.sb(f"kf{j}", [P, KW], F32) for j in range(2)]
        ksq = m.sb("ksq", [P, KW], F32)
        ssq = m.sb("ssq", [P, NKV], F32)
        msq = m.sb("msq", [P, NKV], F32)
        root = m.sb("root", [P, NKV], F32)
        rk = m.sb("rk", [P, NKV], F32)
        kn = [m.sb(f"kn{j}", [P, KW], F32) for j in range(2)]
        vf = [m.sb(f"vf{j}", [P, KW], F32) for j in range(2)]
        pk = [m.ps(f"pk{j}", [P, KW], F32) for j in range(2)]
        pv = [m.ps(f"pv{j}", [P, KW], F32) for j in range(2)]
        pt = [m.ps(f"pt{j}", [P, NKV, P], F32) for j in range(2)]
        zeros = m.sb("zeros", [P, Z_TILES, 2 * C], BF16)
        zeros_made = m.sem("zeros_made")
        zeroed = m.sem("zeroed")
        w_loaded = m.sem("w_loaded")
        c_loaded = m.sem("c_loaded")
        w_hi = m.sem("w_hi")
        w_lo = m.sem("w_lo")
        pk_ready = m.sem("pk_ready")
        pv_ready = m.sem("pv_ready")
        kf_ready = m.sem("kf_ready")
        sq_ready = m.sem("sq_ready")
        step = m.sem("step")
        msq_ready = m.sem("msq_ready")
        root_ready = m.sem("root_ready")
        kn_ready = m.sem("kn_ready")
        pt_ready = m.sem("pt_ready")
        khi_ready = m.sem("khi_ready")
        klo_ready = m.sem("klo_ready")
        vf_ready = m.sem("vf_ready")
        vhi_ready = m.sem("vhi_ready")
        vlo_ready = m.sem("vlo_ready")
        v_stored = m.sem("v_stored")

        with nc.Block() as block:
            @block.sync
            def _(sp):
                for i in range(2):
                    sp.dma_start(w_f[:, i, :, :], w_kv[i]).then_inc(w_loaded, 16)
                sp.dma_start(bias[:, :, :], bias_kv).then_inc(c_loaded, 16)
                sp.dma_start(kw[:, :], kn_w).then_inc(c_loaded, 16)
                sp.wait_ge(zeros_made, 1)
                n_zero = (slot_rows.shape[0] // P) // Z_TILES * Z_TILES
                with sp.Fori(0, n_zero // Z_TILES) as i:
                    sp.dma_start(slot_rows[bass.ds(i * (Z_TILES * P), Z_TILES * P), :]
                                 .rearrange("(s p) c -> p s c", p=P), zeros[:, :, :]).then_inc(zeroed, 16)
                rest = slot_rows.shape[0] // P - n_zero
                sp.dma_start(slot_rows[n_zero * P:, :].rearrange("(s p) c -> p s c", p=P),
                             zeros[:, 0:rest, :]).then_inc(zeroed, 16)
                sp.wait_ge(vlo_ready, NT + LEAD)
                sp.wait_ge(vhi_ready, NT)
                for h in range(2):
                    for g in range(NKV):
                        sp.dma_start(v_parts[g, h], V[h][:, g, :, :]).then_inc(v_stored, 16)
                sp.wait_ge(v_stored, 2 * NKV * 16)
                sp.wait_ge(zeroed, 16 * (n_zero // Z_TILES + 1))

            @block.tensor
            def _(pe):
                pe.sem_inc(pt_ready, LEAD)
                pe.wait_ge(w_hi, 1)
                pe.wait_ge(w_lo, 1)

                def project(t, j):
                    for which, bank, ready, free in ((0, pk, pk_ready, kf_ready), (1, pv, pv_ready, vf_ready)):
                        pe.wait_ge(free, t + 1)
                        for k in range(KC):
                            for a, b in ((0, 0), (0, 1), (1, 0)):
                                ins = pe.matmul(bank[j][:, :], ctxT[a][:, k, bass.ds(t * P, P)],
                                                w[b][:, which, k, :],
                                                start=(k == 0 and a + b == 0), stop=(k == KC - 1 and a == 1))
                        ins.then_inc(ready, 1)

                def transpose_k(t, j):
                    pe.wait_ge(kn_ready, t + 1)
                    pe.wait_ge(klo_ready, t + 1)
                    for h in range(NKV):
                        ins = pe.transpose(pt[j][:, h, :], kn[j][:, h * HD:(h + 1) * HD], ident[:, :])
                    ins.then_inc(pt_ready, 1)

                with pe.Fori(0, NT // 2) as i:
                    project(2 * i, 0)
                    project(2 * i + 1, 1)
                    transpose_k(2 * i, 0)
                    transpose_k(2 * i + 1, 1)

            @block.scalar
            def _(act):
                act.preload_act_table(ACT.Sqrt)
                act.wait_ge(w_loaded, 32)
                act.activation(w[0][:, :, :, :], w_f[:, :, :, :], ACT.Copy).then_inc(w_hi, 1)

                def squares(t, j):
                    act.wait_ge(kf_ready, t + 1 + LEAD)
                    act.activation(ksq[:, :], kf[j][:, :], ACT.Square).then_inc(sq_ready, 1)
                    act.wait_ge(vf_ready, t + 1 + LEAD)
                    act.activation(V[0][:, :, t, :], vf[j][:, :].rearrange("p (g d) -> p g d", d=HD),
                                   ACT.Copy).then_inc(vhi_ready, 1)
                    act.wait_ge(msq_ready, t + 1)
                    act.activation(root[:, :], msq[:, :], ACT.Sqrt).then_inc(root_ready, 1)

                def high(t, j):
                    act.wait_ge(pt_ready, t + 1 + LEAD)
                    act.activation(KT[0][:, :, bass.ds(t * P, P)], pt[j][:, :, :], ACT.Copy).then_inc(khi_ready, 1)

                with act.Fori(0, NT // 2) as i:
                    squares(2 * i, 0)
                    squares(2 * i + 1, 1)
                    high(2 * i, 0)
                    high(2 * i + 1, 1)

            @block.vector
            def _(dve):
                dve.sem_inc(kf_ready, LEAD)
                dve.sem_inc(vf_ready, LEAD)
                dve.sem_inc(klo_ready, LEAD)
                dve.wait_ge(w_hi, 1)
                dve.tensor_tensor(w[1][:, :, :, :], w_f[:, :, :, :], w[0][:, :, :, :], ALU.subtract).then_inc(w_lo, 1)
                dve.wait_ge(c_loaded, 32)
                STEPS = 2

                def normalise(t, j):
                    done = Steps(dve, step, STEPS * t)
                    dve.wait_ge(pk_ready, t + 1)
                    dve.tensor_tensor(kf[j][:, :], pk[j][:, :], bias[:, 0, :], ALU.add).then_inc(kf_ready, 1)
                    dve.wait_ge(pv_ready, t + 1)
                    dve.wait_ge(vlo_ready, t + 1)
                    dve.tensor_tensor(vf[j][:, :], pv[j][:, :], bias[:, 1, :], ALU.add).then_inc(vf_ready, 1)
                    dve.wait_ge(sq_ready, t + 1)
                    done.mark(dve.tensor_reduce(ssq[:, :], ksq[:, :].rearrange("p (g d) -> p g d", d=HD),
                                                AX.X, ALU.add))
                    done.wait()
                    dve.tensor_scalar(msq[:, :], ssq[:, :], 1.0 / HD, RMS_EPS, ALU.mult, ALU.add).then_inc(msq_ready, 1)
                    dve.wait_ge(root_ready, t + 1)
                    done.mark(dve.reciprocal(rk[:, :], root[:, :]))
                    done.wait()
                    dve.wait_ge(pt_ready, t + 1)
                    for h in range(NKV):
                        s = slice(h * HD, (h + 1) * HD)
                        ins = dve.scalar_tensor_tensor(kn[j][:, s], kf[j][:, s], rk[:, h:h + 1], kw[:, :],
                                                       ALU.mult, ALU.mult)
                        if h == NKV - 1:
                            ins.then_inc(kn_ready, 1)
                    assert done.n == STEPS

                def low(t, j):
                    dve.wait_ge(khi_ready, t + 1)
                    dve.tensor_tensor(KT[1][:, :, bass.ds(t * P, P)], pt[j][:, :, :], KT[0][:, :, bass.ds(t * P, P)],
                                      ALU.subtract).then_inc(klo_ready, 1)

                with dve.Fori(0, NT // 2) as i:
                    normalise(2 * i, 0)
                    normalise(2 * i + 1, 1)
                    low(2 * i, 0)
                    low(2 * i + 1, 1)

            @block.gpsimd
            def _(pool):
                pool.sem_inc(vlo_ready, LEAD)
                pool.memset(zeros[:, :, :], 0.0).then_inc(zeros_made, 1)
                with pool.Fori(0, NT // 2) as i:
                    for j in range(2):
                        t = 2 * i + j
                        pool.wait_ge(vhi_ready, t + 1)
                        pool.tensor_tensor(V[1][:, :, t, :], vf[j][:, :].rearrange("p (g d) -> p g d", d=HD),
                                           V[0][:, :, t, :], ALU.subtract).then_inc(vlo_ready, 1)


def stage_attention(nc, X, xnT, KT, v_parts, ident_bf, mask, w_q, w_o, bq_cols, qn_w):
    TILES = GROUP * TPB
    ITS = NKV * B
    T_LAG = 6
    V_LAG = T_LAG + 2
    Q_TURN = {3: 0, 0: 2, 1: 4, 2: 6}
    SLOTS_P = 4
    with ExitStack() as stack:
        m = Names(nc, stack, "att")
        nmask = m.sb("nmask", [P, TPB, S], F32)
        w_f = m.sb("w_f", [P, 4, 512], F32)
        wq = [m.sb(f"wq_{h}", [P, 2 * KC, 512], BF16) for h in ("hi", "lo")]
        wo = [m.sb(f"wo_{h}", [P, GROUP, C], BF16) for h in ("hi", "lo")]
        V = [m.sb(f"V_{h}", [P, 2 * TPB, HD], BF16) for h in ("hi", "lo")]
        bq = m.sb("bq", [P, NH], F32)
        qw = m.sb("qw", [P, 1], F32)
        nqw = m.sb("nqw", [P, 1], F32)
        eps = m.sb("eps", [P, 1], F32)
        ones = m.sb("ones", [P, P], BF16)
        qf = [m.sb(f"qf{h}", [P, S], F32) for h in range(GROUP)]
        sq_f = m.sb("sq_f", [P, S], F32)
        sq = [m.sb(f"sq_{h}", [P, S], BF16) for h in ("hi", "lo")]
        rq = m.sb("rq", [P, S], F32)
        q = [m.sb(f"q_{h}", [P, GROUP, S], BF16) for h in ("hi", "lo")]
        s = [m.sb(f"s{j}", [P, S], F32) for j in range(2)]
        prob = [m.sb(f"prob{j}", [P, S], F32) for j in range(SLOTS_P)]
        p = [[m.sb(f"p_{h}{j}", [P, TPB, S], BF16) for h in ("hi", "lo")] for j in range(2)]
        low = m.sb("low", [P, TILES], F32)
        total = m.sb("total", [P, TILES], F32)
        inv = m.sb("inv", [P, TILES], F32)
        pT = [m.sb(f"pT{j}", [P, 2, S], BF16) for j in range(2)]
        oT = [m.sb(f"oT_{h}", [P, GROUP + 1, S], BF16) for h in ("hi", "lo")]
        bank_q = m.ps("bank_q", [P, 512], F32)
        bank_ss = m.ps("bank_ss", [P, 512], F32)
        bank_s = [m.ps(f"bank_s{j}", [P, 512], F32) for j in range(2)]
        bank_t = [m.ps(f"bank_t{j}", [P, 2, 512], BF16) for j in range(2)]
        bank_o = m.ps("bank_o", [P, 512], F32)
        bank_y = m.ps("bank_y", [P, 512], F32)

        Y0, PV0, S0, T0 = 5, 2 * TILES, TILES, 2 * TPB
        c_loaded = m.sem("c_loaded")
        const_ready = m.sem("const_ready")
        w_loaded = m.sem("w_loaded")
        v_loaded = m.sem("v_loaded")
        wq_split = m.sem("wq_split")
        wo_split = m.sem("wo_split")
        w_high = m.sem("w_high")
        q_proj = m.sem("q_proj")
        qf_ready = m.sem("qf_ready")
        sqf_ready = m.sem("sqf_ready")
        sq_hi = m.sem("sq_hi")
        sq_lo = m.sem("sq_lo")
        ss_ready = m.sem("ss_ready")
        ln_ready = m.sem("ln_ready")
        rq_ready = m.sem("rq_ready")
        qn_ready = m.sem("qn_ready")
        q_hi = m.sem("q_hi")
        q_lo = m.sem("q_lo")
        act_turn = m.sem("act_turn")
        dve_turn = m.sem("dve_turn")
        pool_turn = m.sem("pool_turn")
        s_ready = m.sem("s_ready")
        s_done = m.sem("s_done")
        exp_done = m.sem("exp_done")
        inv_ready = m.sem("inv_ready")
        p_hi = m.sem("p_hi")
        p_lo = m.sem("p_lo")
        t_ready = m.sem("t_ready")
        t_even = m.sem("t_even")
        t_odd = m.sem("t_odd")
        pv_step = m.sem("pv_step")
        o_hi = m.sem("o_hi")
        o_lo = m.sem("o_lo")
        y_ready = m.sem("y_ready")
        x_added = m.sem("x_added")

        def o_slot(it, h):
            return it % 2 * GROUP if h == 0 else h

        def iterations(eng, turns):
            turns(0, True, False, True)
            with eng.Fori(1, ITS - 1) as it:
                turns(it, True, True, True)
            turns(ITS - 1, True, True, False)
            turns(ITS, False, True, False)

        def lagging(it, N, lag, cur, prev):
            if N >= lag:
                return (it, N - lag) if cur else None
            return (it - 1, N - lag + TILES) if prev else None

        def heads(it, N, delay, cur, nxt):
            for h, first in Q_TURN.items():
                if N == first + delay and (cur if h == GROUP - 1 else nxt):
                    yield (it, h) if h == GROUP - 1 else (it + 1, h)

        with nc.Block() as block:
            @block.sync
            def _(sp):
                sp.dma_start(nmask[:, :, :], mask).then_inc(c_loaded, 16)
                sp.dma_start(bq[:, :], bq_cols).then_inc(c_loaded, 16)
                sp.dma_start(qw[:, :], qn_w).then_inc(c_loaded, 16)
                with sp.Fori(0, NKV) as g:
                    for b in range(B):
                        it = g * B + b
                        sp.wait_ge(pv_step, TILES * (it - 1) + PV0)
                        sp.wait_ge(v_loaded, 32 * it + 16)
                        for h in range(2):
                            sp.dma_start(V[h][:, b % 2 * TPB:(b % 2 + 1) * TPB, :],
                                         v_parts[g, h, :, b * TPB:(b + 1) * TPB, :]).then_inc(v_loaded, 16)

            @block.tensor
            def _(pe):
                pe.sem_inc(q_proj, 1)
                pe.sem_inc(ss_ready, 1)
                pe.sem_inc(s_ready, S0)
                pe.sem_inc(t_ready, T0)
                pe.sem_inc(pv_step, PV0)
                pe.sem_inc(y_ready, Y0)
                pe.wait_ge(const_ready, 4)

                def project(it, h, half):
                    g, b = it // B, it % B
                    if half == 0:
                        pe.wait_ge(wq_split, g + 1)
                        pe.wait_ge(qf_ready, GROUP * it + h + 1)
                    for k in (range(KC // 2), range(KC // 2, KC))[half]:
                        for a, c in ((0, 0), (1, 0), (0, 1)):
                            ins = pe.matmul(bank_q[:, :], wq[a][:, g % 2 * KC + k, h * HD:(h + 1) * HD],
                                            xnT[c][:, k, bass.ds(b * S, S)],
                                            start=(k == 0 and a + c == 0), stop=(k == KC - 1 and c == 1))
                    if half == 1:
                        ins.then_inc(q_proj, 1)

                def sum_squares(it, h):
                    n = GROUP * it + h
                    pe.wait_ge(sq_lo, n + 2)
                    pe.wait_ge(ln_ready, n + 1)
                    for a in range(2):
                        ins = pe.matmul(bank_ss[:, :], ones[:, :], sq[a][:, :], start=(a == 0), stop=(a == 1))
                    ins.then_inc(ss_ready, 1)

                def scores(it, N):
                    h, i = N // TPB, N % TPB
                    if i == 0:
                        pe.wait_ge(q_hi, GROUP * it + h + 1)
                        pe.wait_ge(q_lo, GROUP * it + h + 1 + GROUP)
                    pe.wait_ge(s_done, TILES * it + N + 1)
                    for a, c in ((0, 0), (0, 1), (1, 0)):
                        ins = pe.matmul(bank_s[N % 2][:, :], q[a][:, h, i * P:(i + 1) * P],
                                        KT[c][:, it // B, bass.ds(it % B * S, S)],
                                        start=(a + c == 0), stop=(a == 1))
                    ins.then_inc(s_ready, 1)

                def transposes(it, N):
                    h, i = N // TPB, N % TPB
                    if i == 0:
                        pe.wait_ge(p_lo, TILES * it + N + TPB + SLOTS_P)
                    half = (TILES // 2) * it + N // 2
                    pe.wait_ge((t_even, t_odd)[N % 2], half + 1)
                    for a in range(2):
                        for t in range(TPB):
                            ins = pe.transpose(bank_t[N % 2][:, a, t * P:(t + 1) * P],
                                               p[h % 2][a][:, t, i * P:(i + 1) * P], ident_bf[:, :])
                    ins.then_inc(t_ready, 1)

                def times_v(it, N):
                    h, i = N // TPB, N % TPB
                    half = (TILES // 2) * it + N // 2
                    pe.wait_ge((t_even, t_odd)[N % 2], half + 2)
                    if N == 0:
                        pe.wait_ge(v_loaded, 32 * it + 48)
                    if i == 0:
                        pe.wait_ge(o_lo, GROUP * it + h + 1)
                    for a, c in ((0, 0), (0, 1), (1, 0)):
                        ins = pe.matmul(bank_o[:, :], V[a][:, it % 2 * TPB + i, :], pT[N % 2][:, c, :],
                                        start=(i == 0 and a + c == 0), stop=(i == TPB - 1 and a == 1))
                    ins.then_inc(pv_step, 1)

                def output(it, i, half):
                    if half == 0:
                        pe.wait_ge(x_added, 4 * it + i + 1)
                        if i == 0:
                            pe.wait_ge(o_lo, GROUP * it + GROUP + 1)
                            pe.wait_ge(wo_split, it // B * GROUP + GROUP)
                    for h in (range(GROUP // 2), range(GROUP // 2, GROUP))[half]:
                        for a, c in ((0, 0), (0, 1), (1, 0)):
                            ins = pe.matmul(bank_y[:, :], oT[a][:, o_slot(it, h), i * P:(i + 1) * P],
                                            wo[c][:, h, :],
                                            start=(h == 0 and a + c == 0), stop=(h == GROUP - 1 and a == 1))
                    if half == 1:
                        ins.then_inc(y_ready, 1)

                def turns(it, cur, prev, nxt):
                    for N in range(TILES):
                        if cur:
                            scores(it, N)
                        for it_h, h in heads(it, N, 5, cur, nxt):
                            sum_squares(it_h, h)
                        tile = lagging(it, N, T_LAG, cur, prev)
                        if tile:
                            transposes(*tile)
                        tile = lagging(it, N, V_LAG, cur, prev)
                        if tile and tile[1] % TPB:
                            times_v(*tile)
                        for half in range(2):
                            for it_h, h in heads(it, N, half, cur, nxt):
                                project(it_h, h, half)
                        if prev and N >= TILES // 2:
                            output(it - 1, (N - TILES // 2) // 2, N % 2)
                        if tile and tile[1] % TPB == 0:
                            times_v(*tile)

                for h in range(GROUP - 1):
                    for half in range(2):
                        project(0, h, half)
                    if h:
                        sum_squares(0, h - 1)
                sum_squares(0, GROUP - 2)
                iterations(pe, turns)

            @block.scalar
            def _(act):
                act.preload_act_table_set("natural_log_exp_and_others")
                act.sem_inc(qf_ready, 1)
                act.sem_inc(ln_ready, 1)
                act.sem_inc(exp_done, LEAD)
                act.sem_inc(t_odd, 1)
                act.wait_ge(c_loaded, 48)
                act.wait_ge(const_ready, 4)

                def evacuate(it, h):
                    n = GROUP * it + h
                    act.wait_ge(q_proj, n + 2)
                    act.wait_ge(q_lo, n + 1)
                    act.sem_inc(act_turn, 1)
                    act.activation(qf[h][:, :], bank_q[:, :], ACT.Identity,
                                   bias=bq[:, bass.ds(it // B * GROUP + h, 1)]).then_inc(qf_ready, 1)

                def root(it, h):
                    n = GROUP * it + h
                    act.wait_ge(ss_ready, n + 2)
                    act.wait_ge(qn_ready, n + 1)
                    act.activation(rq[:, :], bank_ss[:, :], ACT.Ln, bias=eps[:, :]).then_inc(ln_ready, 1)
                    act.wait_ge(ln_ready, n + 2)
                    act.activation(rq[:, :], rq[:, :], ACT.Exp, scale=-0.5).then_inc(rq_ready, 1)

                def query_high(it, h):
                    n = GROUP * it + h
                    act.wait_ge(qn_ready, n + 2)
                    act.wait_ge(s_ready, TPB * (n - GROUP + 1) + S0)
                    act.activation(q[0][:, h, :], qf[h][:, :], ACT.Copy).then_inc(q_hi, 1)

                def exponent(it, N):
                    n = TILES * it + N
                    act.wait_ge(s_done, n + 1 + LEAD)
                    act.wait_ge(p_lo, n + 1)
                    act.activation(prob[N % SLOTS_P][:, :], s[N % 2][:, :], ACT.Exp, scale=-1.0, bias=low[:, N:N + 1],
                                   accum_out=total[:, N:N + 1]).then_inc(exp_done, 1)

                def prob_high(it, N):
                    n = TILES * it + N
                    act.wait_ge(inv_ready, n + 1)
                    if N % TPB == 0:
                        act.wait_ge(t_ready, n + TPB)
                    act.activation(p[N // TPB % 2][0][:, N % TPB, :], prob[N % SLOTS_P][:, :], ACT.Copy,
                                   scale=inv[:, N:N + 1]).then_inc(p_hi, 1)

                def copy_odd(it, N):
                    act.wait_ge(t_ready, TILES * it + N + 1 + T0)
                    act.wait_ge(pv_step, TILES * it + N - 1 + PV0)
                    act.activation(pT[1][:, :, :], bank_t[1][:, :, :], ACT.Copy).then_inc(t_odd, 1)

                def value_high(it, h):
                    act.wait_ge(pv_step, TILES * it + TPB * (h + 1) + PV0)
                    act.wait_ge(y_ready, 4 * (it - (h == 0)) + Y0)
                    act.activation(oT[0][:, o_slot(it, h), :], bank_o[:, :], ACT.Copy).then_inc(o_hi, 1)

                def turns(it, cur, prev, nxt):
                    for N in range(TILES):
                        tile = lagging(it, N, V_LAG + 1, cur, prev)
                        if tile and tile[1] % TPB == TPB - 1:
                            value_high(tile[0], tile[1] // TPB)
                        tile = lagging(it, N, T_LAG + 1, cur, prev)
                        if tile and tile[1] % 2:
                            copy_odd(*tile)
                        for it_h, h in heads(it, N, 2, cur, nxt):
                            evacuate(it_h, h)
                        if cur:
                            exponent(it, N)
                        tile = lagging(it, N, 1, cur, prev)
                        if tile:
                            prob_high(*tile)
                        for it_h, h in heads(it, N, 6, cur, nxt):
                            root(it_h, h)
                        for it_h, h in heads(it, N, 8, cur, nxt):
                            query_high(it_h, h)

                for h in range(GROUP - 1):
                    evacuate(0, h)
                    if h:
                        root(0, h - 1)
                        query_high(0, h - 1)
                root(0, GROUP - 2)
                query_high(0, GROUP - 2)
                iterations(act, turns)

            @block.vector
            def _(dve):
                dve.sem_inc(qn_ready, 1)
                dve.sem_inc(s_done, LEAD)
                dve.sem_inc(p_lo, SLOTS_P)
                dve.sem_inc(t_even, 1)
                dve.sem_inc(o_lo, 1)
                dve.sem_inc(x_added, 1)
                dve.wait_ge(c_loaded, 48)
                dve.memset(ones[:, :], 1.0).then_inc(const_ready, 1)
                dve.memset(eps[:, :], HD * RMS_EPS).then_inc(const_ready, 1)
                dve.tensor_scalar(nqw[:, :], qw[:, :], -1.0, None, ALU.mult).then_inc(const_ready, 1)
                dve.tensor_scalar(nmask[:, :, :], nmask[:, :, :], -1.0, None, ALU.mult).then_inc(const_ready, 1)
                dve.wait_ge(const_ready, 4)

                def normalise(it, h):
                    dve.wait_ge(rq_ready, GROUP * it + h + 1)
                    dve.scalar_tensor_tensor(qf[h][:, :], qf[h][:, :], nqw[:, 0:1], rq[:, :],
                                             ALU.mult, ALU.mult).then_inc(qn_ready, 1)

                def mask_max(it, N):
                    n = TILES * it + N
                    dve.wait_ge(s_ready, n + 1 + S0)
                    dve.wait_ge(exp_done, n + 1)
                    dve.sem_inc(dve_turn, 1)
                    dve.tensor_tensor_reduce(s[N % 2][:, :], bank_s[N % 2][:, :], nmask[:, N % TPB, :], 1.0, 3.0e38,
                                             ALU.add, ALU.min, low[:, N:N + 1]).then_inc(s_done, 1)

                def invert(it, N):
                    dve.wait_ge(exp_done, TILES * it + N + 1 + LEAD)
                    dve.reciprocal(inv[:, N:N + 1], total[:, N:N + 1]).then_inc(inv_ready, 1)

                def prob_low(it, N):
                    dve.wait_ge(p_hi, TILES * it + N + 1)
                    dve.scalar_tensor_tensor(p[N // TPB % 2][1][:, N % TPB, :], prob[N % SLOTS_P][:, :],
                                             inv[:, N:N + 1], p[N // TPB % 2][0][:, N % TPB, :],
                                             ALU.mult, ALU.subtract).then_inc(p_lo, 1)

                def copy_even(it, N):
                    dve.wait_ge(t_ready, TILES * it + N + 1 + T0)
                    dve.wait_ge(pv_step, TILES * it + N - 1 + PV0)
                    dve.tensor_copy(pT[0][:, :, :], bank_t[0][:, :, :]).then_inc(t_even, 1)

                def value_low(it, h):
                    dve.wait_ge(o_hi, GROUP * it + h + 1)
                    dve.tensor_tensor(oT[1][:, o_slot(it, h), :], bank_o[:, :], oT[0][:, o_slot(it, h), :],
                                      ALU.subtract).then_inc(o_lo, 1)

                def add_output(it, i):
                    dve.wait_ge(y_ready, 4 * it + i + 1 + Y0)
                    xt = X[:, it % B * TPB + i, :]
                    dve.tensor_tensor(xt, bank_y[:, :], xt, ALU.add).then_inc(x_added, 1)

                def turns(it, cur, prev, nxt):
                    for N in range(TILES):
                        if prev and N > TILES // 2 and N % 2 == 0:
                            add_output(it - 1, (N - TILES // 2) // 2 - 1)
                        tile = lagging(it, N, T_LAG + 1, cur, prev)
                        if tile and tile[1] % 2 == 0:
                            copy_even(*tile)
                        tile = lagging(it, N, V_LAG + 1, cur, prev)
                        if tile and tile[1] % TPB == TPB - 1:
                            value_low(tile[0], tile[1] // TPB)
                        if cur:
                            mask_max(it, N)
                        tile = lagging(it, N, 1, cur, prev)
                        if tile:
                            invert(*tile)
                        tile = lagging(it, N, 2, cur, prev)
                        if tile:
                            prob_low(*tile)
                        for it_h, h in heads(it, N, 7, cur, nxt):
                            normalise(it_h, h)
                        if prev and N == TILES - 1:
                            add_output(it - 1, TPB - 1)

                for h in range(GROUP - 1):
                    normalise(0, h)
                iterations(dve, turns)

            @block.gpsimd
            def _(pool):
                pool.sem_inc(q_lo, GROUP)
                pool.sem_inc(sq_lo, 1)
                pool.sem_inc(v_loaded, 16)
                SPLITS = 1 + GROUP
                LOADS = 2

                def split(hi, lo, source, n, done):
                    pool.sem_inc(pool_turn, 1)
                    pool.tensor_copy(hi, source).then_inc(w_high, 1)
                    pool.wait_ge(w_high, n + 1)
                    pool.tensor_tensor(lo, source, hi, ALU.subtract).then_inc(done, 1)

                def split_wq(g, slot):
                    if slot is None:
                        pool.wait_ge(w_loaded, 16)
                        split(wq[0][:, 0:KC, :], wq[1][:, 0:KC, :], w_f[:, :, :], 0, wq_split)
                    else:
                        pool.wait_ge(w_loaded, LOADS * 16 * g)
                        pool.wait_ge(q_proj, GROUP * B * (g - 1) + 1)
                        at = bass.ds(slot, KC)
                        split(wq[0][:, at, :], wq[1][:, at, :], w_f[:, :, :], SPLITS * (g - 1) + 1, wq_split)

                def split_wo(g, h, before):
                    if h == 0:
                        pool.wait_ge(w_loaded, LOADS * 16 * g + 48)
                        pool.wait_ge(y_ready, B * TPB * g + Y0)
                    split(wo[0][:, h, :], wo[1][:, h, :], w_f[:, h, :], before + h, wo_split)

                def squares(it, h):
                    n = GROUP * it + h
                    pool.wait_ge(qf_ready, n + 2)
                    pool.wait_ge(sq_lo, n + 1)
                    pool.wait_ge(ss_ready, n + 1)
                    pool.sem_inc(pool_turn, 1)
                    pool.tensor_tensor(sq_f[:, :], qf[h][:, :], qf[h][:, :], ALU.mult).then_inc(sqf_ready, 1)
                    pool.wait_ge(sqf_ready, n + 1)
                    pool.sem_inc(pool_turn, 1)
                    pool.tensor_copy(sq[0][:, :], sq_f[:, :]).then_inc(sq_hi, 1)
                    pool.wait_ge(sq_hi, n + 1)
                    pool.tensor_tensor(sq[1][:, :], sq_f[:, :], sq[0][:, :], ALU.subtract).then_inc(sq_lo, 1)

                def query_low(it, h):
                    pool.wait_ge(q_hi, GROUP * it + h + 1)
                    pool.tensor_tensor(q[1][:, h, :], qf[h][:, :], q[0][:, h, :], ALU.subtract).then_inc(q_lo, 1)

                def load(source, wait_for, count):
                    pool.wait_ge(wait_for, count)
                    pool.sem_inc(pool_turn, 1)
                    pool.dma_start(w_f[:, :, :], source).then_inc(w_loaded, 16)

                def queries(g, b, last_g=False):
                    it = g * B + b
                    more = not (last_g and b == B - 1)
                    before = SPLITS * g + 2 - last_g
                    squares(it, 3)
                    if b == 1:
                        split_wo(g, 0, before)
                    if more:
                        squares(it + 1, 0)
                        if b == 1:
                            split_wo(g, 1, before)
                        squares(it + 1, 1)
                    query_low(it, 3)
                    if b == 1:
                        split_wo(g, 2, before)
                        split_wo(g, 3, before)
                        if not last_g:
                            load(w_q[(g + 2) % NKV], wo_split, GROUP * g + GROUP)
                    if more:
                        squares(it + 1, 2)
                        for h in range(GROUP - 1):
                            query_low(it + 1, h)
                    if b == 0:
                        if last_g:
                            pool.wait_ge(w_loaded, LOADS * 16 * (g + 1))
                        else:
                            split_wq(g + 1, (g + 1) % 2 * KC)
                        load(w_o[g], wq_split, min(g + 2, NKV) if last_g else g + 2)

                pool.dma_start(w_f[:, :, :], w_q[0]).then_inc(w_loaded, 16)
                split_wq(0, None)
                load(w_q[1], wq_split, 1)
                for h in range(GROUP - 1):
                    squares(0, h)
                for h in range(GROUP - 1):
                    query_low(0, h)
                with pool.Fori(0, NKV - 1) as g:
                    for b in range(B):
                        queries(g, b)
                for b in range(B):
                    queries(NKV - 1, b, last_g=True)


class Rounding:

    def __init__(self, m, width):
        self.v = [m.sb(f"v{j}", [P, width], F32) for j in range(2)]
        self.m = [m.sb(f"m{j}", [P, width], F32) for j in range(2)]
        self.v_ready = m.sem("v_ready")
        self.e_ready = m.sem("e_ready")
        self.m_ready = m.sem("m_ready")
        self.t_ready = m.sem("t_ready")
        self.o_ready = m.sem("o_ready")

    def scale(self, act, n, j, src, func, factor):
        act.wait_ge(self.o_ready, n + 1)
        act.activation(self.v[j][:, :], src, func, scale=factor).then_inc(self.v_ready, 1)

    def magic(self, dve, n, j):
        bits = self.m[j][:, :].bitcast(I32)
        dve.wait_ge(self.o_ready, n + 1)
        dve.wait_ge(self.v_ready, n + 1)
        dve.tensor_scalar(bits, self.v[j][:, :].bitcast(I32), 0x7F800000, None, ALU.bitwise_and).then_inc(self.e_ready, 1)
        dve.wait_ge(self.e_ready, n + 1)
        dve.tensor_scalar(self.m[j][:, :], self.m[j][:, :], 2.0 ** -6, 1.5 * 2.0 ** 20,
                          ALU.max, ALU.mult).then_inc(self.m_ready, 1)

    def add(self, pool, n, j):
        pool.wait_ge(self.m_ready, n + 1)
        pool.tensor_tensor(self.v[j][:, :], self.v[j][:, :], self.m[j][:, :], ALU.add).then_inc(self.t_ready, 1)

    def subtract(self, dve, n, j, out):
        dve.wait_ge(self.t_ready, n + 1)
        dve.tensor_tensor(out, self.v[j][:, :], self.m[j][:, :], ALU.subtract).then_inc(self.o_ready, 1)


def stage_quantise(nc, X, xqT, w8_fc, w8_proj_dram, scales, ident_bf, w_fc, w_proj):
    WIDTH = 1024
    NP = KC * FF // WIDTH
    with ExitStack() as stack:
        m = Names(nc, stack, "quant")
        w_f = [m.sb(f"w_f{i}", [P, KC * FF], F32) for i in range(2)]
        w8_proj = m.sb("w8_proj", [P, FFC * C], BF16)
        xn = m.sb("xn", [P, NT * C], F32)
        xq = [m.sb(f"xq{j}", [P, WIDTH], BF16) for j in range(2)]
        stats = m.sb("stats", [P, NT, 6], F32)
        mv = m.sb("mv", [P, NT, 2], F32)
        rstd = m.sb("rstd", [P, NT], F32)
        top = m.sb("top", [P, 3], F32)
        top_all = m.sb("top_all", [P, 3], F32)
        inv = m.sb("inv", [P, 3], F32)
        pt = [m.ps(f"pt{j}", [P, 8, P], BF16) for j in range(2)]
        rnd = Rounding(m, WIDTH)
        w_loaded = [m.sem(f"w_loaded{i}") for i in range(2)]
        stat = m.sem("stat")
        root_ready = m.sem("root_ready")
        xn_ready = m.sem("xn_ready")
        top_ready = m.sem("top_ready")
        all_ready = m.sem("all_ready")
        step = m.sem("step")
        pt_ready = m.sem("pt_ready")
        xt_ready = m.sem("xt_ready")
        stored = m.sem("stored")

        with nc.Block() as block:
            @block.sync
            def _(sp):
                sp.dma_start(w_f[0][:, :], w_fc).then_inc(w_loaded[0], 16)
                sp.dma_start(w_f[1][:, :], w_proj).then_inc(w_loaded[1], 16)
                sp.wait_ge(rnd.o_ready, 2 * NP + LEAD)
                sp.dma_start(w8_proj_dram, w8_proj[:, :]).then_inc(stored, 16)
                sp.wait_ge(stored, 16)

            @block.vector
            def _(dve):
                dve.sem_inc(rnd.o_ready, LEAD)
                ln_stats(dve, stat, root_ready, X, stats, mv, rstd)
                with dve.Fori(0, NT) as t:
                    dve.tensor_scalar(xn[:, bass.ds(t * C, C)], X[:, t, :], mv[:, t, 0:1], rstd[:, bass.ds(t, 1)],
                                      ALU.subtract, ALU.mult).then_inc(xn_ready, 1)
                for i, src in enumerate((w_f[0], w_f[1], xn)):
                    if i < 2:
                        dve.wait_ge(w_loaded[i], 16)
                    else:
                        dve.wait_ge(xn_ready, NT)
                    dve.tensor_reduce(top[:, i:i + 1], src[:, :], AX.X, ALU.max,
                                      apply_absolute_value=True).then_inc(top_ready, 1)
                done = Steps(dve, step)
                dve.wait_ge(all_ready, 1)
                done.mark(dve.tensor_scalar(scales[:, 0:3], top_all[:, :], 1.0 / FP8_MAX, 1e-6, ALU.mult, ALU.max))
                done.wait()
                done.mark(dve.reciprocal(inv[:, :], scales[:, 0:3]))
                for i, out in enumerate((w8_fc, w8_proj)):
                    flat = out[:, :, :].rearrange("p k f -> p (k f)") if i == 0 else out[:, :]
                    with dve.Fori(0, NP // 2) as c2:
                        for j in range(2):
                            rnd.magic(dve, i * NP + 2 * c2 + j, j)
                        for j in range(2):
                            rnd.subtract(dve, i * NP + 2 * c2 + j, j, flat[:, bass.ds((2 * c2 + j) * WIDTH, WIDTH)])
                with dve.Fori(0, NP // 2) as c2:
                    for j in range(2):
                        rnd.magic(dve, 2 * NP + 2 * c2 + j, j)
                    for j in range(2):
                        dve.wait_ge(pt_ready, 2 * c2 + j + 1)
                        rnd.subtract(dve, 2 * NP + 2 * c2 + j, j, xq[j][:, :])
                    for j in range(2):
                        c = 2 * c2 + j
                        dve.wait_ge(pt_ready, c + 1 + LEAD)
                        for i in range(2):
                            ins = dve.tensor_copy(xqT[:, :, bass.ds((2 * c + i) * P, P)],
                                                  pt[j][:, i * KC:(i + 1) * KC, :])
                        ins.then_inc(xt_ready, 1)

            @block.gpsimd
            def _(pool):
                pool.wait_ge(top_ready, 3)
                pool.partition_all_reduce(top_all[:, :], top[:, :], P, bass.bass_isa.ReduceOp.max).then_inc(all_ready, 1)
                with pool.Fori(0, 3 * NP // 2) as c2:
                    for j in range(2):
                        rnd.add(pool, 2 * c2 + j, j)

            @block.scalar
            def _(act):
                ln_root(act, stat, root_ready, rstd)
                act.wait_ge(step, 2)
                for i, src in enumerate((w_f[0], w_f[1], xn)):
                    with act.Fori(0, NP // 2) as c2:
                        for j in range(2):
                            c = 2 * c2 + j
                            rnd.scale(act, i * NP + c, j, src[:, bass.ds(c * WIDTH, WIDTH)], ACT.Copy, inv[:, i:i + 1])

            @block.tensor
            def _(pe):
                pe.sem_inc(pt_ready, LEAD)
                pe.sem_inc(xt_ready, LEAD)
                with pe.Fori(0, NP // 2) as c2:
                    for j in range(2):
                        c = 2 * c2 + j
                        pe.wait_ge(rnd.o_ready, 2 * NP + c + 1 + LEAD)
                        pe.wait_ge(xt_ready, c + 1)
                        for k in range(8):
                            ins = pe.transpose(pt[j][:, k, :], xq[j][:, k * P:(k + 1) * P], ident_bf[:, :])
                        ins.then_inc(pt_ready, 1)


def stage_up(nc, xqT, w8_fc, R, r_top, scales):
    NG = TOK // 512
    with ExitStack() as stack:
        m = Names(nc, stack, "up")
        s1 = m.sb("s1", [P, 1], F32)
        part = m.sb("part", [P, FFC * NG], F32)
        top = m.sb("top", [P, 1], F32)
        bank = [[m.ps(f"bank{j}_{g}", [P, 512], F32) for g in range(NG)] for j in range(2)]
        s1_ready = m.sem("s1_ready")
        z_ready = m.sem("z_ready")
        r_ready = m.sem("r_ready")
        part_ready = m.sem("part_ready")
        top_ready = m.sem("top_ready")
        all_ready = m.sem("all_ready")

        with nc.Block() as block:
            @block.tensor
            def _(pe):
                with pe.Fori(0, FFC // 2) as f2:
                    for j in range(2):
                        f = 2 * f2 + j
                        for k in range(KC):
                            for g in range(NG):
                                if k == 0:
                                    pe.wait_ge(r_ready, NG * f + g + 1)
                                ins = pe.matmul(bank[j][g][:, :], w8_fc[:, k, bass.ds(f * P, P)],
                                                xqT[:, k, g * 512:(g + 1) * 512], start=(k == 0), stop=(k == KC - 1))
                                if k == KC - 1:
                                    ins.then_inc(z_ready, 1)

            @block.scalar
            def _(act):
                act.sem_inc(r_ready, 2 * NG)
                act.wait_ge(s1_ready, 1)
                with act.Fori(0, FFC // 2) as f2:
                    for j in range(2):
                        f = 2 * f2 + j
                        for g in range(NG):
                            act.wait_ge(z_ready, NG * f + g + 1)
                            act.activation(R[:, f, g * 512:(g + 1) * 512], bank[j][g][:, :], ACT.Relu,
                                           scale=s1[:, 0:1]).then_inc(r_ready, 1)

            @block.vector
            def _(dve):
                dve.tensor_tensor(s1[:, :], scales[:, 2:3], scales[:, 0:1], ALU.mult).then_inc(s1_ready, 1)
                with dve.Fori(0, FFC) as f:
                    for g in range(NG):
                        dve.wait_ge(r_ready, NG * f + g + 1 + 2 * NG)
                        dve.tensor_reduce(part[:, bass.ds(NG * f + g, 1)], R[:, f, g * 512:(g + 1) * 512],
                                          AX.X, ALU.max).then_inc(part_ready, 1)
                dve.wait_ge(part_ready, NG * FFC)
                dve.tensor_reduce(top[:, :], part[:, :], AX.X, ALU.max).then_inc(top_ready, 1)

            @block.gpsimd
            def _(pool):
                pool.wait_ge(top_ready, 1)
                pool.partition_all_reduce(r_top[:, :], top[:, :], P, bass.bass_isa.ReduceOp.max).then_inc(all_ready, 1)
                pool.wait_ge(all_ready, 1)


def stage_down(nc, X, R, r_top, w8_proj_dram, scales, out):
    WIDTH = 1024
    NB = WIDTH // P
    HALVES = TOK // WIDTH
    with ExitStack() as stack:
        m = Names(nc, stack, "down")
        w8 = m.sb("w8", [P, FFC, C], BF16)
        h8 = [m.sb(f"h8{j}", [P, WIDTH], BF16) for j in range(2)]
        h_top = m.sb("h_top", [P, 1], F32)
        h_scale = m.sb("h_scale", [P, 1], F32)
        inv = m.sb("inv", [P, 1], F32)
        root = m.sb("root", [P, 1], F32)
        s2 = m.sb("s2", [P, 1], F32)
        rnd = Rounding(m, WIDTH)
        bank = [m.ps(f"bank{i}", [P, C], F32) for i in range(NB)]
        w_loaded = m.sem("w_loaded")
        step = m.sem("step")
        root_ready = m.sem("root_ready")
        h_used = m.sem("h_used")
        x_ready = m.sem("x_ready")
        stored = m.sem("stored")

        with nc.Block() as block:
            @block.sync
            def _(sp):
                sp.dma_start(w8[:, :, :], w8_proj_dram.rearrange("p (f c) -> p f c", c=C)).then_inc(w_loaded, 16)
                for t in range(NT):
                    b, i = t // TPB, t % TPB
                    sp.wait_ge(x_ready, t + 1 + NB)
                    sp.dma_start(out[b, i * P:(i + 1) * P, :], X[:, t, :]).then_inc(stored, 16)
                sp.wait_ge(stored, 16 * NT)

            @block.vector
            def _(dve):
                dve.sem_inc(rnd.o_ready, LEAD)
                dve.sem_inc(x_ready, NB)
                done = Steps(dve, step)
                done.mark(dve.tensor_tensor(h_top[:, :], r_top[:, :], r_top[:, :], ALU.mult))
                done.wait()
                done.mark(dve.tensor_scalar(h_scale[:, :], h_top[:, :], 1.0 / FP8_MAX, 1e-6, ALU.mult, ALU.max))
                done.wait()
                done.mark(dve.reciprocal(inv[:, :], h_scale[:, :]))
                done.mark(dve.tensor_tensor(s2[:, :], h_scale[:, :], scales[:, 1:2], ALU.mult))
                done.wait()
                with dve.Fori(0, HALVES) as half:
                    with dve.Fori(0, FFC // 2) as f2:
                        for j in range(2):
                            rnd.magic(dve, half * FFC + 2 * f2 + j, j)
                        for j in range(2):
                            n = half * FFC + 2 * f2 + j
                            dve.wait_ge(h_used, n + 1)
                            rnd.subtract(dve, n, j, h8[j][:, :])
                    for i in range(NB):
                        if i == 0:
                            dve.wait_ge(h_used, FFC * (half + 1) + LEAD)
                        xt = X[:, half * NB + i, :]
                        dve.scalar_tensor_tensor(xt, bank[i][:, :], s2[:, 0:1], xt, ALU.mult, ALU.add).then_inc(x_ready, 1)

            @block.scalar
            def _(act):
                act.wait_ge(step, 4)
                act.activation(root[:, :], inv[:, :], ACT.Sqrt).then_inc(root_ready, 1)
                act.wait_ge(root_ready, 1)
                with act.Fori(0, HALVES) as half:
                    with act.Fori(0, FFC // 2) as f2:
                        for j in range(2):
                            rnd.scale(act, half * FFC + 2 * f2 + j, j, R[:, 2 * f2 + j, bass.ds(half * WIDTH, WIDTH)],
                                      ACT.Square, root[:, 0:1])

            @block.gpsimd
            def _(pool):
                with pool.Fori(0, HALVES * FFC // 2) as n2:
                    for j in range(2):
                        rnd.add(pool, 2 * n2 + j, j)

            @block.tensor
            def _(pe):
                pe.sem_inc(h_used, LEAD)
                pe.wait_ge(w_loaded, 16)
                with pe.Fori(0, HALVES) as half:
                    for f in range(FFC):
                        n = half * FFC + f
                        pe.wait_ge(rnd.o_ready, n + 1 + LEAD)
                        for i in range(NB):
                            if f == 0:
                                pe.wait_ge(x_ready, half * NB + i + 1)
                            ins = pe.matmul(bank[i][:, :], h8[f % 2][:, i * P:(i + 1) * P], w8[:, f, :],
                                            start=(f == 0), stop=(f == FFC - 1))
                        ins.then_inc(h_used, 1)


def build(nc, x, ctx_t, wu_cols, w_row, centroids, gate_bias, w_gate_up, w_down, w_table,
          w_kv, bias_kv, kn_w, w_q, w_o, bq_cols, qn_w, mask, w_fc, w_proj, out):
    with ExitStack() as keep:
        def tensor(stack, name, shape, dt, **where):
            return stack.enter_context(nc.sbuf_tensor(name, shape, dt, **where))

        X = tensor(keep, "X", [P, NT, C], F32)
        ident = tensor(keep, "ident", [P, P], F32)
        ident_bf = tensor(keep, "ident_bf", [P, P], BF16)
        v_parts = nc.dram_tensor("v_parts", (NKV, 2, P, NT, HD), BF16, kind="Internal").ap()
        slot_rows = nc.dram_tensor("slot_rows", (TILES_R * SLOTS, 2 * C), BF16, kind="Internal").ap()
        slot_out = nc.dram_tensor("slot_out", (TILES_R * SLOTS, C), F32, kind="Internal").ap()
        with ExitStack() as attention:
            KT = [tensor(attention, f"KT_{h}", [P, NKV, TOK], BF16) for h in ("hi", "lo")]
            with ExitStack() as first:
                ctxT = [tensor(first, f"ctxT_{h}", [P, KC, TOK], BF16) for h in ("hi", "lo")]
                with ExitStack() as wkv:
                    time_row = tensor(wkv, "time_row", [1, S], F32)
                    stage_setup(nc, ident, ident_bf, time_row)
                    stage_wkv(nc, X, ctxT, ident, time_row, x, ctx_t, wu_cols, w_row)
                stage_kv(nc, ctxT, KT, v_parts, ident, w_kv, bias_kv, kn_w, slot_rows)
            with ExitStack() as moe:
                slot = [tensor(moe, f"slot{k}", [P, NT], U32) for k in range(2)]
                share = [tensor(moe, f"share{k}", [P, NT], F32) for k in range(2)]
                w_rows = tensor(moe, "w_rows", [P, TILES_R], U32)
                with ExitStack() as shared:
                    rows = tensor(shared, "rows", [P, NT, 2 * C], BF16)
                    xnT = [tensor(shared, f"xnT1_{h}", [P, KC, TOK], BF16) for h in ("hi", "lo")]
                    stage_route(nc, X, xnT, rows, share, slot, w_rows, ident, centroids, gate_bias)
                    stage_shared(nc, X, xnT, rows, slot, slot_rows, w_gate_up, w_down)
                stage_routed(nc, slot_rows, slot_out, w_rows, w_table)
                stage_combine(nc, X, share, slot, slot_out)
            xnT = [tensor(attention, f"xnT2_{h}", [P, KC, TOK], BF16) for h in ("hi", "lo")]
            stage_norm(nc, X, xnT, ident)
            stage_attention(nc, X, xnT, KT, v_parts, ident_bf, mask, w_q, w_o, bq_cols, qn_w)
        w8_proj = nc.dram_tensor("w8_proj", (P, FFC * C), BF16, kind="Internal").ap()
        scales = tensor(keep, "scales", [P, 3], F32)
        r_top = tensor(keep, "r_top", [P, 1], F32)
        with ExitStack() as hidden:
            with ExitStack() as up:
                right = bass.opposite_side(nc.default_side)
                xqT = tensor(up, "xqT", [P, KC, TOK], BF16, side=right)
                w8_fc = tensor(up, "w8_fc", [P, KC, FF], BF16, side=right)
                stage_quantise(nc, X, xqT, w8_fc, w8_proj, scales, ident_bf, w_fc, w_proj)
                R = tensor(hidden, "R", [P, FFC, TOK], F32)
                stage_up(nc, xqT, w8_fc, R, r_top, scales)
            stage_down(nc, X, R, r_top, w8_proj, scales, out)


def kernel(**inputs):
    import numpy as np
    import concourse.bacc as bacc
    from concourse.bass_utils import run_bass_kernel_spmd

    def host(name):
        return np.asarray(inputs[name])

    w, u = host("L0_xattn_w"), host("L0_xattn_u")
    def by_partition(gate, up, down):
        gu = np.concatenate([gate, up], axis=2).reshape(-1, KC, P, 2 * F_EXP).transpose(0, 2, 1, 3)
        return gu, down.reshape(-1, FC, P, C).transpose(0, 2, 1, 3)

    gu, dn = by_partition(host("L0_ffn_wg"), host("L0_ffn_wu"), host("L0_ffn_wd"))
    gu_s, dn_s = by_partition(*(host(n).reshape(C, 2, F_EXP).transpose(1, 0, 2) for n in ("L0_ffn_wg_s", "L0_ffn_wu_s")),
                              host("L0_ffn_wd_s").reshape(2, F_EXP, C))
    arrays = {
        "w_fc": host("L1_ffn_w_fc").T.reshape(KC, P, FF).transpose(1, 0, 2).reshape(P, KC * FF),
        "w_proj": host("L1_ffn_w_proj").T.reshape(FFC, P, C).transpose(1, 0, 2).reshape(P, FFC * C),
        "w_kv": np.stack([host(n).reshape(KC, P, NKV * HD).transpose(1, 0, 2) for n in ("L1_xattn_Wk", "L1_xattn_Wv")]),
        "bias_kv": np.tile(np.stack([host("L1_xattn_bk"), host("L1_xattn_bv")]), (P, 1, 1)),
        "kn_w": np.tile(host("L1_xattn_kn_w"), (P, 1)),
        "qn_w": host("L1_xattn_qn_w").reshape(P, 1),
        "bq_cols": host("L1_xattn_bq").reshape(NH, HD).T,
        "w_q": host("L1_xattn_Wq").reshape(KC, P, NKV, GROUP * HD).transpose(2, 1, 0, 3),
        "w_o": host("L1_xattn_Wo").reshape(NKV, GROUP, HD, C).transpose(0, 2, 1, 3),
        "mask": host("mask_1xSxS2_ff0")[0].reshape(TPB, P, S).transpose(1, 0, 2),
        "centroids": host("L0_ffn_centroids").T.reshape(KC, P, E_ROUTED).transpose(1, 0, 2),
        "gate_bias": np.tile(host("L0_ffn_gate_bias"), (P, 1)),
        "w_gate_up": gu_s,
        "w_down": dn_s,
        "w_table": np.concatenate([gu.reshape(E_ROUTED * P, -1), dn.reshape(E_ROUTED * P, -1)], axis=1),
        "x": host("x"),
        "ctx_t": host("ctx_2048").transpose(0, 2, 1),
        "wu_cols": np.stack([w.reshape(KC, P).T, u.reshape(KC, P).T], axis=1),
        "w_row": w.reshape(1, C),
    }
    arrays = {name: np.ascontiguousarray(a) for name, a in arrays.items()}
    nc = bacc.Bacc("TRN2", target_bir_lowering=False, num_devices=1)
    aps = {name: nc.dram_tensor(name, a.shape, mybir.dt.from_np(a.dtype), kind="ExternalInput").ap()
           for name, a in arrays.items()}
    out = nc.dram_tensor("out", (B, S, C), F32, kind="ExternalOutput").ap()
    build(nc, out=out, **aps)
    r = run_bass_kernel_spmd(nc, [arrays], core_ids=[0])
    return r.results[0]["out"]
```

```python
from contextlib import ExitStack

import concourse.bass as bass
from concourse import mybir

F32 = mybir.dt.float32
BF16 = mybir.dt.bfloat16
I32 = mybir.dt.int32
U32 = mybir.dt.uint32
ALU = mybir.AluOpType
ACT = mybir.ActivationFunctionType
AX = mybir.AxisListType

P = 128
B, S, C = 4, 512, 512
TOK = B * S
NT = TOK // P
TPB = S // P
KC = C // P
LN_EPS = 1e-5
E_ROUTED = 16
F_EXP = 256
FC = F_EXP // P
SHARED_RATIO = 0.1
NH, NKV, HD = 16, 4, 128
GROUP = NH // NKV
RMS_EPS = 1e-6
FF = 2048
FFC = FF // P
FP8_MAX = 448.0


LEAD = 2


class Steps:

    def __init__(self, eng, sem, base=0):
        self.eng, self.sem, self.base, self.n = eng, sem, base, 0

    def mark(self, ins):
        ins.then_inc(self.sem, 1)
        self.n += 1

    def wait(self):
        self.eng.wait_ge(self.sem, self.base + self.n)


class Names:

    def __init__(self, nc, stack, stage):
        self.nc, self.stack, self.stage, self.sems = nc, stack, stage, []
        stack.callback(self.clear)

    def clear(self):
        self.nc.clear_and_free_semaphores(self.sems)
        self.nc.all_engine_barrier()

    def sb(self, name, shape, dt):
        return self.stack.enter_context(self.nc.sbuf_tensor(f"{self.stage}_{name}", shape, dt))

    def ps(self, name, shape, dt):
        return self.stack.enter_context(self.nc.psum_tensor(f"{self.stage}_{name}", shape, dt))

    def sem(self, name):
        self.sems.append(self.nc.alloc_semaphore(f"{self.stage}_{name}"))
        return self.sems[-1]


def one_behind(eng, count, first, second):
    first(0, 0)
    with eng.Fori(0, count // 2 - 1) as i:
        first(2 * i + 1, 1)
        second(2 * i, 0)
        first(2 * i + 2, 0)
        second(2 * i + 1, 1)
    first(count - 1, 1)
    second(count - 2, 0)
    second(count - 1, 1)


def stage_setup(nc, ident, ident_bf, time_row):
    made = nc.alloc_semaphore("setup_made")
    with nc.Block() as block:
        @block.gpsimd
        def _(pool):
            pool.memset(ident[:, :], 0.0).then_inc(made, 1)
            pool.memset(ident_bf[:, :], 0.0).then_inc(made, 1)
            pool.wait_ge(made, 2)
            for m in (ident, ident_bf):
                pool.affine_select(out=m[:, :], in_=m[:, :], compare_op=ALU.not_equal, fill=1.0, base=0,
                                   pattern=[[-1, P]], channel_multiplier=1).then_inc(made, 1)
            pool.iota(time_row[:, :], [[1, S]], base=0, channel_multiplier=0,
                      allow_small_or_imprecise_dtypes=True).then_inc(made, 1)
            pool.wait_ge(made, 5)


def ln_stats(dve, sem, root_ready, X, stats, mv, rstd, start=0, loaded=None):
    for b in range(B if start == 0 else 0):
        if loaded:
            dve.wait_ge(loaded[b], 16)
        with dve.Fori(b * TPB, (b + 1) * TPB) as t:
            dve.bn_stats(stats[:, t, :], X[:, t, :]).then_inc(sem, 1)
    if start == 0:
        dve.wait_ge(sem, NT)
    for t in range(NT):
        dve.bn_aggr(mv[:, t, :], stats[:, t, :]).then_inc(sem, 1)
    dve.wait_ge(sem, start + 2 * NT)
    dve.tensor_scalar(rstd[:, :], mv[:, :, 1], LN_EPS, None, ALU.add).then_inc(sem, 1)
    dve.wait_ge(root_ready, 1)
    dve.reciprocal(rstd[:, :], rstd[:, :]).then_inc(sem, 1)
    dve.wait_ge(sem, start + 2 * NT + 2)


def ln_root(act, sem, root_ready, rstd, start=0):
    act.wait_ge(sem, start + 2 * NT + 1)
    act.activation(rstd[:, :], rstd[:, :], ACT.Sqrt).then_inc(root_ready, 1)


def stage_wkv(nc, X, ctxT, ident, time_row, x, ctx_t, wu_cols, w_row, w_kv_parts, w_kv):
    ctxT_hi, ctxT_lo = ctxT
    with ExitStack() as stack:
        m = Names(nc, stack, "wkv")
        cols = m.sb("cols", [P, 2, KC], F32)
        cw, cu = cols[:, 0, :], cols[:, 1, :]
        wrow = m.sb("wrow", [1, C], F32)
        nwrow = m.sb("nwrow", [1, C], F32)
        wpos = m.sb("wpos", [P, KC], F32)
        upos = m.sb("upos", [P, KC], F32)
        wneg = m.sb("wneg", [P, KC], F32)
        bias_state = m.sb("bias_state", [P, KC], F32)
        bias_now = m.sb("bias_now", [P, KC], F32)
        decay = m.sb("decay", [P, KC], F32)
        stats = m.sb("stats", [P, NT, 6], F32)
        mv = m.sb("mv", [P, NT, 2], F32)
        rstd = m.sb("rstd", [P, NT], F32)
        shift = m.sb("shift", [P, NT], F32)
        w_f = m.sb("w_f", [P, 2, KC, NKV * HD], F32)
        xn = [m.sb(f"xn{j}", [P, TPB, P], F32) for j in range(2)]
        v = [m.sb(f"v{c}", [P, S], F32) for c in range(KC)]
        g_state = [m.sb(f"g_state{j}", [P, S], F32) for j in range(2)]
        g_now = [m.sb(f"g_now{j}", [P, S], F32) for j in range(2)]
        f_state = [m.sb(f"f_state{j}", [P, S], F32) for j in range(2)]
        f_now = [m.sb(f"f_now{j}", [P, S], F32) for j in range(2)]
        s_scan = [m.sb(f"s_scan{j}", [P, S + 1], F32) for j in range(2)]
        q_scan = [m.sb(f"q_scan{j}", [P, S + 1], F32) for j in range(2)]
        num = [m.sb(f"num{j}", [P, S], F32) for j in range(2)]
        den = [m.sb(f"den{j}", [P, S], F32) for j in range(2)]
        y = [m.sb(f"y{j}", [P, S], F32) for j in range(2)]
        pk = [m.ps(f"pk{j}", [P, S], F32) for j in range(2)]
        py = [m.ps(f"py{j}", [P, TPB, P], F32) for j in range(2)]

        x_loaded = [m.sem(f"x_loaded{b}") for b in range(B)]
        par_loaded = m.sem("par_loaded")
        w_loaded = m.sem("w_loaded")
        w_hi = m.sem("w_hi")
        v_loaded = [m.sem(f"v_loaded{c}") for c in range(KC)]
        par = m.sem("par")
        decay_ready = m.sem("decay_ready")
        stat = m.sem("stat")
        root_ready = m.sem("root_ready")
        shift_ready = m.sem("shift_ready")
        norm_turn = m.sem("norm_turn")
        xn_ready = m.sem("xn_ready")
        k_ready = m.sem("k_ready")
        g_ready = m.sem("g_ready")
        hi_ready = m.sem("hi_ready")
        fst_ready = m.sem("fst_ready")
        fnow_ready = m.sem("fnow_ready")
        scan_done = m.sem("scan_done")
        nd_done = m.sem("nd_done")
        rec_done = m.sem("rec_done")
        v_split = m.sem("v_split")
        v_copied = m.sem("v_copied")
        y_ready = m.sem("y_ready")
        yt_ready = m.sem("yt_ready")
        x_added = m.sem("x_added")

        def turns(eng, *steps):
            def batch(b):
                for c in range(KC):
                    for step, lag in steps:
                        earlier = c < lag
                        if isinstance(b, int) and (b == 0 and earlier or b == B and not earlier):
                            continue
                        step(b + (c - lag) // KC, (c - lag) % KC)
            batch(0)
            with eng.Fori(1, B) as b:
                batch(b)
            batch(B)

        with nc.Block() as block:
            @block.sync
            def _(sp):
                sp.dma_start(cols[:, :, :], wu_cols).then_inc(par_loaded, 16)
                sp.dma_start(wrow[:, :], w_row).then_inc(par_loaded, 16)
                for b in range(B):
                    sp.dma_start(X[:, b * TPB:(b + 1) * TPB, :],
                                 x[b].rearrange("(t p) c -> p t c", p=P)).then_inc(x_loaded[b], 16)
                for i in range(2):
                    sp.dma_start(w_f[:, i, :, :], w_kv[i]).then_inc(w_loaded, 16)
                with sp.Fori(0, B) as b:
                    for c in range(KC):
                        sp.wait_ge(v_split, b * KC + c + 1)
                        sp.wait_ge(v_copied, b * KC + c + 1)
                        sp.dma_start(v[c][:, :], ctx_t[b, c * P:(c + 1) * P, :]).then_inc(v_loaded[c], 16)

            @block.vector
            def _(dve):
                dve.sem_inc(y_ready, LEAD)
                dve.sem_inc(x_added, LEAD)
                dve.wait_ge(par_loaded, 32)
                dve.tensor_scalar(wpos[:, :], cw, 0.0, None, ALU.max).then_inc(par, 1)
                dve.tensor_scalar(upos[:, :], cu, 0.0, None, ALU.max).then_inc(par, 1)
                dve.tensor_scalar(wneg[:, :], cw, 0.0, None, ALU.min).then_inc(par, 1)
                dve.tensor_scalar(nwrow[:, :], wrow[:, :], 0.0, -1.0, ALU.max, ALU.mult).then_inc(par, 1)
                dve.wait_ge(par, 4)
                dve.tensor_tensor(bias_now[:, :], cu, upos[:, :], ALU.subtract).then_inc(par, 1)
                dve.tensor_tensor(bias_state[:, :], wpos[:, :], upos[:, :], ALU.add).then_inc(par, 1)
                dve.wait_ge(par, 6)
                dve.tensor_scalar(bias_state[:, :], bias_state[:, :], -1.0, None, ALU.mult).then_inc(par, 1)
                for j in range(2):
                    dve.memset(s_scan[j][:, 0:1], 0.0).then_inc(par, 1)
                    dve.memset(q_scan[j][:, 0:1], 0.0).then_inc(par, 1)
                ln_stats(dve, stat, root_ready, X, stats, mv, rstd, loaded=x_loaded)
                dve.scalar_tensor_tensor(shift[:, :], mv[:, :, 0], -1.0, rstd[:, :], ALU.mult, ALU.mult
                                         ).then_inc(shift_ready, 1)

                def scans(b, c):
                    j, n = c % 2, b * KC + c
                    dve.wait_ge(g_ready, n + 1 + LEAD)
                    dve.wait_ge(fst_ready, n + 1)
                    for scan, g in ((q_scan, g_state), (s_scan, f_state)):
                        dve.tensor_tensor_scan(scan[j][:, 1:S + 1], decay[:, c:c + 1].to_broadcast([P, S]),
                                               g[j][:, :], 0.0, ALU.mult, ALU.add).then_inc(scan_done, 1)

                def divide(b, c):
                    j, n = c % 2, b * KC + c
                    dve.wait_ge(nd_done, 2 * n + 2 + 2 * LEAD)
                    dve.wait_ge(yt_ready, n + 1)
                    dve.tensor_copy(y[j][:, 0:1], v[c][:, 0:1]).then_inc(v_copied, 1)
                    dve.reciprocal(den[j][:, :], den[j][:, :]).then_inc(rec_done, 1)
                    dve.wait_ge(rec_done, n + 1)
                    dve.tensor_tensor(y[j][:, 1:S], num[j][:, 1:S], den[j][:, 1:S], ALU.mult).then_inc(y_ready, 1)

                def add(b, c):
                    dve.wait_ge(yt_ready, b * KC + c + 1 + LEAD)
                    xs = X[:, bass.ds(b * TPB, TPB), c * P:(c + 1) * P]
                    dve.tensor_tensor(xs, py[c % 2][:, :, :], xs, ALU.add).then_inc(x_added, 1)

                dve.wait_ge(decay_ready, 1)
                turns(dve, (scans, 2), (divide, 3), (add, 4))

            @block.scalar
            def _(act):
                act.sem_inc(v_split, KC)
                act.sem_inc(v_copied, KC)
                act.sem_inc(g_ready, LEAD)
                act.wait_ge(w_loaded, 32)
                act.activation(w_kv_parts[0][:, :, :, :], w_f[:, :, :, :], ACT.Copy).then_inc(w_hi, 1)
                ln_root(act, stat, root_ready, rstd)
                act.wait_ge(par, 11)
                act.activation(decay[:, :], wneg[:, :], ACT.Exp).then_inc(decay_ready, 1)

                def normalise(b, c):
                    act.wait_ge(k_ready, b * KC + c + 1)
                    act.sem_inc(norm_turn, 1)
                    for i in range(TPB):
                        t = b * TPB + i
                        ins = act.activation(xn[c % 2][:, i, :], X[:, t, c * P:(c + 1) * P], ACT.Identity,
                                             scale=rstd[:, bass.ds(t, 1)], bias=shift[:, bass.ds(t, 1)])
                    ins.then_inc(xn_ready, 1)

                def exponentials(b, c):
                    j, n = c % 2, b * KC + c
                    act.wait_ge(k_ready, n + 1 + LEAD)
                    act.wait_ge(nd_done, 2 * n + 2)
                    act.activation(g_state[j][:, :], pk[j][:, :], ACT.Exp, bias=bias_state[:, c:c + 1])
                    act.activation(g_now[j][:, :], pk[j][:, :], ACT.Exp, bias=bias_now[:, c:c + 1]).then_inc(g_ready, 1)
                    act.wait_ge(v_loaded[c], b * 16 + 16)
                    act.activation(ctxT_hi[:, c, bass.ds(b * S, S)], v[c][:, :], ACT.Copy).then_inc(hi_ready, 1)

                act.wait_ge(shift_ready, 1)
                turns(act, (normalise, 0), (exponentials, 1))

            @block.gpsimd
            def _(pool):
                pool.sem_inc(nd_done, 2 * LEAD)
                pool.wait_ge(w_hi, 1)
                pool.tensor_tensor(w_kv_parts[1][:, :, :, :], w_f[:, :, :, :], w_kv_parts[0][:, :, :, :], ALU.subtract)

                def times_v(b, c):
                    j, n = c % 2, b * KC + c
                    pool.wait_ge(v_loaded[c], b * 16 + 16)
                    pool.wait_ge(g_ready, n + 1 + LEAD)
                    for f, g, ready in ((f_state, g_state, fst_ready), (f_now, g_now, fnow_ready)):
                        pool.tensor_tensor(f[j][:, :], g[j][:, :], v[c][:, :], ALU.mult).then_inc(ready, 1)
                    pool.wait_ge(hi_ready, n + 1)
                    pool.tensor_tensor(ctxT_lo[:, c, bass.ds(b * S, S)], v[c][:, :],
                                       ctxT_hi[:, c, bass.ds(b * S, S)], ALU.subtract).then_inc(v_split, 1)

                def sums(b, c):
                    j, n = c % 2, b * KC + c
                    pool.wait_ge(scan_done, 2 * n + 2)
                    pool.wait_ge(fnow_ready, n + 1)
                    pool.wait_ge(y_ready, n + 1)
                    for out, scan, now in ((den, q_scan, g_now), (num, s_scan, f_now)):
                        pool.tensor_tensor(out[j][:, :], scan[j][:, 0:S], now[j][:, :], ALU.add).then_inc(nd_done, 1)

                turns(pool, (sums, 2), (times_v, 1))

            @block.tensor
            def _(pe):
                pe.sem_inc(k_ready, LEAD)
                pe.sem_inc(yt_ready, LEAD)
                pe.wait_ge(par, 11)

                def keys(b, c):
                    j, n = c % 2, b * KC + c
                    pe.wait_ge(xn_ready, n + 1)
                    pe.wait_ge(g_ready, n + 1)
                    pe.matmul(pk[j][:, :], nwrow[0:1, c * P:(c + 1) * P], time_row[0:1, :], start=True, stop=False)
                    for i in range(TPB):
                        ins = pe.matmul(pk[j][:, i * P:(i + 1) * P], xn[j][:, i, :], ident[:, :],
                                        start=False, stop=(i == TPB - 1))
                    ins.then_inc(k_ready, 1)

                def transpose_back(b, c):
                    j, n = c % 2, b * KC + c
                    pe.wait_ge(y_ready, n + 1 + LEAD)
                    pe.wait_ge(x_added, n + 1)
                    for i in range(TPB):
                        ins = pe.transpose(py[j][:, i, :], y[j][:, i * P:(i + 1) * P], ident[:, :])
                    ins.then_inc(yt_ready, 1)

                turns(pe, (keys, 0), (transpose_back, 3))


def ln_transpose(m, X, xnT, ident, router=None, stats=None):
    xnT_hi, xnT_lo = xnT
    start = -NT if stats else 0
    stats = stats or m.sb("stats", [P, NT, 6], F32)
    mv = m.sb("mv", [P, NT, 2], F32)
    rstd = m.sb("rstd", [P, NT], F32)
    xn = [m.sb(f"xn{j}", [P, C], F32) for j in range(2)]
    xf = [m.sb(f"xf{j}", [P, KC, P], F32) for j in range(2)]
    pt = [m.ps(f"pt{j}", [P, KC, P], F32) for j in range(2)]
    pl = [m.ps(f"pl{j}", [P, E_ROUTED], F32) for j in range(2)] if router else None
    stat = m.sem("stat")
    root_ready = m.sem("root_ready")
    xn_ready = m.sem("xn_ready")
    pt_ready = m.sem("pt_ready")
    xf_ready = m.sem("xf_ready")
    lo_ready = m.sem("lo_ready")
    logit_ready = m.sem("logit_ready")
    aff_ready = m.sem("aff_ready")
    row_hi = m.sem("row_hi")
    row_lo = m.sem("row_lo")

    def vector(dve):
        ln_stats(dve, stat, root_ready, X, stats, mv, rstd, start)
        with dve.Fori(0, NT // 2) as i:
            for j in range(2):
                t = 2 * i + j
                dve.wait_ge(pt_ready, t + 1)
                if router:
                    dve.wait_ge(row_lo, t + 1)
                dve.tensor_scalar(xn[j][:, :], X[:, t, :], mv[:, t, 0:1], rstd[:, bass.ds(t, 1)],
                                  ALU.subtract, ALU.mult).then_inc(xn_ready, 1)

    def nothing(t, j):
        pass

    def tensor(pe):
        pe.sem_inc(pt_ready, LEAD)
        if router:
            pe.sem_inc(logit_ready, LEAD)

        def transpose(t, j):
            pe.wait_ge(xn_ready, t + 1)
            pe.wait_ge(xf_ready, t + 1)
            for k in range(KC):
                ins = pe.transpose(pt[j][:, k, :], xn[j][:, k * P:(k + 1) * P], ident[:, :])
            ins.then_inc(pt_ready, 1)

        def logits(t, j):
            pe.wait_ge(xf_ready, t + 1 + LEAD)
            pe.wait_ge(aff_ready, t + 1)
            for k in range(KC):
                ins = pe.matmul(pl[j][:, :], xf[j][:, k, :], router[0][:, k, :], start=(k == 0), stop=(k == KC - 1))
            ins.then_inc(logit_ready, 1)

        one_behind(pe, NT, transpose, logits if router else nothing)

    def scalar(act):
        act.sem_inc(xf_ready, LEAD)
        if router:
            act.sem_inc(aff_ready, LEAD)
        ln_root(act, stat, root_ready, rstd, start)
        if router:
            act.preload_act_table(ACT.Sigmoid)

        def copy_out(t, j):
            if router:
                act.wait_ge(xn_ready, t + 1)
                act.activation(router[2][:, t, 0:C], xn[j][:, :], ACT.Copy).then_inc(row_hi, 1)
            act.wait_ge(pt_ready, t + 1 + LEAD)
            act.wait_ge(lo_ready, t + 1)
            if router:
                act.wait_ge(logit_ready, t + 1)
            act.activation(xnT_hi[:, :, bass.ds(t * P, P)], pt[j][:, :, :], ACT.Copy)
            act.activation(xf[j][:, :, :], pt[j][:, :, :], ACT.Copy).then_inc(xf_ready, 1)

        def affinity(t, j):
            act.wait_ge(logit_ready, t + 1 + LEAD)
            act.activation(router[1][:, t, :], pl[j][:, :], ACT.Sigmoid).then_inc(aff_ready, 1)

        one_behind(act, NT, copy_out, affinity if router else nothing)

    def gpsimd(pool):
        pool.sem_inc(lo_ready, LEAD)
        if router:
            pool.sem_inc(row_lo, LEAD)
        with pool.Fori(0, NT // 2) as i:
            for j in range(2):
                t = 2 * i + j
                if router:
                    pool.wait_ge(row_hi, t + 1)
                    pool.tensor_tensor(router[2][:, t, C:], xn[j][:, :], router[2][:, t, 0:C],
                                       ALU.subtract).then_inc(row_lo, 1)
                pool.wait_ge(xf_ready, t + 1 + LEAD)
                pool.tensor_tensor(xnT_lo[:, :, bass.ds(t * P, P)], xf[j][:, :, :],
                                   xnT_hi[:, :, bass.ds(t * P, P)], ALU.subtract).then_inc(lo_ready, 1)

    return vector, tensor, scalar, gpsimd, aff_ready


SLOTS = 256
SUB = SLOTS // P
TILES_R = (2 * TOK + E_ROUTED * (SLOTS - 1)) // SLOTS
W_ROW = KC * 2 * F_EXP + FC * C
GU = KC * 2 * F_EXP


def stage_route(nc, X, xnT, rows, share, slot, w_rows, ident, centroids, gate_bias, ff_part, scales, inv_w, gu, dn,
                w_gate_up, w_down):
    with ExitStack() as stack:
        m = Names(nc, stack, "route")
        wide = [P, NT, E_ROUTED]
        cent = m.sb("cent", [P, KC, E_ROUTED], F32)
        bias = m.sb("bias", [P, E_ROUTED], F32)
        aff = m.sb("aff", wide, F32)
        biased = m.sb("biased", wide, F32)
        top_v = m.sb("top_v", [P, NT, 8], F32)
        top_i = m.sb("top_i", [P, NT, 8], U32)
        top_f = m.sb("top_f", [P, NT, 2], F32)
        expert_no = m.sb("expert_no", wide, F32)
        tile_no = m.sb("tile_no", [P, TILES_R, E_ROUTED], F32)
        row_no = m.sb("row_no", [P, TILES_R], F32)
        earlier = m.sb("earlier", [P, P], BF16)
        ones = m.sb("ones", [P, P], BF16)
        hot = [m.sb(f"hot{k}", wide, F32) for k in range(2)]
        both = m.sb("both", [P, NT * E_ROUTED], BF16)
        picked = [m.sb(f"picked{k}", wide, F32) for k in range(2)]
        total = m.sb("total", [P, NT], F32)
        before = m.sb("before", [P, NT + 1, E_ROUTED], F32)
        filled = m.sb("filled", [P, E_ROUTED], F32)
        filled_i = m.sb("filled_i", [P, E_ROUTED], I32)
        tiles = m.sb("tiles", [P, E_ROUTED], F32)
        tiles_end = m.sb("tiles_end", [P, E_ROUTED], F32)
        base = m.sb("base", [P, E_ROUTED], F32)
        one_row = m.sb("one_row", [P, E_ROUTED], F32)
        place = m.sb("place", wide, F32)
        slot_f = [m.sb(f"slot_f{k}", [P, NT], F32) for k in range(2)]
        passed = m.sb("passed", [P, TILES_R, E_ROUTED], F32)
        owner = m.sb("owner", [P, TILES_R], F32)
        p_rank = m.ps("p_rank", [P, NT * E_ROUTED], F32)
        p_count = m.ps("p_count", [P, NT, E_ROUTED], F32)
        ff_top = m.sb("ff_top", [P, 2], F32)
        ff_top_all = m.sb("ff_top_all", [P, 2], F32)
        top_ready = m.sem("top_ready")
        all_ready = m.sem("all_ready")
        gu_f = [m.sb(f"gu_f{e}", [P, KC, 2 * F_EXP], F32) for e in range(2)]
        dn_f = [m.sb(f"dn_f{e}", [P, FC, C], F32) for e in range(2)]
        shared_loaded = m.sem("shared_loaded")
        shared_hi = m.sem("shared_hi")
        loaded = m.sem("loaded")
        made = m.sem("made")
        step = m.sem("step")
        both_ready = m.sem("both_ready")
        count_ready = m.sem("count_ready")
        vector, tensor, scalar, gpsimd, aff_ready = ln_transpose(m, X, xnT, ident, (cent, aff, rows))

        with nc.Block() as block:
            @block.sync
            def _(sp):
                sp.dma_start(cent[:, :, :], centroids).then_inc(loaded, 16)
                sp.dma_start(bias[:, :], gate_bias).then_inc(loaded, 16)
                for e in range(2):
                    sp.dma_start(gu_f[e][:, :, :], w_gate_up[e]).then_inc(shared_loaded, 16)
                    sp.dma_start(dn_f[e][:, :, :], w_down[e]).then_inc(shared_loaded, 16)
                sp.wait_ge(loaded, 32)

            @block.tensor
            def _(pe):
                pe.wait_ge(loaded, 32)
                tensor(pe)
                pe.wait_ge(both_ready, 1)
                pe.wait_ge(made, 6)
                pe.matmul(p_count[:, :, :].rearrange("p t e -> p (t e)"), ones[:, :], both[:, :],
                          start=True, stop=True).then_inc(count_ready, 1)
                pe.matmul(p_rank[:, :], earlier[:, :], both[:, :], start=True, stop=True).then_inc(count_ready, 1)

            @block.scalar
            def _(act):
                scalar(act)
                act.wait_ge(shared_loaded, 64)
                for e in range(2):
                    for parts, full in ((gu[e], gu_f[e]), (dn[e], dn_f[e])):
                        act.activation(parts[0][:, :, :], full[:, :, :], ACT.Copy).then_inc(shared_hi, 1)

            @block.gpsimd
            def _(pool):
                pool.iota(expert_no[:, :, :], [[0, NT], [1, E_ROUTED]], base=0, channel_multiplier=0,
                          allow_small_or_imprecise_dtypes=True).then_inc(made, 1)
                pool.iota(tile_no[:, :, :], [[1, TILES_R], [0, E_ROUTED]], base=0, channel_multiplier=0,
                          allow_small_or_imprecise_dtypes=True).then_inc(made, 1)
                pool.iota(row_no[:, :], [[0, TILES_R]], base=0, channel_multiplier=1,
                          allow_small_or_imprecise_dtypes=True).then_inc(made, 1)
                pool.memset(ones[:, :], 1.0).then_inc(made, 1)
                pool.memset(earlier[:, :], 1.0).then_inc(made, 1)
                pool.wait_ge(made, 5)
                pool.affine_select(out=earlier[:, :], in_=earlier[:, :], compare_op=ALU.is_gt, fill=0.0, base=0,
                                   pattern=[[1, P]], channel_multiplier=-1).then_inc(made, 1)
                gpsimd(pool)
                pool.wait_ge(top_ready, 1)
                pool.partition_all_reduce(ff_top_all[:, :], ff_top[:, :], P,
                                          bass.bass_isa.ReduceOp.max).then_inc(all_ready, 1)
                for e in range(2):
                    for i, (parts, full) in enumerate(((gu[e], gu_f[e]), (dn[e], dn_f[e]))):
                        pool.wait_ge(shared_hi, 2 * e + i + 1)
                        pool.tensor_tensor(parts[1][:, :, :], full[:, :, :], parts[0][:, :, :], ALU.subtract)

            @block.vector
            def _(dve):
                dve.tensor_reduce(ff_top[:, :], ff_part[:, :].rearrange("p (w t) -> p w t", w=2), AX.X,
                                  ALU.max).then_inc(top_ready, 1)
                dve.memset(before[:, 0, :], 0.0).then_inc(step, 1)
                dve.memset(one_row[:, :], 1.0).then_inc(step, 1)
                vector(dve)
                done = Steps(dve, step)
                done.n = 2
                dve.wait_ge(loaded, 32)
                dve.wait_ge(made, 3)
                dve.wait_ge(aff_ready, NT + LEAD)
                done.mark(dve.tensor_tensor(biased[:, :, :], aff[:, :, :],
                                            bias[:, :].unsqueeze(1).to_broadcast(wide), ALU.add))
                done.wait()
                for t in range(NT):
                    done.mark(dve.max(top_v[:, t, :], biased[:, t, :]))
                done.wait()
                for t in range(NT):
                    done.mark(dve.max_index(top_i[:, t, :], top_v[:, t, :], biased[:, t, :]))
                done.wait()
                done.mark(dve.tensor_copy(top_f[:, :, :], top_i[:, :, 0:2]))
                done.wait()
                for k in range(2):
                    done.mark(dve.tensor_tensor(hot[k][:, :, :], expert_no[:, :, :],
                                                top_f[:, :, k:k + 1].to_broadcast(wide), ALU.is_equal))
                done.wait()
                dve.tensor_tensor(both[:, :], hot[0][:, :, :].rearrange("p t e -> p (t e)"),
                                  hot[1][:, :, :].rearrange("p t e -> p (t e)"), ALU.add).then_inc(both_ready, 1)
                for k in range(2):
                    done.mark(dve.tensor_tensor(picked[k][:, :, :], aff[:, :, :], hot[k][:, :, :], ALU.mult))
                done.wait()
                for k in range(2):
                    done.mark(dve.tensor_reduce(share[k][:, :], picked[k][:, :, :], AX.X, ALU.add))
                done.wait()
                done.mark(dve.tensor_tensor(total[:, :], share[0][:, :], share[1][:, :], ALU.add))
                done.wait()
                done.mark(dve.tensor_scalar(total[:, :], total[:, :], 1e-9, None, ALU.add))
                done.wait()
                done.mark(dve.reciprocal(total[:, :], total[:, :]))
                done.wait()
                for k in range(2):
                    done.mark(dve.tensor_tensor(share[k][:, :], share[k][:, :], total[:, :], ALU.mult))
                dve.wait_ge(count_ready, 2)
                for t in range(NT):
                    done.wait()
                    done.mark(dve.tensor_tensor(before[:, t + 1, :], before[:, t, :], p_count[:, t, :], ALU.add))
                done.wait()
                done.mark(dve.tensor_scalar(filled[:, :], before[:, NT, :], SLOTS - 1.0, None, ALU.add))
                done.wait()
                done.mark(dve.tensor_copy(filled_i[:, :], filled[:, :]))
                done.wait()
                done.mark(dve.tensor_scalar(filled_i[:, :], filled_i[:, :], SLOTS.bit_length() - 1, None,
                                            ALU.arith_shift_right))
                done.wait()
                done.mark(dve.tensor_copy(tiles[:, :], filled_i[:, :]))
                done.wait()
                done.mark(dve.tensor_tensor_scan(tiles_end[:, :], one_row[:, :], tiles[:, :], 0.0, ALU.mult, ALU.add))
                done.wait()
                done.mark(dve.tensor_tensor(base[:, :], tiles_end[:, :], tiles[:, :], ALU.subtract))
                done.wait()
                done.mark(dve.tensor_scalar(base[:, :], base[:, :], float(SLOTS), None, ALU.mult))
                done.mark(dve.tensor_tensor(place[:, :, :], p_rank[:, :].rearrange("p (t e) -> p t e", e=E_ROUTED),
                                            before[:, 0:NT, :], ALU.add))
                done.wait()
                done.mark(dve.tensor_tensor(place[:, :, :], place[:, :, :],
                                            base[:, :].unsqueeze(1).to_broadcast(wide), ALU.add))
                done.wait()
                for k in range(2):
                    done.mark(dve.tensor_tensor(picked[k][:, :, :], place[:, :, :], hot[k][:, :, :], ALU.mult))
                done.wait()
                for k in range(2):
                    done.mark(dve.tensor_reduce(slot_f[k][:, :], picked[k][:, :, :], AX.X, ALU.add))
                done.wait()
                for k in range(2):
                    done.mark(dve.tensor_copy(slot[k][:, :], slot_f[k][:, :]))
                done.mark(dve.tensor_tensor(passed[:, :, :], tile_no[:, :, :], tiles_end[:, :].unsqueeze(1)
                                            .to_broadcast([P, TILES_R, E_ROUTED]), ALU.is_ge))
                done.wait()
                done.mark(dve.tensor_reduce(owner[:, :], passed[:, :, :], AX.X, ALU.add))
                done.wait()
                done.mark(dve.tensor_scalar(owner[:, :], owner[:, :], E_ROUTED - 1.0, float(P), ALU.min, ALU.mult))
                done.wait()
                done.mark(dve.tensor_tensor(owner[:, :], owner[:, :], row_no[:, :], ALU.add))
                done.wait()
                done.mark(dve.tensor_copy(w_rows[:, :], owner[:, :]))
                dve.wait_ge(all_ready, 1)
                done.mark(dve.tensor_scalar(scales[:, 0:2], ff_top_all[:, :], 1.0 / FP8_MAX, 1e-6, ALU.mult, ALU.max))
                done.wait()
                done.mark(dve.reciprocal(inv_w[:, :], scales[:, 0:2]))
                done.wait()


def stage_norm(nc, X, xnT, ident, stats):
    with ExitStack() as stack:
        vector, tensor, scalar, gpsimd, _ = ln_transpose(Names(nc, stack, "norm"), X, xnT, ident, stats=stats)
        with nc.Block() as block:
            block.tensor(tensor)
            block.scalar(scalar)
            block.vector(vector)
            block.gpsimd(gpsimd)


def stage_shared(nc, X, xnT, rows, slot, slot_rows, gu, dn, w_ff, w8_ff, inv_w):
    n_exp = 2
    NG = TOK // 512
    Y_LEAD = 2 * 4 * NG
    with ExitStack() as stack:
        m = Names(nc, stack, "shared")
        act_g = [m.sb(f"act_g{f}", [P, 512], F32) for f in range(FC)]
        hid = [m.sb(f"hid{f}", [P, 512], F32) for f in range(FC)]
        hid_hi = [m.sb(f"hid_hi{f}", [P, 512], BF16) for f in range(FC)]
        hid_lo = [m.sb(f"hid_lo{f}", [P, 512], BF16) for f in range(FC)]
        pg = [m.ps(f"pg{f}", [P, 512], F32) for f in range(FC)]
        pu = [m.ps(f"pu{f}", [P, 512], F32) for f in range(FC)]
        py = [m.ps(f"py{i}", [P, C], F32) for i in range(4)]

        Q_PIECES = 4
        Q_W = w_ff.shape[1] // (n_exp * NG * Q_PIECES)
        ff = [m.sb(f"ff{j}", [P, Q_W], F32) for j in range(Q_PIECES)]
        ff_v = [m.sb(f"ff_v{j}", [P, Q_W], F32) for j in range(Q_PIECES)]
        ff_m = [m.sb(f"ff_m{j}", [P, Q_W], F32) for j in range(2)]
        ff_8 = [m.sb(f"ff_8{j}", [P, Q_W], BF16) for j in range(Q_PIECES)]
        ff_loaded = [m.sem(f"ff_loaded{j}") for j in range(Q_PIECES)]
        ff_stored = [m.sem(f"ff_stored{j}") for j in range(Q_PIECES)]
        v_ready = m.sem("v_ready")
        e_ready = m.sem("e_ready")
        m_ready = m.sem("m_ready")
        t_ready = m.sem("t_ready")
        o_ready = m.sem("o_ready")
        pg_ready = m.sem("pg_ready")
        pu_ready = m.sem("pu_ready")
        g_ready = m.sem("g_ready")
        hid_ready = m.sem("hid_ready")
        hi_ready = m.sem("hi_ready")
        lo_ready = m.sem("lo_ready")
        y_ready = m.sem("y_ready")
        y_added = m.sem("y_added")
        scattered = m.sem("scattered")

        with nc.Block() as block:
            @block.sync
            def _(sp):
                def load(n):
                    for j in range(Q_PIECES):
                        sp.wait_ge(v_ready, Q_PIECES * n + j + 1)
                        sp.dma_start(ff[j][:, :], w_ff[:, bass.ds((Q_PIECES * n + j) * Q_W, Q_W)]
                                     ).then_inc(ff_loaded[j], 16)

                def store(n):
                    for j in range(Q_PIECES):
                        sp.wait_ge(o_ready, Q_PIECES * n + j + 1 + Q_PIECES)
                        sp.dma_start(w8_ff[:, bass.ds((Q_PIECES * n + j) * Q_W, Q_W)], ff_8[j][:, :]
                                     ).then_inc(ff_stored[j], 16)

                load(0)
                with sp.Fori(1, n_exp * NG) as n:
                    load(n)
                    store(n - 1)
                store(n_exp * NG - 1)
                for j in range(Q_PIECES):
                    sp.wait_ge(ff_stored[j], 16 + 16 * n_exp * NG)

            @block.gpsimd
            def _(pool):
                for t in range(NT):
                    for k in range(2):
                        pool.indirect_dma_start(slot_rows, bass.IndirectOffsetOnAxis(ap=slot[k][:, t:t + 1], axis=0),
                                                rows[:, t, :], None).then_inc(scattered, 16)
                pool.wait_ge(scattered, 2 * NT * 16)

            @block.tensor
            def _(pe):
                pe.sem_inc(y_ready, Y_LEAD)
                for j in range(2):
                    with pe.Fori(0, NG) as g:
                        n = j * NG + g
                        for f in range(FC):
                            for which, bank, ready in ((0, pg, pg_ready), (1, pu, pu_ready)):
                                pe.wait_ge((g_ready, hid_ready)[which], FC * n + f + 1)
                                for k in range(KC):
                                    for a, b in ((0, 0), (0, 1), (1, 0)):
                                        col = which * F_EXP + f * P
                                        ins = pe.matmul(bank[f][:, :], gu[j][a][:, k, col:col + P],
                                                        xnT[b][:, k, bass.ds(g * 512, 512)],
                                                        start=(k == 0 and a + b == 0),
                                                        stop=(k == KC - 1 and a == 1))
                                ins.then_inc(ready, 1)
                        for f in range(FC):
                            pe.wait_ge(lo_ready, FC * n + f + 1)
                            for i in range(4):
                                if f == 0:
                                    pe.wait_ge(y_added, 4 * n + i + 1)
                                for h, w in ((hid_hi, 0), (hid_hi, 1), (hid_lo, 0)):
                                    ins = pe.matmul(py[i][:, :], h[f][:, i * P:(i + 1) * P], dn[j][w][:, f, :],
                                                    start=(f == 0 and h is hid_hi and w == 0),
                                                    stop=(f == FC - 1 and h is hid_lo))
                                if f == FC - 1:
                                    ins.then_inc(y_ready, 1)

            @block.scalar
            def _(act):
                act.preload_act_table(ACT.Silu)
                act.sem_inc(g_ready, LEAD)
                act.sem_inc(v_ready, Q_PIECES)
                for e in range(n_exp):
                    with act.Fori(0, NG) as g:
                        n = e * NG + g
                        for j in range(Q_PIECES):
                            act.wait_ge(ff_loaded[j], 16 * n + 16)
                            act.wait_ge(o_ready, Q_PIECES * n + j + 1)
                            act.activation(ff_v[j][:, :], ff[j][:, :], ACT.Copy, scale=inv_w[:, e:e + 1]
                                           ).then_inc(v_ready, 1)
                        for f in range(FC):
                            act.wait_ge(pg_ready, FC * n + f + 1)
                            act.wait_ge(hid_ready, FC * n + f + 1)
                            act.activation(act_g[f][:, :], pg[f][:, :], ACT.Silu).then_inc(g_ready, 1)
                            act.wait_ge(hid_ready, FC * n + f + 1 + LEAD)
                            act.wait_ge(y_ready, 4 * n + Y_LEAD)
                            act.activation(hid_hi[f][:, :], hid[f][:, :], ACT.Copy).then_inc(hi_ready, 1)

            @block.vector
            def _(dve):
                dve.sem_inc(hid_ready, LEAD)
                dve.sem_inc(y_added, 4)
                dve.sem_inc(o_ready, Q_PIECES)
                for j in range(Q_PIECES):
                    dve.sem_inc(ff_stored[j], 16)

                def hidden(n, f):
                    dve.wait_ge(g_ready, FC * n + f + 1 + LEAD)
                    dve.wait_ge(pu_ready, FC * n + f + 1)
                    dve.tensor_tensor(hid[f][:, :], act_g[f][:, :], pu[f][:, :], ALU.mult).then_inc(hid_ready, 1)
                    dve.wait_ge(hi_ready, FC * n + f + 1)
                    dve.tensor_tensor(hid_lo[f][:, :], hid[f][:, :], hid_hi[f][:, :],
                                      ALU.subtract).then_inc(lo_ready, 1)

                def round_pieces(n, pieces):
                    for j in pieces:
                        i = Q_PIECES * n + j
                        dve.wait_ge(v_ready, i + 1 + Q_PIECES)
                        dve.wait_ge(o_ready, i + 3)
                        dve.tensor_scalar(ff_m[j % 2][:, :].bitcast(I32), ff_v[j][:, :].bitcast(I32), 0x7F800000, None,
                                          ALU.bitwise_and).then_inc(e_ready, 1)
                    for j in pieces:
                        dve.wait_ge(e_ready, Q_PIECES * n + j + 1)
                        dve.tensor_scalar(ff_m[j % 2][:, :], ff_m[j % 2][:, :], 2.0 ** -6, 1.5 * 2.0 ** 20,
                                          ALU.max, ALU.mult).then_inc(m_ready, 1)
                    for j in pieces:
                        dve.wait_ge(m_ready, Q_PIECES * n + j + 1)
                        dve.tensor_tensor(ff_v[j][:, :], ff_v[j][:, :], ff_m[j % 2][:, :], ALU.add).then_inc(t_ready, 1)
                    for j in pieces:
                        dve.wait_ge(t_ready, Q_PIECES * n + j + 1)
                        dve.wait_ge(ff_stored[j], 16 * n + 16)
                        dve.tensor_tensor(ff_8[j][:, :], ff_v[j][:, :], ff_m[j % 2][:, :],
                                          ALU.subtract).then_inc(o_ready, 1)

                with dve.Fori(0, n_exp) as e:
                    with dve.Fori(0, NG) as g:
                        n = e * NG + g
                        round_pieces(n, (0, 1))
                        hidden(n, 0)
                        round_pieces(n, (2, 3))
                        hidden(n, 1)
                        for i in range(4):
                            dve.wait_ge(y_ready, 4 * n + i + 1 + Y_LEAD)
                            xt = X[:, 4 * g + i, :]
                            dve.scalar_tensor_tensor(xt, py[i][:, :], SHARED_RATIO, xt,
                                                     ALU.mult, ALU.add).then_inc(y_added, 1)


def stage_routed(nc, slot_rows, slot_out, w_rows, w_table):
    assert TILES_R % 2 == 1
    with ExitStack() as stack:
        m = Names(nc, stack, "routed")
        w_f = [m.sb(f"w_f{j}", [P, W_ROW], F32) for j in range(2)]
        w = [[m.sb(f"w_{h}{j}", [P, W_ROW], BF16) for h in ("hi", "lo")] for j in range(2)]
        row = [m.sb(f"row{j}", [P, 1], U32) for j in range(2)]
        xr = [m.sb(f"xr{j}", [P, SUB, 2 * C], BF16) for j in range(2)]
        xT = [[m.sb(f"xT_{h}{j}", [P, KC, SLOTS], BF16) for h in ("hi", "lo")] for j in range(2)]
        act_g = [m.sb(f"act_g{f}", [P, SLOTS], F32) for f in range(FC)]
        hid = [m.sb(f"hid{f}", [P, SLOTS], F32) for f in range(FC)]
        hid_p = [[[m.sb(f"hid_{h}{f}{j}", [P, SLOTS], BF16) for h in ("hi", "lo")] for f in range(FC)]
                 for j in range(2)]
        y = [m.sb(f"y{j}", [P, SUB, C], F32) for j in range(2)]
        pt = [m.ps(f"pt_{h}", [P, KC, SLOTS], BF16) for h in ("hi", "lo")]
        pg = [m.ps(f"pg{f}", [P, 512], F32) for f in range(FC)]
        pu = [m.ps(f"pu{f}", [P, 512], F32) for f in range(FC)]
        py = [m.ps(f"py{s}", [P, C], F32) for s in range(SUB)]
        ident_bf = m.sb("ident", [P, P], BF16)

        made = m.sem("made")
        x_loaded = [m.sem(f"x_loaded{j}") for j in range(2)]
        w_loaded = [m.sem(f"w_loaded{j}") for j in range(2)]
        stored = [m.sem(f"stored{j}") for j in range(2)]
        t_ready = m.sem("t_ready")
        xt_hi = m.sem("xt_hi")
        xt_lo = m.sem("xt_lo")
        gu_hi = m.sem("gu_hi")
        gu_lo = m.sem("gu_lo")
        dn_hi = m.sem("dn_hi")
        dn_lo = m.sem("dn_lo")
        turn = m.sem("turn")
        row_ready = m.sem("row_ready")
        pg_ready = m.sem("pg_ready")
        pu_ready = m.sem("pu_ready")
        g_ready = m.sem("g_ready")
        hid_ready = m.sem("hid_ready")
        hi_ready = m.sem("hi_ready")
        lo_ready = m.sem("lo_ready")
        y_ready = m.sem("y_ready")
        y_copied = m.sem("y_copied")

        def walk(eng, first, last, turn_of):
            i = first
            if i % 2:
                turn_of(i, 1)
                i += 1
            with eng.Fori(0, (last + 1 - i) // 2) as m2:
                for j in range(2):
                    turn_of(2 * m2 + i + j, j)
            if (last + 1 - i) % 2:
                turn_of(last, last % 2)

        with nc.Block() as block:
            @block.sync
            def _(sp):
                def load(i, j):
                    sp.wait_ge(t_ready, i + 1)
                    sp.dma_start(xr[j][:, :, :], slot_rows[bass.ds(i * SLOTS, SLOTS), :]
                                 .rearrange("(s p) c -> p s c", p=P)).then_inc(x_loaded[j], 16)

                walk(sp, 0, TILES_R - 1, load)

            @block.tensor
            def _(pe):
                pe.sem_inc(t_ready, LEAD)
                pe.sem_inc(pu_ready, 2 * FC)
                pe.sem_inc(y_ready, 2 * SUB)
                pe.wait_ge(made, 2)

                def transposes(i, j):
                    pe.wait_ge(x_loaded[j], 16 * ((i - j) // 2 + 1) if isinstance(i, int) else 8 * (i - j) + 16)
                    pe.wait_ge(xt_hi, i + LEAD)
                    pe.wait_ge(xt_lo, i + LEAD)
                    for h in range(2):
                        for s in range(SUB):
                            for k in range(KC):
                                ins = pe.transpose(pt[h][:, k, s * P:(s + 1) * P],
                                                   xr[j][:, s, h * C + k * P:h * C + (k + 1) * P], ident_bf[:, :])
                    ins.then_inc(t_ready, 1)

                def gate_up(i, j, f):
                    if f == 0:
                        pe.wait_ge(gu_lo, i + 1)
                        pe.wait_ge(xt_hi, i + 1 + LEAD)
                        pe.wait_ge(xt_lo, i + 1 + LEAD)
                    for which, bank, ready, free in ((0, pg, pg_ready, g_ready), (1, pu, pu_ready, hid_ready)):
                        pe.wait_ge(free, FC * i + f + 1)
                        for k in range(KC):
                            at = k * 2 * F_EXP + which * F_EXP + f * P
                            for a, b in ((0, 0), (0, 1), (1, 0)):
                                ins = pe.matmul(bank[f][:, 0:SLOTS], w[j][a][:, at:at + P], xT[j][b][:, k, :],
                                                start=(k == 0 and a + b == 0), stop=(k == KC - 1 and a == 1))
                        ins.then_inc(ready, 1)

                def down(i, j):
                    pe.wait_ge(dn_lo, i + 1)
                    for f in range(FC):
                        pe.wait_ge(lo_ready, FC * i + f + 1 + FC)
                        for s in range(SUB):
                            if f == 0:
                                pe.wait_ge(y_copied, SUB * i + s + 1)
                            for a, b in ((0, 0), (0, 1), (1, 0)):
                                at = GU + f * C
                                ins = pe.matmul(py[s][:, :], hid_p[j][f][a][:, s * P:(s + 1) * P],
                                                w[j][b][:, at:at + C], start=(f == 0 and a + b == 0),
                                                stop=(f == FC - 1 and a == 1))
                            if f == FC - 1:
                                ins.then_inc(y_ready, 1)

                def turn_of(i, j):
                    gate_up(i, j, 0)
                    transposes(i + 1, 1 - j)
                    down(i - 1, 1 - j)
                    gate_up(i, j, 1)

                transposes(0, 0)
                gate_up(0, 0, 0)
                transposes(1, 1)
                gate_up(0, 0, 1)
                walk(pe, 1, TILES_R - 2, turn_of)
                gate_up(TILES_R - 1, 0, 0)
                down(TILES_R - 2, 1)
                gate_up(TILES_R - 1, 0, 1)
                down(TILES_R - 1, 0)

            @block.scalar
            def _(act):
                act.preload_act_table(ACT.Silu)
                act.sem_inc(xt_hi, LEAD)
                act.sem_inc(g_ready, FC)

                def weights(i, j, part):
                    if part == 0:
                        act.wait_ge(w_loaded[j], 8 * (i - j) + 16)
                        act.wait_ge(pu_ready, FC * i + FC)
                    if part == 2:
                        act.wait_ge(y_ready, SUB * i + SUB)
                    at = slice(part * GU // 2, min((part + 1) * GU // 2, W_ROW))
                    ins = act.activation(w[j][0][:, at], w_f[j][:, at], ACT.Copy)
                    if part:
                        ins.then_inc((gu_hi, dn_hi)[part - 1], 1)

                def x_high(i, j):
                    act.wait_ge(t_ready, i + 1 + LEAD)
                    act.wait_ge(pu_ready, FC * i + FC)
                    act.activation(xT[j][0][:, :, :], pt[0][:, :, :], ACT.Copy).then_inc(xt_hi, 1)

                def store(i, j):
                    act.wait_ge(y_copied, SUB * i + 2 * SUB)
                    act.dma_start(slot_out[bass.ds(i * SLOTS, SLOTS), :].rearrange("(s p) c -> p s c", p=P),
                                  y[j][:, :, :]).then_inc(stored[j], 16)

                def silu(i, f):
                    act.wait_ge(pg_ready, FC * i + f + 1)
                    act.wait_ge(hid_ready, FC * i + f + 1)
                    act.activation(act_g[f][:, :], pg[f][:, 0:SLOTS], ACT.Silu).then_inc(g_ready, 1)

                def hidden_high(i, j, f):
                    act.wait_ge(hid_ready, FC * i + f + 1 + FC)
                    act.wait_ge(y_ready, SUB * i + SUB)
                    act.activation(hid_p[j][f][0][:, :], hid[f][:, :], ACT.Copy).then_inc(hi_ready, 1)

                def turn_of(i, j):
                    if not isinstance(i, int) or i >= 2:
                        store(i - 2, j)
                    silu(i - 1, 1)
                    weights(i + 1, 1 - j, 0)
                    hidden_high(i - 1, 1 - j, 1)
                    weights(i + 1, 1 - j, 1)
                    silu(i, 0)
                    x_high(i + 1, 1 - j)
                    hidden_high(i, j, 0)
                    weights(i + 1, 1 - j, 2)

                for part in range(3):
                    weights(0, 0, part)
                x_high(0, 0)
                weights(1, 1, 0)
                weights(1, 1, 1)
                silu(0, 0)
                x_high(1, 1)
                hidden_high(0, 0, 0)
                weights(1, 1, 2)
                walk(act, 1, TILES_R - 2, turn_of)
                last = TILES_R - 1
                silu(last - 1, 1)
                hidden_high(last - 1, 1, 1)
                silu(last, 0)
                hidden_high(last, 0, 0)
                store(last - 2, 0)
                silu(last, 1)
                hidden_high(last, 0, 1)
                store(last - 1, 1)
                store(last, 0)
                for j in range(2):
                    act.wait_ge(stored[j], 16 + 16 * ((TILES_R + 1 - j) // 2))

            @block.vector
            def _(dve):
                dve.sem_inc(xt_lo, LEAD)
                dve.sem_inc(hid_ready, FC)
                dve.sem_inc(lo_ready, FC)
                dve.sem_inc(y_copied, SUB)
                dve.sem_inc(stored[0], 16)
                dve.sem_inc(stored[1], 16)

                def x_low(i, j):
                    dve.wait_ge(t_ready, i + 1 + LEAD)
                    dve.wait_ge(pu_ready, FC * i + FC)
                    dve.tensor_copy(xT[j][1][:, :, :], pt[1][:, :, :]).then_inc(xt_lo, 1)

                def hidden(i, f):
                    dve.wait_ge(g_ready, FC * i + f + 1 + FC)
                    dve.wait_ge(pu_ready, FC * i + f + 1 + 2 * FC)
                    dve.wait_ge(lo_ready, FC * i + f + 1)
                    dve.tensor_tensor(hid[f][:, :], act_g[f][:, :], pu[f][:, 0:SLOTS], ALU.mult).then_inc(hid_ready, 1)

                def hidden_low(i, j, f):
                    dve.wait_ge(hi_ready, FC * i + f + 1)
                    dve.tensor_tensor(hid_p[j][f][1][:, :], hid[f][:, :], hid_p[j][f][0][:, :],
                                      ALU.subtract).then_inc(lo_ready, 1)

                def down_low(i, j):
                    dve.wait_ge(dn_hi, i + 1)
                    dve.tensor_tensor(w[j][1][:, GU:], w_f[j][:, GU:], w[j][0][:, GU:], ALU.subtract).then_inc(dn_lo, 1)

                def copy_out(i, j):
                    for s in range(SUB):
                        dve.wait_ge(y_ready, SUB * i + s + 1 + 2 * SUB)
                        if s == 0:
                            dve.wait_ge(stored[j], 8 * (i - j) + 16)
                        dve.tensor_copy(y[j][:, s, :], py[s][:, :]).then_inc(y_copied, 1)

                def turn_of(i, j):
                    hidden(i - 1, 1)
                    hidden_low(i - 1, 1 - j, 1)
                    hidden(i, 0)
                    x_low(i + 1, 1 - j)
                    hidden_low(i, j, 0)
                    copy_out(i - 1, 1 - j)
                    down_low(i + 1, 1 - j)

                down_low(0, 0)
                x_low(0, 0)
                hidden(0, 0)
                x_low(1, 1)
                hidden_low(0, 0, 0)
                down_low(1, 1)
                walk(dve, 1, TILES_R - 2, turn_of)
                last = TILES_R - 1
                hidden(last - 1, 1)
                hidden_low(last - 1, 1, 1)
                hidden(last, 0)
                hidden_low(last, 0, 0)
                copy_out(last - 1, 1)
                hidden(last, 1)
                hidden_low(last, 0, 1)
                copy_out(last, 0)

            @block.gpsimd
            def _(pool):
                pool.memset(ident_bf[:, :], 0.0).then_inc(made, 1)
                pool.wait_ge(made, 1)
                pool.affine_select(out=ident_bf[:, :], in_=ident_bf[:, :], compare_op=ALU.not_equal, fill=1.0, base=0,
                                   pattern=[[-1, P]], channel_multiplier=1).then_inc(made, 1)

                def fetch(i, j):
                    pool.tensor_copy(row[j][:, :], w_rows[:, bass.ds(i, 1)]).then_inc(row_ready, 1)
                    pool.wait_ge(row_ready, i + 1)
                    pool.sem_inc(turn, 1)
                    pool.indirect_dma_start(w_f[j][:, :], None, w_table,
                                            bass.IndirectOffsetOnAxis(ap=row[j][:, :], axis=0)
                                            ).then_inc(w_loaded[j], 16)

                def low(i, j):
                    pool.wait_ge(gu_hi, i + 1)
                    pool.tensor_tensor(w[j][1][:, 0:GU], w_f[j][:, 0:GU], w[j][0][:, 0:GU],
                                       ALU.subtract).then_inc(gu_lo, 1)

                def turn_of(i, j):
                    low(i, j)
                    pool.wait_ge(gu_lo, i + 1)
                    pool.wait_ge(dn_lo, i + 1)
                    pool.sem_inc(turn, 1)
                    fetch(i + 2, j)

                fetch(0, 0)
                fetch(1, 1)
                walk(pool, 0, TILES_R - 3, turn_of)
                low(TILES_R - 2, 1)
                low(TILES_R - 1, 0)


def stage_combine(nc, X, share, slot, slot_out, stats):
    DEPTH = 4
    with ExitStack() as stack:
        m = Names(nc, stack, "combine")
        y = [[m.sb(f"y{k}{j}", [P, C], F32) for k in range(2)] for j in range(DEPTH)]
        fetched = [m.sem(f"fetched{j}") for j in range(DEPTH)]
        x_added = m.sem("x_added")
        stats_ready = m.sem("stats_ready")
        with nc.Block() as block:
            @block.gpsimd
            def _(pool):
                for t in range(NT):
                    if t >= DEPTH:
                        pool.wait_ge(x_added, 2 * (t - DEPTH + 1))
                    for k in range(2):
                        pool.indirect_dma_start(y[t % DEPTH][k][:, :], None, slot_out,
                                                bass.IndirectOffsetOnAxis(ap=slot[k][:, t:t + 1], axis=0)
                                                ).then_inc(fetched[t % DEPTH], 16)

            @block.vector
            def _(dve):
                for t in range(NT):
                    dve.wait_ge(fetched[t % DEPTH], 32 * (t // DEPTH + 1))
                    for k in range(2):
                        if k:
                            dve.wait_ge(x_added, 2 * t + 1)
                        dve.scalar_tensor_tensor(X[:, t, :], y[t % DEPTH][k][:, :], share[k][:, t:t + 1], X[:, t, :],
                                                 ALU.mult, ALU.add).then_inc(x_added, 1)
                    dve.wait_ge(x_added, 2 * t + 2)
                    dve.bn_stats(stats[:, t, :], X[:, t, :]).then_inc(stats_ready, 1)


def stage_kv(nc, ctxT, KT, v_parts, ident, w, bias_kv, kn_w, slot_rows, w_ff, ff_part):
    W_PIECE = w_ff.shape[1] // NT
    Z_TILES = 4
    KW = NKV * HD
    with ExitStack() as stack:
        m = Names(nc, stack, "kv")
        bias = m.sb("bias", [P, 2, KW], F32)
        kw = m.sb("kw", [P, HD], F32)
        V = [m.sb(f"V_{h}", [P, NKV, NT, HD], BF16) for h in ("hi", "lo")]
        kf = [m.sb(f"kf{j}", [P, KW], F32) for j in range(2)]
        ksq = m.sb("ksq", [P, KW], F32)
        ssq = m.sb("ssq", [P, NKV], F32)
        msq = m.sb("msq", [P, NKV], F32)
        root = m.sb("root", [P, NKV], F32)
        rk = m.sb("rk", [P, NKV], F32)
        kn = [m.sb(f"kn{j}", [P, KW], F32) for j in range(2)]
        vf = [m.sb(f"vf{j}", [P, KW], F32) for j in range(2)]
        pk = [m.ps(f"pk{j}", [P, KW], F32) for j in range(2)]
        pv = [m.ps(f"pv{j}", [P, KW], F32) for j in range(2)]
        pt = [m.ps(f"pt{j}", [P, NKV, P], F32) for j in range(2)]
        zeros = m.sb("zeros", [P, Z_TILES, 2 * C], BF16)
        ff = [m.sb(f"ff{j}", [P, W_PIECE], F32) for j in range(2)]
        ff_loaded = [m.sem(f"ff_loaded{j}") for j in range(2)]
        ff_max = m.sem("ff_max")
        zeros_made = m.sem("zeros_made")
        zeroed = m.sem("zeroed")
        c_loaded = m.sem("c_loaded")
        pk_ready = m.sem("pk_ready")
        pv_ready = m.sem("pv_ready")
        kf_ready = m.sem("kf_ready")
        sq_ready = m.sem("sq_ready")
        step = m.sem("step")
        msq_ready = m.sem("msq_ready")
        root_ready = m.sem("root_ready")
        kn_ready = m.sem("kn_ready")
        pt_ready = m.sem("pt_ready")
        khi_ready = m.sem("khi_ready")
        klo_ready = m.sem("klo_ready")
        vf_ready = m.sem("vf_ready")
        vhi_ready = m.sem("vhi_ready")
        vlo_ready = m.sem("vlo_ready")
        v_stored = m.sem("v_stored")

        with nc.Block() as block:
            @block.sync
            def _(sp):
                sp.dma_start(bias[:, :, :], bias_kv).then_inc(c_loaded, 16)
                sp.dma_start(kw[:, :], kn_w).then_inc(c_loaded, 16)
                sp.wait_ge(zeros_made, 1)
                zero_rows = slot_rows.shape[0] // NT
                z_parts = zero_rows // Z_TILES
                assert z_parts * Z_TILES * NT == slot_rows.shape[0] and z_parts <= P
                V_TILES = 4

                def pieces(i):
                    for j in range(V_TILES):
                        t = V_TILES * i + j
                        sp.wait_ge(ff_max, t + 1)
                        sp.dma_start(ff[j % 2][:, :], w_ff[:, bass.ds(t * W_PIECE, W_PIECE)]
                                     ).then_inc(ff_loaded[j % 2], 16)
                        sp.dma_start(slot_rows[bass.ds(t * zero_rows, zero_rows), :]
                                     .rearrange("(s p) c -> p s c", p=z_parts), zeros[0:z_parts, :, :]
                                     ).then_inc(zeroed, 16)

                def store_v(i):
                    sp.wait_ge(vlo_ready, V_TILES * (i + 1) + LEAD)
                    for h in range(2):
                        for g in range(NKV):
                            sp.dma_start(v_parts[g, h, :, bass.ds(V_TILES * i, V_TILES), :],
                                         V[h][:, g, bass.ds(V_TILES * i, V_TILES), :]).then_inc(v_stored, 16)

                pieces(0)
                with sp.Fori(1, NT // V_TILES) as i:
                    pieces(i)
                    store_v(i - 1)
                store_v(NT // V_TILES - 1)
                sp.wait_ge(v_stored, (NT // V_TILES) * 2 * NKV * 16)
                sp.wait_ge(zeroed, 16 * NT)

            @block.tensor
            def _(pe):
                pe.sem_inc(pt_ready, LEAD)

                def project(t, j):
                    for which, bank, ready, free in ((0, pk, pk_ready, kf_ready), (1, pv, pv_ready, vf_ready)):
                        pe.wait_ge(free, t + 1)
                        for k in range(KC):
                            for a, b in ((0, 0), (0, 1), (1, 0)):
                                ins = pe.matmul(bank[j][:, :], ctxT[a][:, k, bass.ds(t * P, P)],
                                                w[b][:, which, k, :],
                                                start=(k == 0 and a + b == 0), stop=(k == KC - 1 and a == 1))
                        ins.then_inc(ready, 1)

                def transpose_k(t, j):
                    pe.wait_ge(kn_ready, t + 1)
                    pe.wait_ge(klo_ready, t + 1)
                    for h in range(NKV):
                        ins = pe.transpose(pt[j][:, h, :], kn[j][:, h * HD:(h + 1) * HD], ident[:, :])
                    ins.then_inc(pt_ready, 1)

                one_behind(pe, NT, project, transpose_k)

            @block.scalar
            def _(act):
                act.preload_act_table(ACT.Sqrt)

                def squares(t, j):
                    act.wait_ge(kf_ready, t + 1 + LEAD)
                    act.activation(ksq[:, :], kf[j][:, :], ACT.Square).then_inc(sq_ready, 1)
                    act.wait_ge(vf_ready, t + 1 + LEAD)
                    act.activation(V[0][:, :, t, :], vf[j][:, :].rearrange("p (g d) -> p g d", d=HD),
                                   ACT.Copy).then_inc(vhi_ready, 1)
                    act.wait_ge(msq_ready, t + 1)
                    act.activation(root[:, :], msq[:, :], ACT.Sqrt).then_inc(root_ready, 1)

                def high(t, j):
                    act.wait_ge(pt_ready, t + 1 + LEAD)
                    act.activation(KT[0][:, :, bass.ds(t * P, P)], pt[j][:, :, :], ACT.Copy).then_inc(khi_ready, 1)

                one_behind(act, NT, squares, high)

            @block.vector
            def _(dve):
                dve.sem_inc(kf_ready, LEAD)
                dve.sem_inc(vf_ready, LEAD)
                dve.sem_inc(klo_ready, LEAD)
                dve.sem_inc(ff_max, LEAD)
                dve.wait_ge(c_loaded, 32)
                STEPS = 2

                def normalise(t, j):
                    done = Steps(dve, step, STEPS * t)
                    dve.wait_ge(pk_ready, t + 1)
                    dve.tensor_tensor(kf[j][:, :], pk[j][:, :], bias[:, 0, :], ALU.add).then_inc(kf_ready, 1)
                    dve.wait_ge(pv_ready, t + 1)
                    dve.wait_ge(vlo_ready, t + 1)
                    dve.tensor_tensor(vf[j][:, :], pv[j][:, :], bias[:, 1, :], ALU.add).then_inc(vf_ready, 1)
                    dve.wait_ge(sq_ready, t + 1)
                    done.mark(dve.tensor_reduce(ssq[:, :], ksq[:, :].rearrange("p (g d) -> p g d", d=HD),
                                                AX.X, ALU.add))
                    done.wait()
                    dve.tensor_scalar(msq[:, :], ssq[:, :], 1.0 / HD, RMS_EPS, ALU.mult, ALU.add).then_inc(msq_ready, 1)
                    dve.wait_ge(root_ready, t + 1)
                    done.mark(dve.reciprocal(rk[:, :], root[:, :]))
                    done.wait()
                    dve.wait_ge(pt_ready, t + 1)
                    for h in range(NKV):
                        s = slice(h * HD, (h + 1) * HD)
                        ins = dve.scalar_tensor_tensor(kn[j][:, s], kf[j][:, s], rk[:, h:h + 1], kw[:, :],
                                                       ALU.mult, ALU.mult)
                        if h == NKV - 1:
                            ins.then_inc(kn_ready, 1)
                    assert done.n == STEPS

                def low(t, j):
                    dve.wait_ge(khi_ready, t + 1)
                    dve.tensor_tensor(KT[1][:, :, bass.ds(t * P, P)], pt[j][:, :, :], KT[0][:, :, bass.ds(t * P, P)],
                                      ALU.subtract).then_inc(klo_ready, 1)

                def weight_max(t, j):
                    dve.wait_ge(ff_loaded[j], 8 * (t - j) + 16)
                    dve.tensor_reduce(ff_part[:, bass.ds(t, 1)], ff[j][:, :], AX.X, ALU.max,
                                      apply_absolute_value=True).then_inc(ff_max, 1)

                def first(t, j):
                    normalise(t, j)
                    weight_max(t, j)

                one_behind(dve, NT, first, low)

            @block.gpsimd
            def _(pool):
                pool.sem_inc(vlo_ready, LEAD)
                pool.memset(zeros[:, :, :], 0.0).then_inc(zeros_made, 1)
                with pool.Fori(0, NT // 2) as i:
                    for j in range(2):
                        t = 2 * i + j
                        pool.wait_ge(vhi_ready, t + 1)
                        pool.tensor_tensor(V[1][:, :, t, :], vf[j][:, :].rearrange("p (g d) -> p g d", d=HD),
                                           V[0][:, :, t, :], ALU.subtract).then_inc(vlo_ready, 1)


def stage_attention(nc, X, xnT, KT, v_parts, ident_bf, mask, w_q, w_o, bq_cols, qn_w):
    TILES = GROUP * TPB
    ITS = NKV * B
    T_LAG = 6
    V_LAG = T_LAG + 2
    Q_TURN = {3: 0, 0: 2, 1: 4, 2: 6}
    SLOTS_P = 4
    with ExitStack() as stack:
        m = Names(nc, stack, "att")
        nmask = m.sb("nmask", [P, TPB, S], F32)
        w_f = m.sb("w_f", [P, 4, 512], F32)
        wq = [m.sb(f"wq_{h}", [P, 2 * KC, 512], BF16) for h in ("hi", "lo")]
        wo = [m.sb(f"wo_{h}", [P, GROUP, C], BF16) for h in ("hi", "lo")]
        V = [m.sb(f"V_{h}", [P, 2 * TPB, HD], BF16) for h in ("hi", "lo")]
        bq = m.sb("bq", [P, NH], F32)
        qw = m.sb("qw", [P, 1], F32)
        nqw = m.sb("nqw", [P, 1], F32)
        eps = m.sb("eps", [P, 1], F32)
        ones = m.sb("ones", [P, P], BF16)
        qf = [m.sb(f"qf{h}", [P, S], F32) for h in range(GROUP)]
        sq_f = m.sb("sq_f", [P, S], F32)
        sq = [m.sb(f"sq_{h}", [P, S], BF16) for h in ("hi", "lo")]
        rq = m.sb("rq", [P, S], F32)
        q = [m.sb(f"q_{h}", [P, GROUP, S], BF16) for h in ("hi", "lo")]
        s = [m.sb(f"s{j}", [P, S], F32) for j in range(2)]
        prob = [m.sb(f"prob{j}", [P, S], F32) for j in range(SLOTS_P)]
        p = [[m.sb(f"p_{h}{j}", [P, TPB, S], BF16) for h in ("hi", "lo")] for j in range(2)]
        low = m.sb("low", [P, TILES], F32)
        total = m.sb("total", [P, TILES], F32)
        inv = m.sb("inv", [P, TILES], F32)
        pT = [m.sb(f"pT{j}", [P, 2, S], BF16) for j in range(2)]
        oT = [m.sb(f"oT_{h}", [P, GROUP + 1, S], BF16) for h in ("hi", "lo")]
        bank_q = m.ps("bank_q", [P, 512], F32)
        bank_ss = m.ps("bank_ss", [P, 512], F32)
        bank_s = [m.ps(f"bank_s{j}", [P, 512], F32) for j in range(2)]
        bank_t = [m.ps(f"bank_t{j}", [P, 2, 512], BF16) for j in range(2)]
        bank_o = m.ps("bank_o", [P, 512], F32)
        bank_y = m.ps("bank_y", [P, 512], F32)

        Y0, PV0, S0, T0 = 5, 2 * TILES, TILES, 2 * TPB
        c_loaded = m.sem("c_loaded")
        const_ready = m.sem("const_ready")
        w_loaded = m.sem("w_loaded")
        v_loaded = m.sem("v_loaded")
        wq_split = m.sem("wq_split")
        wo_split = m.sem("wo_split")
        w_high = m.sem("w_high")
        q_proj = m.sem("q_proj")
        qf_ready = m.sem("qf_ready")
        sqf_ready = m.sem("sqf_ready")
        sq_hi = m.sem("sq_hi")
        sq_lo = m.sem("sq_lo")
        ss_ready = m.sem("ss_ready")
        ln_ready = m.sem("ln_ready")
        rq_ready = m.sem("rq_ready")
        qn_ready = m.sem("qn_ready")
        q_hi = m.sem("q_hi")
        q_lo = m.sem("q_lo")
        act_turn = m.sem("act_turn")
        dve_turn = m.sem("dve_turn")
        pool_turn = m.sem("pool_turn")
        s_ready = m.sem("s_ready")
        s_done = m.sem("s_done")
        exp_done = m.sem("exp_done")
        inv_ready = m.sem("inv_ready")
        p_hi = m.sem("p_hi")
        p_lo = m.sem("p_lo")
        t_ready = m.sem("t_ready")
        t_even = m.sem("t_even")
        t_odd = m.sem("t_odd")
        pv_step = m.sem("pv_step")
        o_hi = m.sem("o_hi")
        o_lo = m.sem("o_lo")
        y_ready = m.sem("y_ready")
        x_added = m.sem("x_added")

        def o_slot(it, h):
            return it % 2 * GROUP if h == 0 else h

        def iterations(eng, turns):
            turns(0, True, False, True)
            with eng.Fori(1, ITS - 1) as it:
                turns(it, True, True, True)
            turns(ITS - 1, True, True, False)
            turns(ITS, False, True, False)

        def lagging(it, N, lag, cur, prev):
            if N >= lag:
                return (it, N - lag) if cur else None
            return (it - 1, N - lag + TILES) if prev else None

        def heads(it, N, delay, cur, nxt):
            for h, first in Q_TURN.items():
                if N == first + delay and (cur if h == GROUP - 1 else nxt):
                    yield (it, h) if h == GROUP - 1 else (it + 1, h)

        with nc.Block() as block:
            @block.sync
            def _(sp):
                sp.dma_start(nmask[:, :, :], mask).then_inc(c_loaded, 16)
                sp.dma_start(bq[:, :], bq_cols).then_inc(c_loaded, 16)
                sp.dma_start(qw[:, :], qn_w).then_inc(c_loaded, 16)
                with sp.Fori(0, NKV) as g:
                    for b in range(B):
                        it = g * B + b
                        sp.wait_ge(pv_step, TILES * (it - 1) + PV0)
                        sp.wait_ge(v_loaded, 32 * it + 16)
                        for h in range(2):
                            sp.dma_start(V[h][:, b % 2 * TPB:(b % 2 + 1) * TPB, :],
                                         v_parts[g, h, :, b * TPB:(b + 1) * TPB, :]).then_inc(v_loaded, 16)

            @block.tensor
            def _(pe):
                pe.sem_inc(q_proj, 1)
                pe.sem_inc(ss_ready, 1)
                pe.sem_inc(s_ready, S0)
                pe.sem_inc(t_ready, T0)
                pe.sem_inc(pv_step, PV0)
                pe.sem_inc(y_ready, Y0)
                pe.wait_ge(const_ready, 4)

                def project(it, h, half):
                    g, b = it // B, it % B
                    if half == 0:
                        pe.wait_ge(wq_split, g + 1)
                        pe.wait_ge(qf_ready, GROUP * it + h + 1)
                    for k in (range(KC // 2), range(KC // 2, KC))[half]:
                        for a, c in ((0, 0), (1, 0), (0, 1)):
                            ins = pe.matmul(bank_q[:, :], wq[a][:, g % 2 * KC + k, h * HD:(h + 1) * HD],
                                            xnT[c][:, k, bass.ds(b * S, S)],
                                            start=(k == 0 and a + c == 0), stop=(k == KC - 1 and c == 1))
                    if half == 1:
                        ins.then_inc(q_proj, 1)

                def sum_squares(it, h):
                    n = GROUP * it + h
                    pe.wait_ge(sq_lo, n + 2)
                    pe.wait_ge(ln_ready, n + 1)
                    for a in range(2):
                        ins = pe.matmul(bank_ss[:, :], ones[:, :], sq[a][:, :], start=(a == 0), stop=(a == 1))
                    ins.then_inc(ss_ready, 1)

                def scores(it, N):
                    h, i = N // TPB, N % TPB
                    if i == 0:
                        pe.wait_ge(q_hi, GROUP * it + h + 1)
                        pe.wait_ge(q_lo, GROUP * it + h + 1 + GROUP)
                    pe.wait_ge(s_done, TILES * it + N + 1)
                    for a, c in ((0, 0), (0, 1), (1, 0)):
                        ins = pe.matmul(bank_s[N % 2][:, :], q[a][:, h, i * P:(i + 1) * P],
                                        KT[c][:, it // B, bass.ds(it % B * S, S)],
                                        start=(a + c == 0), stop=(a == 1))
                    ins.then_inc(s_ready, 1)

                def transposes(it, N):
                    h, i = N // TPB, N % TPB
                    if i == 0:
                        pe.wait_ge(p_lo, TILES * it + N + TPB + SLOTS_P)
                    half = (TILES // 2) * it + N // 2
                    pe.wait_ge((t_even, t_odd)[N % 2], half + 1)
                    for a in range(2):
                        for t in range(TPB):
                            ins = pe.transpose(bank_t[N % 2][:, a, t * P:(t + 1) * P],
                                               p[h % 2][a][:, t, i * P:(i + 1) * P], ident_bf[:, :])
                    ins.then_inc(t_ready, 1)

                def times_v(it, N):
                    h, i = N // TPB, N % TPB
                    half = (TILES // 2) * it + N // 2
                    pe.wait_ge((t_even, t_odd)[N % 2], half + 2)
                    if N == 0:
                        pe.wait_ge(v_loaded, 32 * it + 48)
                    if i == 0:
                        pe.wait_ge(o_lo, GROUP * it + h + 1)
                    for a, c in ((0, 0), (0, 1), (1, 0)):
                        ins = pe.matmul(bank_o[:, :], V[a][:, it % 2 * TPB + i, :], pT[N % 2][:, c, :],
                                        start=(i == 0 and a + c == 0), stop=(i == TPB - 1 and a == 1))
                    ins.then_inc(pv_step, 1)

                def output(it, i, half):
                    if half == 0:
                        pe.wait_ge(x_added, 4 * it + i + 1)
                        if i == 0:
                            pe.wait_ge(o_lo, GROUP * it + GROUP + 1)
                    if i == 0:
                        pe.wait_ge(wo_split, it // B * GROUP + GROUP // 2 * (half + 1))
                    for h in (range(GROUP // 2), range(GROUP // 2, GROUP))[half]:
                        for a, c in ((0, 0), (0, 1), (1, 0)):
                            ins = pe.matmul(bank_y[:, :], oT[a][:, o_slot(it, h), i * P:(i + 1) * P],
                                            wo[c][:, h, :],
                                            start=(h == 0 and a + c == 0), stop=(h == GROUP - 1 and a == 1))
                    if half == 1:
                        ins.then_inc(y_ready, 1)

                def turns(it, cur, prev, nxt):
                    for N in range(TILES):
                        if cur:
                            scores(it, N)
                        for it_h, h in heads(it, N, 5, cur, nxt):
                            sum_squares(it_h, h)
                        tile = lagging(it, N, T_LAG, cur, prev)
                        if tile:
                            transposes(*tile)
                        tile = lagging(it, N, V_LAG, cur, prev)
                        if tile and tile[1] % TPB:
                            times_v(*tile)
                        for half in range(2):
                            for it_h, h in heads(it, N, half, cur, nxt):
                                project(it_h, h, half)
                        if prev and N >= TILES // 2:
                            output(it - 1, (N - TILES // 2) // 2, N % 2)
                        if tile and tile[1] % TPB == 0:
                            times_v(*tile)

                for h in range(GROUP - 1):
                    for half in range(2):
                        project(0, h, half)
                    if h:
                        sum_squares(0, h - 1)
                sum_squares(0, GROUP - 2)
                iterations(pe, turns)

            @block.scalar
            def _(act):
                act.preload_act_table_set("natural_log_exp_and_others")
                act.sem_inc(qf_ready, 1)
                act.sem_inc(ln_ready, 1)
                act.sem_inc(exp_done, LEAD)
                act.sem_inc(t_odd, 1)
                act.wait_ge(w_loaded, 16)
                act.activation(wq[0][:, 0:KC, :], w_f[:, :, :], ACT.Copy).then_inc(w_high, 1)
                act.wait_ge(c_loaded, 48)
                act.wait_ge(const_ready, 4)

                def evacuate(it, h):
                    n = GROUP * it + h
                    act.wait_ge(q_proj, n + 2)
                    act.wait_ge(q_lo, n + 1)
                    act.sem_inc(act_turn, 1)
                    act.activation(qf[h][:, :], bank_q[:, :], ACT.Identity,
                                   bias=bq[:, bass.ds(it // B * GROUP + h, 1)]).then_inc(qf_ready, 1)

                def root(it, h):
                    n = GROUP * it + h
                    act.wait_ge(ss_ready, n + 2)
                    act.wait_ge(qn_ready, n + 1)
                    act.activation(rq[:, :], bank_ss[:, :], ACT.Ln, bias=eps[:, :]).then_inc(ln_ready, 1)
                    act.wait_ge(ln_ready, n + 2)
                    act.activation(rq[:, :], rq[:, :], ACT.Exp, scale=-0.5).then_inc(rq_ready, 1)

                def query_high(it, h):
                    n = GROUP * it + h
                    act.wait_ge(qn_ready, n + 2)
                    act.wait_ge(s_ready, TPB * (n - GROUP + 1) + S0)
                    act.activation(q[0][:, h, :], qf[h][:, :], ACT.Copy).then_inc(q_hi, 1)

                def exponent(it, N):
                    n = TILES * it + N
                    act.wait_ge(s_done, n + 1 + LEAD)
                    act.wait_ge(p_lo, n + 1)
                    act.activation(prob[N % SLOTS_P][:, :], s[N % 2][:, :], ACT.Exp, scale=-1.0, bias=low[:, N:N + 1],
                                   accum_out=total[:, N:N + 1]).then_inc(exp_done, 1)

                def prob_high(it, N):
                    n = TILES * it + N
                    act.wait_ge(inv_ready, n + 1)
                    if N % TPB == 0:
                        act.wait_ge(t_ready, n + TPB)
                    act.activation(p[N // TPB % 2][0][:, N % TPB, :], prob[N % SLOTS_P][:, :], ACT.Copy,
                                   scale=inv[:, N:N + 1]).then_inc(p_hi, 1)

                def copy_odd(it, N):
                    act.wait_ge(t_ready, TILES * it + N + 1 + T0)
                    act.wait_ge(pv_step, TILES * it + N - 1 + PV0)
                    act.activation(pT[1][:, :, :], bank_t[1][:, :, :], ACT.Copy).then_inc(t_odd, 1)

                def value_high(it, h):
                    act.wait_ge(pv_step, TILES * it + TPB * (h + 1) + PV0)
                    act.wait_ge(y_ready, 4 * (it - (h == 0)) + Y0)
                    act.activation(oT[0][:, o_slot(it, h), :], bank_o[:, :], ACT.Copy).then_inc(o_hi, 1)

                def turns(it, cur, prev, nxt):
                    for N in range(TILES):
                        tile = lagging(it, N, V_LAG + 1, cur, prev)
                        if tile and tile[1] % TPB == TPB - 1:
                            value_high(tile[0], tile[1] // TPB)
                        tile = lagging(it, N, T_LAG + 1, cur, prev)
                        if tile and tile[1] % 2:
                            copy_odd(*tile)
                        for it_h, h in heads(it, N, 2, cur, nxt):
                            evacuate(it_h, h)
                        if cur:
                            exponent(it, N)
                        tile = lagging(it, N, 1, cur, prev)
                        if tile:
                            prob_high(*tile)
                        for it_h, h in heads(it, N, 6, cur, nxt):
                            root(it_h, h)
                        for it_h, h in heads(it, N, 8, cur, nxt):
                            query_high(it_h, h)

                for h in range(GROUP - 1):
                    evacuate(0, h)
                    if h:
                        root(0, h - 1)
                        query_high(0, h - 1)
                root(0, GROUP - 2)
                query_high(0, GROUP - 2)
                iterations(act, turns)

            @block.vector
            def _(dve):
                dve.sem_inc(qn_ready, 1)
                dve.sem_inc(s_done, LEAD)
                dve.sem_inc(p_lo, SLOTS_P)
                dve.sem_inc(t_even, 1)
                dve.sem_inc(o_lo, 1)
                dve.sem_inc(x_added, 1)
                dve.wait_ge(c_loaded, 48)
                dve.memset(ones[:, :], 1.0).then_inc(const_ready, 1)
                dve.memset(eps[:, :], HD * RMS_EPS).then_inc(const_ready, 1)
                dve.tensor_scalar(nqw[:, :], qw[:, :], -1.0, None, ALU.mult).then_inc(const_ready, 1)
                dve.tensor_scalar(nmask[:, :, :], nmask[:, :, :], -1.0, None, ALU.mult).then_inc(const_ready, 1)
                dve.wait_ge(const_ready, 4)

                def normalise(it, h):
                    dve.wait_ge(rq_ready, GROUP * it + h + 1)
                    dve.scalar_tensor_tensor(qf[h][:, :], qf[h][:, :], nqw[:, 0:1], rq[:, :],
                                             ALU.mult, ALU.mult).then_inc(qn_ready, 1)

                def mask_max(it, N):
                    n = TILES * it + N
                    dve.wait_ge(s_ready, n + 1 + S0)
                    dve.wait_ge(exp_done, n + 1)
                    dve.sem_inc(dve_turn, 1)
                    dve.tensor_tensor_reduce(s[N % 2][:, :], bank_s[N % 2][:, :], nmask[:, N % TPB, :], 1.0, 3.0e38,
                                             ALU.add, ALU.min, low[:, N:N + 1]).then_inc(s_done, 1)

                def invert(it, N):
                    dve.wait_ge(exp_done, TILES * it + N + 1 + LEAD)
                    dve.reciprocal(inv[:, N:N + 1], total[:, N:N + 1]).then_inc(inv_ready, 1)

                def prob_low(it, N):
                    dve.wait_ge(p_hi, TILES * it + N + 1)
                    dve.scalar_tensor_tensor(p[N // TPB % 2][1][:, N % TPB, :], prob[N % SLOTS_P][:, :],
                                             inv[:, N:N + 1], p[N // TPB % 2][0][:, N % TPB, :],
                                             ALU.mult, ALU.subtract).then_inc(p_lo, 1)

                def copy_even(it, N):
                    dve.wait_ge(t_ready, TILES * it + N + 1 + T0)
                    dve.wait_ge(pv_step, TILES * it + N - 1 + PV0)
                    dve.tensor_copy(pT[0][:, :, :], bank_t[0][:, :, :]).then_inc(t_even, 1)

                def value_low(it, h):
                    dve.wait_ge(o_hi, GROUP * it + h + 1)
                    dve.tensor_tensor(oT[1][:, o_slot(it, h), :], bank_o[:, :], oT[0][:, o_slot(it, h), :],
                                      ALU.subtract).then_inc(o_lo, 1)

                def add_output(it, i):
                    dve.wait_ge(y_ready, 4 * it + i + 1 + Y0)
                    xt = X[:, it % B * TPB + i, :]
                    dve.tensor_tensor(xt, bank_y[:, :], xt, ALU.add).then_inc(x_added, 1)

                def turns(it, cur, prev, nxt):
                    for N in range(TILES):
                        if prev and N > TILES // 2 and N % 2 == 0:
                            add_output(it - 1, (N - TILES // 2) // 2 - 1)
                        tile = lagging(it, N, T_LAG + 1, cur, prev)
                        if tile and tile[1] % 2 == 0:
                            copy_even(*tile)
                        tile = lagging(it, N, V_LAG + 1, cur, prev)
                        if tile and tile[1] % TPB == TPB - 1:
                            value_low(tile[0], tile[1] // TPB)
                        if cur:
                            mask_max(it, N)
                        tile = lagging(it, N, 1, cur, prev)
                        if tile:
                            invert(*tile)
                        tile = lagging(it, N, 2, cur, prev)
                        if tile:
                            prob_low(*tile)
                        for it_h, h in heads(it, N, 7, cur, nxt):
                            normalise(it_h, h)
                        if prev and N == TILES - 1:
                            add_output(it - 1, TPB - 1)

                for h in range(GROUP - 1):
                    normalise(0, h)
                iterations(dve, turns)

            @block.gpsimd
            def _(pool):
                pool.sem_inc(q_lo, GROUP)
                pool.sem_inc(sq_lo, 1)
                pool.sem_inc(v_loaded, 16)
                SPLITS = 1 + GROUP

                def split(hi, lo, source, n, done):
                    pool.sem_inc(pool_turn, 1)
                    pool.tensor_copy(hi, source).then_inc(w_high, 1)
                    pool.wait_ge(w_high, n + 1)
                    pool.tensor_tensor(lo, source, hi, ALU.subtract).then_inc(done, 1)

                def split_wq(g):
                    pool.wait_ge(w_loaded, 32 * g + 16)
                    pool.wait_ge(q_proj, GROUP * B * (g - 1) + 1)
                    at = bass.ds(g % 2 * KC, KC)
                    split(wq[0][:, at, :], wq[1][:, at, :], w_f[:, :, :], SPLITS * g, wq_split)

                def split_wo(g, h):
                    if h == 0:
                        pool.wait_ge(w_loaded, 32 * g + 32)
                        pool.wait_ge(y_ready, B * TPB * g + Y0)
                    split(wo[0][:, h, :], wo[1][:, h, :], w_f[:, h, :], SPLITS * g + 1 + h, wo_split)

                def squares(it, h):
                    n = GROUP * it + h
                    pool.wait_ge(qf_ready, n + 2)
                    pool.wait_ge(sq_lo, n + 1)
                    pool.wait_ge(ss_ready, n + 1)
                    pool.sem_inc(pool_turn, 1)
                    pool.tensor_tensor(sq_f[:, :], qf[h][:, :], qf[h][:, :], ALU.mult).then_inc(sqf_ready, 1)
                    pool.wait_ge(sqf_ready, n + 1)
                    pool.sem_inc(pool_turn, 1)
                    pool.tensor_copy(sq[0][:, :], sq_f[:, :]).then_inc(sq_hi, 1)
                    pool.wait_ge(sq_hi, n + 1)
                    pool.tensor_tensor(sq[1][:, :], sq_f[:, :], sq[0][:, :], ALU.subtract).then_inc(sq_lo, 1)

                def query_low(it, h):
                    pool.wait_ge(q_hi, GROUP * it + h + 1)
                    pool.tensor_tensor(q[1][:, h, :], qf[h][:, :], q[0][:, h, :], ALU.subtract).then_inc(q_lo, 1)

                def load(source, wait_for, count):
                    pool.wait_ge(wait_for, count)
                    pool.sem_inc(pool_turn, 1)
                    pool.dma_start(w_f[:, :, :], source).then_inc(w_loaded, 16)

                def queries(g, b, last_g=False):
                    it = g * B + b
                    more = not (last_g and b == B - 1)
                    if b == 1:
                        split_wo(g, 0)
                        split_wo(g, 1)
                    squares(it, 3)
                    if b == 1:
                        split_wo(g, 2)
                    if more:
                        squares(it + 1, 0)
                        if b == 1:
                            split_wo(g, 3)
                            if not last_g:
                                load(w_q[g + 1], wo_split, GROUP * g + GROUP)
                        squares(it + 1, 1)
                    query_low(it, 3)
                    if more:
                        squares(it + 1, 2)
                        for h in range(GROUP - 1):
                            query_low(it + 1, h)
                    if b == 1 and not last_g:
                        split_wq(g + 1)
                        load(w_o[g + 1], wq_split, g + 2)

                pool.dma_start(w_f[:, :, :], w_q[0]).then_inc(w_loaded, 16)
                pool.wait_ge(w_high, 1)
                pool.tensor_tensor(wq[1][:, 0:KC, :], w_f[:, :, :], wq[0][:, 0:KC, :], ALU.subtract
                                   ).then_inc(wq_split, 1)
                load(w_o[0], wq_split, 1)
                for h in range(GROUP - 1):
                    squares(0, h)
                for h in range(GROUP - 1):
                    query_low(0, h)
                with pool.Fori(0, NKV - 1) as g:
                    for b in range(B):
                        queries(g, b)
                for b in range(B):
                    queries(NKV - 1, b, last_g=True)


class Rounding:
    SLOTS = 4

    def __init__(self, m, width):
        self.v = [m.sb(f"v{j}", [P, width], F32) for j in range(self.SLOTS)]
        self.e = m.sb("e", [P, width], F32)
        self.m = [m.sb(f"m{j}", [P, width], BF16) for j in range(2)]
        self.v_ready = m.sem("v_ready")
        self.e_ready = m.sem("e_ready")
        self.m_ready = m.sem("m_ready")
        self.t_ready = m.sem("t_ready")
        self.o_ready = m.sem("o_ready")

    def start(self, dve):
        dve.sem_inc(self.o_ready, self.SLOTS)
        dve.sem_inc(self.m_ready, 1)

    def scale(self, act, n, j, src, func, factor):
        act.wait_ge(self.o_ready, n + 1)
        act.activation(self.v[j][:, :], src, func, scale=factor).then_inc(self.v_ready, 1)

    def magic(self, dve, n, j):
        dve.wait_ge(self.o_ready, n - 1 + self.SLOTS)
        dve.wait_ge(self.v_ready, n + 1)
        dve.wait_ge(self.m_ready, n + 1)
        dve.tensor_scalar(self.e[:, :].bitcast(I32), self.v[j][:, :].bitcast(I32), 0x7F800000, None,
                          ALU.bitwise_and).then_inc(self.e_ready, 1)
        dve.wait_ge(self.e_ready, n + 1)
        dve.tensor_scalar(self.m[j % 2][:, :], self.e[:, :], 2.0 ** -6, 1.5 * 2.0 ** 20,
                          ALU.max, ALU.mult).then_inc(self.m_ready, 1)

    def add(self, pool, n, j):
        pool.wait_ge(self.m_ready, n + 2)
        pool.tensor_tensor(self.v[j][:, :], self.v[j][:, :], self.m[j % 2][:, :], ALU.add).then_inc(self.t_ready, 1)

    def subtract(self, dve, n, j, out):
        dve.wait_ge(self.t_ready, n + 1)
        dve.tensor_tensor(out, self.v[j][:, :], self.m[j % 2][:, :], ALU.subtract).then_inc(self.o_ready, 1)


def stage_quantise(nc, X, xqT, w8_fc, w8_ff, scales, ident_bf):
    WIDTH = 1024
    NP = NT * C // WIDTH
    SL = Rounding.SLOTS
    with ExitStack() as stack:
        m = Names(nc, stack, "quant")
        xn = m.sb("xn", [P, NT * C], F32)
        xq = [m.sb(f"xq{j}", [P, WIDTH], BF16) for j in range(2)]
        stats = m.sb("stats", [P, NT, 6], F32)
        mv = m.sb("mv", [P, NT, 2], F32)
        rstd = m.sb("rstd", [P, NT], F32)
        shift = m.sb("shift", [P, NT], F32)
        part = m.sb("part", [P, NT], F32)
        top = m.sb("top", [P, 1], F32)
        top_all = m.sb("top_all", [P, 1], F32)
        inv = m.sb("inv", [P, 1], F32)
        pt = [m.ps(f"pt{j}", [P, 8, P], BF16) for j in range(2)]
        rnd = Rounding(m, WIDTH)
        w_loaded = m.sem("w_loaded")
        stat = m.sem("stat")
        root_ready = m.sem("root_ready")
        shift_ready = m.sem("shift_ready")
        xn_ready = m.sem("xn_ready")
        part_ready = m.sem("part_ready")
        top_ready = m.sem("top_ready")
        all_ready = m.sem("all_ready")
        step = m.sem("step")
        pt_ready = m.sem("pt_ready")
        xt_ready = m.sem("xt_ready")

        with nc.Block() as block:
            @block.sync
            def _(sp):
                sp.dma_start(w8_fc[:, :, :].rearrange("p k f -> p (k f)"), w8_ff[:, 0:KC * FF]).then_inc(w_loaded, 16)
                sp.wait_ge(w_loaded, 16)

            @block.vector
            def _(dve):
                rnd.start(dve)
                ln_stats(dve, stat, root_ready, X, stats, mv, rstd)
                dve.scalar_tensor_tensor(shift[:, :], mv[:, :, 0], -1.0, rstd[:, :], ALU.mult, ALU.mult
                                         ).then_inc(shift_ready, 1)
                with dve.Fori(0, NT) as t:
                    dve.wait_ge(xn_ready, t + 1)
                    dve.tensor_reduce(part[:, bass.ds(t, 1)], xn[:, bass.ds(t * C, C)], AX.X, ALU.max,
                                      apply_absolute_value=True).then_inc(part_ready, 1)
                dve.wait_ge(part_ready, NT)
                dve.tensor_reduce(top[:, :], part[:, :], AX.X, ALU.max).then_inc(top_ready, 1)
                done = Steps(dve, step)
                dve.wait_ge(all_ready, 1)
                done.mark(dve.tensor_scalar(scales[:, 2:3], top_all[:, :], 1.0 / FP8_MAX, 1e-6, ALU.mult, ALU.max))
                done.wait()
                done.mark(dve.reciprocal(inv[:, :], scales[:, 2:3]))

                for n in range(NP + 2):
                    if n >= 2:
                        dve.wait_ge(pt_ready, n - 1)
                        rnd.subtract(dve, n - 2, (n - 2) % SL, xq[n % 2][:, :])
                    if n < NP:
                        rnd.magic(dve, n, n % SL)

            @block.gpsimd
            def _(pool):
                pool.wait_ge(top_ready, 1)
                pool.partition_all_reduce(top_all[:, :], top[:, :], P, bass.bass_isa.ReduceOp.max).then_inc(all_ready, 1)
                with pool.Fori(0, NP // SL) as i:
                    for j in range(SL):
                        rnd.add(pool, SL * i + j, j)

            @block.scalar
            def _(act):
                ln_root(act, stat, root_ready, rstd)
                act.wait_ge(shift_ready, 1)
                for t in range(NT):
                    act.activation(xn[:, t * C:(t + 1) * C], X[:, t, :], ACT.Identity, scale=rstd[:, t:t + 1],
                                   bias=shift[:, t:t + 1]).then_inc(xn_ready, 1)
                act.wait_ge(step, 2)

                def copy_out(n):
                    act.wait_ge(pt_ready, n + 1 + LEAD)
                    for i in range(2):
                        ins = act.activation(xqT[:, :, (2 * n + i) * P:(2 * n + i + 1) * P],
                                             pt[n % 2][:, i * KC:(i + 1) * KC, :], ACT.Copy)
                    ins.then_inc(xt_ready, 1)

                for n in range(NP + SL):
                    if n < NP:
                        rnd.scale(act, n, n % SL, xn[:, n * WIDTH:(n + 1) * WIDTH], ACT.Copy, inv[:, 0:1])
                    if n >= SL:
                        copy_out(n - SL)

            @block.tensor
            def _(pe):
                pe.sem_inc(pt_ready, LEAD)
                pe.sem_inc(xt_ready, LEAD)
                with pe.Fori(0, NP // 2) as c2:
                    for j in range(2):
                        c = 2 * c2 + j
                        pe.wait_ge(rnd.o_ready, c + 1 + SL)
                        pe.wait_ge(xt_ready, c + 1)
                        for k in range(8):
                            ins = pe.transpose(pt[j][:, k, :], xq[j][:, k * P:(k + 1) * P], ident_bf[:, :])
                        ins.then_inc(pt_ready, 1)


def stage_up(nc, xqT, w8_fc, R, r_top, scales):
    NG = TOK // 512
    with ExitStack() as stack:
        m = Names(nc, stack, "up")
        s1 = m.sb("s1", [P, 1], F32)
        part = m.sb("part", [P, FFC * NG], F32)
        top = m.sb("top", [P, 1], F32)
        bank = [[m.ps(f"bank{j}_{g}", [P, 512], F32) for g in range(NG)] for j in range(2)]
        s1_ready = m.sem("s1_ready")
        z_ready = m.sem("z_ready")
        r_ready = m.sem("r_ready")
        part_ready = m.sem("part_ready")
        top_ready = m.sem("top_ready")
        all_ready = m.sem("all_ready")

        with nc.Block() as block:
            @block.tensor
            def _(pe):
                with pe.Fori(0, FFC // 2) as f2:
                    for j in range(2):
                        f = 2 * f2 + j
                        for k in range(KC):
                            for g in range(NG):
                                if k == 0:
                                    pe.wait_ge(r_ready, NG * f + g + 1)
                                ins = pe.matmul(bank[j][g][:, :], w8_fc[:, k, bass.ds(f * P, P)],
                                                xqT[:, k, g * 512:(g + 1) * 512], start=(k == 0), stop=(k == KC - 1))
                                if k == KC - 1:
                                    ins.then_inc(z_ready, 1)

            @block.scalar
            def _(act):
                act.sem_inc(r_ready, 2 * NG)
                act.wait_ge(s1_ready, 1)
                with act.Fori(0, FFC // 2) as f2:
                    for j in range(2):
                        f = 2 * f2 + j
                        for g in range(NG):
                            act.wait_ge(z_ready, NG * f + g + 1)
                            act.activation(R[:, f, g * 512:(g + 1) * 512], bank[j][g][:, :], ACT.Relu,
                                           scale=s1[:, 0:1]).then_inc(r_ready, 1)

            @block.vector
            def _(dve):
                dve.tensor_tensor(s1[:, :], scales[:, 2:3], scales[:, 0:1], ALU.mult).then_inc(s1_ready, 1)
                with dve.Fori(0, FFC) as f:
                    for g in range(NG):
                        dve.wait_ge(r_ready, NG * f + g + 1 + 2 * NG)
                        dve.tensor_reduce(part[:, bass.ds(NG * f + g, 1)], R[:, f, g * 512:(g + 1) * 512],
                                          AX.X, ALU.max).then_inc(part_ready, 1)
                dve.wait_ge(part_ready, NG * FFC)
                dve.tensor_reduce(top[:, :], part[:, :], AX.X, ALU.max).then_inc(top_ready, 1)

            @block.gpsimd
            def _(pool):
                pool.wait_ge(top_ready, 1)
                pool.partition_all_reduce(r_top[:, :], top[:, :], P, bass.bass_isa.ReduceOp.max).then_inc(all_ready, 1)
                pool.wait_ge(all_ready, 1)


def stage_down(nc, X, R, r_top, w8_ff, scales, out):
    WIDTH = 1024
    NB = WIDTH // P
    HALVES = TOK // WIDTH
    SL = Rounding.SLOTS
    with ExitStack() as stack:
        m = Names(nc, stack, "down")
        w8 = m.sb("w8", [P, FFC, C], BF16)
        h8 = [m.sb(f"h8{j}", [P, WIDTH], BF16) for j in range(2)]
        h_top = m.sb("h_top", [P, 1], F32)
        h_scale = m.sb("h_scale", [P, 1], F32)
        inv = m.sb("inv", [P, 1], F32)
        root = m.sb("root", [P, 1], F32)
        s2 = m.sb("s2", [P, 1], F32)
        rnd = Rounding(m, WIDTH)
        bank = [m.ps(f"bank{i}", [P, C], F32) for i in range(NB)]
        w_loaded = m.sem("w_loaded")
        step = m.sem("step")
        root_ready = m.sem("root_ready")
        h_used = m.sem("h_used")
        x_ready = m.sem("x_ready")
        stored = m.sem("stored")

        with nc.Block() as block:
            @block.sync
            def _(sp):
                sp.dma_start(w8[:, :, :], w8_ff[:, KC * FF:].rearrange("p (f c) -> p f c", c=C)).then_inc(w_loaded, 16)
                for t in range(NT):
                    b, i = t // TPB, t % TPB
                    sp.wait_ge(x_ready, t + 1 + NB)
                    sp.dma_start(out[b, i * P:(i + 1) * P, :], X[:, t, :]).then_inc(stored, 16)
                sp.wait_ge(stored, 16 * NT)

            @block.vector
            def _(dve):
                rnd.start(dve)
                dve.sem_inc(x_ready, NB)
                done = Steps(dve, step)
                done.mark(dve.tensor_tensor(h_top[:, :], r_top[:, :], r_top[:, :], ALU.mult))
                done.wait()
                done.mark(dve.tensor_scalar(h_scale[:, :], h_top[:, :], 1.0 / FP8_MAX, 1e-6, ALU.mult, ALU.max))
                done.wait()
                done.mark(dve.reciprocal(inv[:, :], h_scale[:, :]))
                done.mark(dve.tensor_tensor(s2[:, :], h_scale[:, :], scales[:, 1:2], ALU.mult))
                done.wait()

                def subtract(n, j):
                    dve.wait_ge(h_used, n + 1)
                    rnd.subtract(dve, n, j, h8[j % 2][:, :])

                def add_sums(half):
                    for i in range(NB):
                        if i == 0:
                            dve.wait_ge(h_used, FFC * (half + 1) + LEAD)
                        xt = X[:, half * NB + i, :]
                        dve.scalar_tensor_tensor(xt, bank[i][:, :], s2[:, 0:1], xt, ALU.mult, ALU.add).then_inc(x_ready, 1)

                rnd.magic(dve, 0, 0)
                rnd.magic(dve, 1, 1)
                for half in range(HALVES):
                    last = half == HALVES - 1
                    with dve.Fori(0, FFC // SL - last) as f4:
                        for j in range(SL):
                            n = half * FFC + SL * f4 + j
                            subtract(n, j)
                            rnd.magic(dve, n + 2, (j + 2) % SL)
                    if last:
                        for j in range(SL):
                            n = HALVES * FFC - SL + j
                            subtract(n, j)
                            if j < 2:
                                rnd.magic(dve, n + 2, j + 2)
                    add_sums(half)

            @block.scalar
            def _(act):
                act.wait_ge(step, 4)
                act.activation(root[:, :], inv[:, :], ACT.Sqrt).then_inc(root_ready, 1)
                act.wait_ge(root_ready, 1)
                with act.Fori(0, HALVES) as half:
                    with act.Fori(0, FFC // SL) as f4:
                        for j in range(SL):
                            f = SL * f4 + j
                            rnd.scale(act, half * FFC + f, j, R[:, f, bass.ds(half * WIDTH, WIDTH)],
                                      ACT.Square, root[:, 0:1])

            @block.gpsimd
            def _(pool):
                with pool.Fori(0, HALVES * FFC // SL) as n4:
                    for j in range(SL):
                        rnd.add(pool, SL * n4 + j, j)

            @block.tensor
            def _(pe):
                pe.sem_inc(h_used, LEAD)
                pe.wait_ge(w_loaded, 16)
                with pe.Fori(0, HALVES) as half:
                    for f in range(FFC):
                        n = half * FFC + f
                        pe.wait_ge(rnd.o_ready, n + 1 + SL)
                        for i in range(NB):
                            if f == 0:
                                pe.wait_ge(x_ready, half * NB + i + 1)
                            ins = pe.matmul(bank[i][:, :], h8[f % 2][:, i * P:(i + 1) * P], w8[:, f, :],
                                            start=(f == 0), stop=(f == FFC - 1))
                        ins.then_inc(h_used, 1)


def build(nc, x, ctx_t, wu_cols, w_row, centroids, gate_bias, w_gate_up, w_down, w_table,
          w_kv, bias_kv, kn_w, w_q, w_o, bq_cols, qn_w, mask, w_ff, out):
    with ExitStack() as keep:
        def tensor(stack, name, shape, dt, **where):
            return stack.enter_context(nc.sbuf_tensor(name, shape, dt, **where))

        X = tensor(keep, "X", [P, NT, C], F32)
        ident = tensor(keep, "ident", [P, P], F32)
        ident_bf = tensor(keep, "ident_bf", [P, P], BF16)
        v_parts = nc.dram_tensor("v_parts", (NKV, 2, P, NT, HD), BF16, kind="Internal").ap()
        slot_rows = nc.dram_tensor("slot_rows", (TILES_R * SLOTS, 2 * C), BF16, kind="Internal").ap()
        slot_out = nc.dram_tensor("slot_out", (TILES_R * SLOTS, C), F32, kind="Internal").ap()
        w8_ff = nc.dram_tensor("w8_ff", (P, KC * FF + FFC * C), BF16, kind="Internal").ap()
        scales = tensor(keep, "scales", [P, 3], F32)
        inv_w = tensor(keep, "inv_w", [P, 2], F32)
        stats = tensor(keep, "stats", [P, NT, 6], F32)
        ff_part = tensor(keep, "ff_part", [P, NT], F32)
        with ExitStack() as attention:
            KT = [tensor(attention, f"KT_{h}", [P, NKV, TOK], BF16) for h in ("hi", "lo")]
            with ExitStack() as first:
                ctxT = [tensor(first, f"ctxT_{h}", [P, KC, TOK], BF16) for h in ("hi", "lo")]
                w_kv_parts = [tensor(first, f"w_kv_{h}", [P, 2, KC, NKV * HD], BF16) for h in ("hi", "lo")]
                with ExitStack() as wkv:
                    time_row = tensor(wkv, "time_row", [1, S], F32)
                    stage_setup(nc, ident, ident_bf, time_row)
                    stage_wkv(nc, X, ctxT, ident, time_row, x, ctx_t, wu_cols, w_row, w_kv_parts, w_kv)
                stage_kv(nc, ctxT, KT, v_parts, ident, w_kv_parts, bias_kv, kn_w, slot_rows, w_ff, ff_part)
            with ExitStack() as moe:
                slot = [tensor(moe, f"slot{k}", [P, NT], U32) for k in range(2)]
                share = [tensor(moe, f"share{k}", [P, NT], F32) for k in range(2)]
                w_rows = tensor(moe, "w_rows", [P, TILES_R], U32)
                with ExitStack() as shared:
                    rows = tensor(shared, "rows", [P, NT, 2 * C], BF16)
                    xnT = [tensor(shared, f"xnT1_{h}", [P, KC, TOK], BF16) for h in ("hi", "lo")]
                    gu = [[tensor(shared, f"gu_{h}{e}", [P, KC, 2 * F_EXP], BF16) for h in ("hi", "lo")] for e in range(2)]
                    dn = [[tensor(shared, f"dn_{h}{e}", [P, FC, C], BF16) for h in ("hi", "lo")] for e in range(2)]
                    stage_route(nc, X, xnT, rows, share, slot, w_rows, ident, centroids, gate_bias,
                                ff_part, scales, inv_w, gu, dn, w_gate_up, w_down)
                    stage_shared(nc, X, xnT, rows, slot, slot_rows, gu, dn, w_ff, w8_ff, inv_w)
                stage_routed(nc, slot_rows, slot_out, w_rows, w_table)
                stage_combine(nc, X, share, slot, slot_out, stats)
            xnT = [tensor(attention, f"xnT2_{h}", [P, KC, TOK], BF16) for h in ("hi", "lo")]
            stage_norm(nc, X, xnT, ident, stats)
            stage_attention(nc, X, xnT, KT, v_parts, ident_bf, mask, w_q, w_o, bq_cols, qn_w)
        r_top = tensor(keep, "r_top", [P, 1], F32)
        with ExitStack() as hidden:
            with ExitStack() as up:
                right = bass.opposite_side(nc.default_side)
                xqT = tensor(up, "xqT", [P, KC, TOK], BF16, side=right)
                w8_fc = tensor(up, "w8_fc", [P, KC, FF], BF16, side=right)
                stage_quantise(nc, X, xqT, w8_fc, w8_ff, scales, ident_bf)
                R = tensor(hidden, "R", [P, FFC, TOK], F32)
                stage_up(nc, xqT, w8_fc, R, r_top, scales)
            stage_down(nc, X, R, r_top, w8_ff, scales, out)


def kernel(**inputs):
    import numpy as np
    import concourse.bacc as bacc
    from concourse.bass_utils import run_bass_kernel_spmd

    def host(name):
        return np.asarray(inputs[name])

    w, u = host("L0_xattn_w"), host("L0_xattn_u")
    def by_partition(gate, up, down):
        gu = np.concatenate([gate, up], axis=2).reshape(-1, KC, P, 2 * F_EXP).transpose(0, 2, 1, 3)
        return gu, down.reshape(-1, FC, P, C).transpose(0, 2, 1, 3)

    gu, dn = by_partition(host("L0_ffn_wg"), host("L0_ffn_wu"), host("L0_ffn_wd"))
    gu_s, dn_s = by_partition(*(host(n).reshape(C, 2, F_EXP).transpose(1, 0, 2) for n in ("L0_ffn_wg_s", "L0_ffn_wu_s")),
                              host("L0_ffn_wd_s").reshape(2, F_EXP, C))
    arrays = {
        "w_ff": np.concatenate([host("L1_ffn_w_fc").T.reshape(KC, P, FF).transpose(1, 0, 2).reshape(P, KC * FF),
                                host("L1_ffn_w_proj").T.reshape(FFC, P, C).transpose(1, 0, 2).reshape(P, FFC * C)],
                               axis=1),
        "w_kv": np.stack([host(n).reshape(KC, P, NKV * HD).transpose(1, 0, 2) for n in ("L1_xattn_Wk", "L1_xattn_Wv")]),
        "bias_kv": np.tile(np.stack([host("L1_xattn_bk"), host("L1_xattn_bv")]), (P, 1, 1)),
        "kn_w": np.tile(host("L1_xattn_kn_w"), (P, 1)),
        "qn_w": host("L1_xattn_qn_w").reshape(P, 1),
        "bq_cols": host("L1_xattn_bq").reshape(NH, HD).T,
        "w_q": host("L1_xattn_Wq").reshape(KC, P, NKV, GROUP * HD).transpose(2, 1, 0, 3),
        "w_o": host("L1_xattn_Wo").reshape(NKV, GROUP, HD, C).transpose(0, 2, 1, 3),
        "mask": host("mask_1xSxS2_ff0")[0].reshape(TPB, P, S).transpose(1, 0, 2),
        "centroids": host("L0_ffn_centroids").T.reshape(KC, P, E_ROUTED).transpose(1, 0, 2),
        "gate_bias": np.tile(host("L0_ffn_gate_bias"), (P, 1)),
        "w_gate_up": gu_s,
        "w_down": dn_s,
        "w_table": np.concatenate([gu.reshape(E_ROUTED * P, -1), dn.reshape(E_ROUTED * P, -1)], axis=1),
        "x": host("x"),
        "ctx_t": host("ctx_2048").transpose(0, 2, 1),
        "wu_cols": np.stack([w.reshape(KC, P).T, u.reshape(KC, P).T], axis=1),
        "w_row": w.reshape(1, C),
    }
    arrays = {name: np.ascontiguousarray(a) for name, a in arrays.items()}
    nc = bacc.Bacc("TRN2", target_bir_lowering=False, num_devices=1)
    aps = {name: nc.dram_tensor(name, a.shape, mybir.dt.from_np(a.dtype), kind="ExternalInput").ap()
           for name, a in arrays.items()}
    out = nc.dram_tensor("out", (B, S, C), F32, kind="ExternalOutput").ap()
    build(nc, out=out, **aps)
    r = run_bass_kernel_spmd(nc, [arrays], core_ids=[0])
    return r.results[0]["out"]
```
